# Optimizing a Trainium2 kernel written in Bass

```python
import numpy as np
import jax
import jax.numpy as jnp

def _softmax(x, axis=-1):
    return jax.nn.softmax(x, axis=axis)

def _gelu(x):
    return jax.nn.gelu(x, approximate=True)

def _silu(x):
    return jax.nn.silu(x)

def _sigmoid(x):
    return jax.nn.sigmoid(x)

def _layernorm(x, axis=-1, eps=1e-05):
    m = jnp.mean(x, axis=axis, keepdims=True)
    v = jnp.var(x, axis=axis, keepdims=True)
    return (x - m) / jnp.sqrt(v + eps)

def _scatter_add(tgt, idx, src, axis=0):
    return tgt.at[idx].add(src)

def _segment_sum(src, seg, n):
    return jax.ops.segment_sum(src, seg, n)
kernel_name = 'mk_hybrid_d1_jaxref_r8_99d317'

def setup_inputs(seed: int=0):
    np.random.seed(seed)
    _w = jnp.asarray

    def _L0_attn_a_setup():
        import jax, jax.numpy as jnp
        import numpy as np
        D_MODEL = 128
        N_HEADS = 16
        HEAD_DIM = D_MODEL // N_HEADS
        SCALE = HEAD_DIM ** (-0.5)

        def apply_rotary(x):
            seq_len = x.shape[-2]
            freqs = 10000.0 ** (jnp.arange(0, HEAD_DIM, 2.0, dtype=jnp.float32) / HEAD_DIM)
            t = jnp.arange(seq_len, dtype=jnp.float32)
            angles = t[:, None] * freqs[None, :]
            sin = jnp.sin(angles)[None, None]
            cos = jnp.cos(angles)[None, None]
            x1, x2 = (x[..., ::2], x[..., 1::2])
            return jnp.concatenate([x1 * cos - x2 * sin, x2 * cos + x1 * sin], axis=-1)
        key = jax.random.key(seed)
        ks = jax.random.split(key, 5)
        B, T = (2, 256)
        std = D_MODEL ** (-0.5)
        return {'x': jax.random.normal(ks[0], (B, T, D_MODEL), dtype=jnp.float32), 'qkv_w': jax.random.normal(ks[1], (D_MODEL, 3 * D_MODEL), dtype=jnp.float32) * std, 'qkv_b': jnp.zeros((3 * D_MODEL,), dtype=jnp.float32), 'out_w': jax.random.normal(ks[2], (D_MODEL, D_MODEL), dtype=jnp.float32) * std, 'out_b': jnp.zeros((D_MODEL,), dtype=jnp.float32)}
    _L0_attn_a_in = _L0_attn_a_setup()

    def _L0_attn_b_setup():
        import jax, jax.numpy as jnp
        import numpy as np
        D_MODEL = 128
        EXPAND = 2
        D_INNER = EXPAND * D_MODEL
        D_STATE = 16
        DT_RANK = (D_MODEL + 15) // 16
        EPS = 1e-05
        FP_ITERS = 8
        STEP = 0.99
        B_SZ, L_SEQ = (2, 256)

        def _shift1(y):
            return jnp.pad(y, ((0, 0), (1, 0), (0, 0)))[:, :-1, :]

        def _selective_scan(u, delta, A, Bm, Cm, D):

            def step(h, inp):
                dt_t, u_t, b_t, c_t = inp
                h = jnp.exp(dt_t[:, :, None] * A) * h + (dt_t * u_t)[:, :, None] * b_t[:, None, :]
                y = jnp.einsum('bdn,bn->bd', h, c_t) + D * u_t
                return (h, y)
            b, l, d = u.shape
            h0 = jnp.zeros((b, d, A.shape[1]), u.dtype)
            xs = tuple((jnp.moveaxis(a, 1, 0) for a in (delta, u, Bm, Cm)))
            _, ys = jax.lax.scan(step, h0, xs)
            return jnp.moveaxis(ys, 0, 1)
        key = jax.random.key(seed)
        ks = jax.random.split(key, 12)
        f32 = jnp.float32
        hidden_states = jax.random.normal(ks[0], (B_SZ, L_SEQ, D_MODEL), f32)
        W_in = jax.random.normal(ks[1], (2 * D_INNER, D_MODEL), f32) * D_MODEL ** (-0.5)
        W_x = jax.random.normal(ks[2], (DT_RANK + 2 * D_STATE, D_INNER), f32) * D_INNER ** (-0.5)
        W_dt = jax.random.uniform(ks[3], (D_INNER, DT_RANK), f32, -DT_RANK ** (-0.5), DT_RANK ** (-0.5))
        dt = jnp.exp(jax.random.uniform(ks[4], (D_INNER,), f32) * (np.log(0.1) - np.log(0.001)) + np.log(0.001))
        dt = jnp.clip(dt, 0.0001)
        b_dt = dt + jnp.log(-jnp.expm1(-dt))
        A_log = jnp.log(jnp.tile(jnp.arange(1, D_STATE + 1, dtype=f32)[None, :], (D_INNER, 1)))
        W_bc = jax.random.normal(ks[5], (2 * D_STATE, D_INNER), f32) * D_INNER ** (-0.5)
        W_zy = jax.random.normal(ks[6], (D_INNER, D_INNER), f32) * D_INNER ** (-0.5)
        W_mix = jax.random.normal(ks[7], (D_INNER, D_INNER), f32) * D_INNER ** (-0.5)
        D = jnp.ones((D_INNER,), f32)
        ln_gamma = jnp.ones((D_INNER,), f32)
        ln_beta = jnp.zeros((D_INNER,), f32)
        W_out = jax.random.normal(ks[8], (D_MODEL, D_INNER), f32) * D_INNER ** (-0.5)
        return dict(hidden_states=hidden_states, W_in=W_in, W_x=W_x, W_dt=W_dt, b_dt=b_dt, A_log=A_log, W_bc=W_bc, W_zy=W_zy, W_mix=W_mix, D=D, ln_gamma=ln_gamma, ln_beta=ln_beta, W_out=W_out)
    _L0_attn_b_in = _L0_attn_b_setup()

    def _L0_ffn_setup():
        import jax, jax.numpy as jnp
        import numpy as np
        D_MODEL, D_FF, N_EXPERTS, TOP_K = (128, 256, 8, 2)
        B, S = (2, 256)
        key = jax.random.key(seed)
        ks = jax.random.split(key, 6)
        sd = 1.0 / np.sqrt(D_MODEL)
        sf = 1.0 / np.sqrt(D_FF)
        return {'x': jax.random.normal(ks[0], (B, S, D_MODEL), jnp.float32), 'router_w': jax.random.normal(ks[1], (N_EXPERTS, D_MODEL), jnp.float32) * sd, 'gate_w': jax.random.normal(ks[2], (N_EXPERTS, D_MODEL, D_FF), jnp.float32) * sd, 'gate_b': jnp.zeros((N_EXPERTS, D_FF), jnp.float32), 'up_w': jax.random.normal(ks[3], (N_EXPERTS, D_MODEL, D_FF), jnp.float32) * sd, 'up_b': jnp.zeros((N_EXPERTS, D_FF), jnp.float32), 'down_w': jax.random.normal(ks[4], (N_EXPERTS, D_FF, D_MODEL), jnp.float32) * sf, 'down_b': jnp.zeros((N_EXPERTS, D_MODEL), jnp.float32)}
    _L0_ffn_in = _L0_ffn_setup()
    _d = {'L0_attn_a_x': _L0_attn_a_in['x'], 'L0_attn_a_qkv_w': _L0_attn_a_in['qkv_w'], 'L0_attn_a_qkv_b': _L0_attn_a_in['qkv_b'], 'L0_attn_a_out_w': _L0_attn_a_in['out_w'], 'L0_attn_a_out_b': _L0_attn_a_in['out_b'], 'L0_attn_b_W_in': _L0_attn_b_in['W_in'], 'L0_attn_b_W_x': _L0_attn_b_in['W_x'], 'L0_attn_b_W_dt': _L0_attn_b_in['W_dt'], 'L0_attn_b_b_dt': _L0_attn_b_in['b_dt'], 'L0_attn_b_A_log': _L0_attn_b_in['A_log'], 'L0_attn_b_W_bc': _L0_attn_b_in['W_bc'], 'L0_attn_b_W_zy': _L0_attn_b_in['W_zy'], 'L0_attn_b_W_mix': _L0_attn_b_in['W_mix'], 'L0_attn_b_D': _L0_attn_b_in['D'], 'L0_attn_b_ln_gamma': _L0_attn_b_in['ln_gamma'], 'L0_attn_b_ln_beta': _L0_attn_b_in['ln_beta'], 'L0_attn_b_W_out': _L0_attn_b_in['W_out'], 'L0_ffn_router_w': _L0_ffn_in['router_w'], 'L0_ffn_gate_w': _L0_ffn_in['gate_w'], 'L0_ffn_gate_b': _L0_ffn_in['gate_b'], 'L0_ffn_up_w': _L0_ffn_in['up_w'], 'L0_ffn_up_b': _L0_ffn_in['up_b'], 'L0_ffn_down_w': _L0_ffn_in['down_w'], 'L0_ffn_down_b': _L0_ffn_in['down_b']}
    _x0 = _d['L0_attn_a_x']
    _d['L0_attn_a_x'] = jax.random.normal(jax.random.fold_in(jax.random.key(seed), 1), (16, 512, 128), dtype=_x0.dtype)
    del _x0
    return _d

def reference(L0_attn_a_x, L0_attn_a_qkv_w, L0_attn_a_qkv_b, L0_attn_a_out_w, L0_attn_a_out_b, L0_attn_b_W_in, L0_attn_b_W_x, L0_attn_b_W_dt, L0_attn_b_b_dt, L0_attn_b_A_log, L0_attn_b_W_bc, L0_attn_b_W_zy, L0_attn_b_W_mix, L0_attn_b_D, L0_attn_b_ln_gamma, L0_attn_b_ln_beta, L0_attn_b_W_out, L0_ffn_router_w, L0_ffn_gate_w, L0_ffn_gate_b, L0_ffn_up_w, L0_ffn_up_b, L0_ffn_down_w, L0_ffn_down_b):

    def _L0_attn_a_ref(x, qkv_w, qkv_b, out_w, out_b):
        import jax, jax.numpy as jnp
        import numpy as np
        D_MODEL = 128
        N_HEADS = 16
        HEAD_DIM = D_MODEL // N_HEADS
        SCALE = HEAD_DIM ** (-0.5)

        def apply_rotary(x):
            seq_len = x.shape[-2]
            freqs = 10000.0 ** (jnp.arange(0, HEAD_DIM, 2.0, dtype=jnp.float32) / HEAD_DIM)
            t = jnp.arange(seq_len, dtype=jnp.float32)
            angles = t[:, None] * freqs[None, :]
            sin = jnp.sin(angles)[None, None]
            cos = jnp.cos(angles)[None, None]
            x1, x2 = (x[..., ::2], x[..., 1::2])
            return jnp.concatenate([x1 * cos - x2 * sin, x2 * cos + x1 * sin], axis=-1)
        B, T, D = x.shape
        qkv = x @ qkv_w + qkv_b
        q, k, v = jnp.split(qkv, 3, axis=-1)

        def to_heads(a):
            return a.reshape(B, T, N_HEADS, HEAD_DIM).transpose(0, 2, 1, 3)
        q, k, v = (to_heads(q), to_heads(k), to_heads(v))
        q = apply_rotary(q)
        k = apply_rotary(k)
        scores = jnp.einsum('bhqd,bhkd->bhqk', q, k) * SCALE
        weights = jax.nn.softmax(scores, axis=-1)
        attn = jnp.einsum('bhqk,bhkd->bhqd', weights, v)
        attn = attn.transpose(0, 2, 1, 3).reshape(B, T, D)
        return attn @ out_w + out_b

    def _L0_attn_b_ref(hidden_states, W_in, W_x, W_dt, b_dt, A_log, W_bc, W_zy, W_mix, D, ln_gamma, ln_beta, W_out):
        import jax, jax.numpy as jnp
        import numpy as np
        D_MODEL = 128
        EXPAND = 2
        D_INNER = EXPAND * D_MODEL
        D_STATE = 16
        DT_RANK = (D_MODEL + 15) // 16
        EPS = 1e-05
        FP_ITERS = 8
        STEP = 0.99
        B_SZ, L_SEQ = (2, 256)

        def _shift1(y):
            return jnp.pad(y, ((0, 0), (1, 0), (0, 0)))[:, :-1, :]

        def _selective_scan(u, delta, A, Bm, Cm, D):

            def step(h, inp):
                dt_t, u_t, b_t, c_t = inp
                h = jnp.exp(dt_t[:, :, None] * A) * h + (dt_t * u_t)[:, :, None] * b_t[:, None, :]
                y = jnp.einsum('bdn,bn->bd', h, c_t) + D * u_t
                return (h, y)
            b, l, d = u.shape
            h0 = jnp.zeros((b, d, A.shape[1]), u.dtype)
            xs = tuple((jnp.moveaxis(a, 1, 0) for a in (delta, u, Bm, Cm)))
            _, ys = jax.lax.scan(step, h0, xs)
            return jnp.moveaxis(ys, 0, 1)
        xz = hidden_states @ W_in.T
        x, z = (xz[..., :D_INNER], xz[..., D_INNER:])
        x_dbl = x @ W_x.T
        dt_low = x_dbl[..., :DT_RANK]
        B0 = x_dbl[..., DT_RANK:DT_RANK + D_STATE]
        C0 = x_dbl[..., DT_RANK + D_STATE:]
        delta = jax.nn.softplus(dt_low @ W_dt.T + b_dt)
        A = -jnp.exp(A_log)

        def layer_norm(y):
            m = jnp.mean(y, -1, keepdims=True)
            v = jnp.var(y, -1, keepdims=True)
            return ln_gamma * (y - m) * jax.lax.rsqrt(v + EPS) + ln_beta

        def bc_normalize(v):
            n = jnp.linalg.norm(v, axis=-1, keepdims=True)
            return v / jnp.maximum(n, EPS)

        def fp_step(y_prev):
            x_tilde = (x - y_prev) @ W_mix.T + y_prev
            bc = _shift1(y_prev) @ W_bc.T
            Bt = bc_normalize(B0 + bc[..., :D_STATE])
            Ct = bc_normalize(C0 + bc[..., D_STATE:])
            y = _selective_scan(x_tilde, delta, A, Bt, Ct, D)
            return layer_norm(y)
        y0 = jnp.zeros_like(x)
        y_star = jax.lax.fori_loop(0, FP_ITERS, lambda i, y: y + STEP * (fp_step(y) - y), y0)
        y_star = jax.lax.stop_gradient(y_star)
        y = fp_step(y_star)
        z2 = z + _shift1(y) @ W_zy.T
        return jax.nn.silu(z2) * y @ W_out.T

    def _L0_ffn_ref(x, router_w, gate_w, gate_b, up_w, up_b, down_w, down_b):
        import jax, jax.numpy as jnp
        import numpy as np
        D_MODEL, D_FF, N_EXPERTS, TOP_K = (128, 256, 8, 2)
        B, S = (2, 256)
        b, s, d = x.shape
        xf = x.reshape(b * s, d)
        n = xf.shape[0]
        router_logits = xf @ router_w.T
        probs = jax.nn.softmax(router_logits, axis=-1)
        topv, topi = jax.lax.top_k(probs, TOP_K)
        mask = jnp.zeros_like(probs).at[jnp.arange(n)[:, None], topi].set(1.0)
        probs = probs * mask
        probs = probs / (probs.sum(axis=-1, keepdims=True) + 1e-09)
        g = jnp.einsum('nd,edf->nef', xf, gate_w) + gate_b
        u = jnp.einsum('nd,edf->nef', xf, up_w) + up_b
        h = jax.nn.silu(g) * u
        expert_out = jnp.einsum('nef,efd->ned', h, down_w) + down_b
        y = jnp.einsum('ne,ned->nd', probs, expert_out)
        return y.reshape(b, s, d)
    x = L0_attn_a_x
    x = x + _L0_attn_a_ref(_layernorm(x, axis=-1), L0_attn_a_qkv_w, L0_attn_a_qkv_b, L0_attn_a_out_w, L0_attn_a_out_b)
    x = x + _L0_ffn_ref(_layernorm(x, axis=-1), L0_ffn_router_w, L0_ffn_gate_w, L0_ffn_gate_b, L0_ffn_up_w, L0_ffn_up_b, L0_ffn_down_w, L0_ffn_down_b)
    x = x + _L0_attn_b_ref(_layernorm(x, axis=-1), L0_attn_b_W_in, L0_attn_b_W_x, L0_attn_b_W_dt, L0_attn_b_b_dt, L0_attn_b_A_log, L0_attn_b_W_bc, L0_attn_b_W_zy, L0_attn_b_W_mix, L0_attn_b_D, L0_attn_b_ln_gamma, L0_attn_b_ln_beta, L0_attn_b_W_out)
    x = x + _L0_ffn_ref(_layernorm(x, axis=-1), L0_ffn_router_w, L0_ffn_gate_w, L0_ffn_gate_b, L0_ffn_up_w, L0_ffn_up_b, L0_ffn_down_w, L0_ffn_down_b)
    return x

_drawn_inputs = setup_inputs


def setup_inputs(seed=0):
    import zlib

    import numpy as np

    out = dict(_drawn_inputs(seed))
    spreads = {'L0_attn_a_qkv_b': (0.0, 0.1),
     'L0_attn_a_out_b': (0.0, 0.1),
     'L0_attn_b_D': (1.0, 0.2),
     'L0_attn_b_ln_gamma': (1.0, 0.2),
     'L0_attn_b_ln_beta': (0.0, 0.1),
     'L0_ffn_gate_b': (0.0, 0.1),
     'L0_ffn_up_b': (0.0, 0.1),
     'L0_ffn_down_b': (0.0, 0.1)}
    factors = {}
    for name, (base, spread) in spreads.items():
        noise = np.random.default_rng([zlib.crc32(name.encode()), seed]).standard_normal(out[name].shape)
        drawn = base * np.exp(spread * noise) if base else spread * noise
        out[name] = jnp.asarray(drawn.astype(out[name].dtype))
    for name, factor in factors.items():
        out[name] = (out[name] * factor).astype(out[name].dtype)
    return out
```

```python
from contextlib import ExitStack

import numpy as np
import concourse.bass as bass
from concourse import mybir

P = 128
F32 = mybir.dt.float32
U32 = mybir.dt.uint32
ALU = mybir.AluOpType
ACT = mybir.ActivationFunctionType
AX = mybir.AxisListType.X

B, T, DM = 16, 512, 128
TB = T // P
NH, HD = 16, 8
HG = 4
SCALE = HD ** -0.5
NE, DF = 8, 256
FB = DF // P
DI, NS, DR = 256, 16, 8
DB = DI // P
GC = 8
NG = DI // GC
NR = 32 // GC
ITERS, STEP, EPS = 8, 0.99, 1e-5
TH = T // 2
HB = TH // P
RING = (0, 1, 2, 4)
NHID, NPROD = 8, 8
PE_X, PE_Z, PE_V, PE_Y, PE_C, PE_D = 3, 3, 7, 9, 11, 15
DVE_VAR, DVE_NORM, DVE_Y, DVE_BC, DVE_BCN, DVE_DU, DVE_FILL = 7, 9, 12, 16, 18, 19, 22
LAG = 2
ORDER = [16 * h + NR * q + r for h in range(DB) for r in range(NR) for q in range(4)]


class Place:

    def __init__(self, seq, section, turn=0):
        self.seq, self.section, self.turn = seq, section, turn


class Signal:

    def __init__(self, sem, before, turn, behind, unit=1):
        self.sem, self.n, self.unit = sem, (before, turn, behind), unit
        self.seen = [0, 0, 0]
        self.total = before + ITERS * turn + behind

    def up(self, at):
        self.seen[at.section] += 1
        return self.unit

    def count(self, at, k):
        before, turn, _ = self.n
        skipped = (0, before, before + ITERS * turn)[at.section]
        value = at.seq * (self.total * self.unit) + (skipped + k) * self.unit
        return value + at.turn * (turn * self.unit) if at.section == 1 else value

    def last(self, at):
        return self.count(at, self.seen[at.section])


def hybrid_kernel(nc, t, out):
    with ExitStack() as ctx:
        sems = []

        def sb(name, shape, dt=F32):
            return ctx.enter_context(nc.sbuf_tensor(name, shape, dt))

        def signal(name, before=0, turn=0, behind=0, unit=1):
            s = Signal(ctx.enter_context(nc.semaphore(name)), before, turn, behind, unit)
            sems.append((name, s))
            return s

        ps = ctx.enter_context(nc.psum_tensor("ps", [P, 8, 512], F32))

        WEIGHTS = {
            "ident": [P, P], "sel": [P, NR, 32], "cosine": [P, TB, 4], "sine": [P, TB, 4],
            "headmask": [P, NH], "experts": [P, NE],
            "qkv_w": [P, 3 * DM], "qkv_b": [P, 3 * DM], "out_w": [P, DM], "out_b": [P, DM],
            "w_in": [P, 2 * DI], "w_x": [P, DB, DR + 2 * NS], "a_log": [P, NG],
            "w_bc": [P, DB, 2 * NS], "w_zy": [P, DB, DI], "w_mix": [P, DB, DI],
            "skip": [P, DI], "gamma": [P, DB], "beta": [P, DB], "w_out": [P, DB, DM],
            "router": [P, NE], "gate_b": [P, NE, FB],
            "up_b": [P, NE, FB],
        }
        w = {name: sb("w_" + name, shape) for name, shape in WEIGHTS.items()}
        w_dt = sb("w_dt", [DR + 1, DI])
        down_b = sb("down_b", [NE, DM])
        ident = w["ident"]

        eps = sb("eps", [P, 1])
        one = sb("one", [P, 1])
        held = sb("held", [P, 32])
        gamma_s = sb("gamma_s", [P, DB])
        beta_s = sb("beta_s", [P, DB])
        decay = sb("decay", [P, NG])
        mix_y = sb("mix_y", [P, DB, DI])
        hend = sb("hend", [P, NG])
        mix_yd = sb("mix_yd", [P, DB, DI])

        x_in = sb("x_in", [P, TB, DM])
        x_res = sb("x_res", [P, TB, DM])
        x_out = sb("x_out", [P, TB, DM])
        xnT = sb("xnT", [P, T])
        stats = sb("stats", [P, TB, 6])
        meanvar = sb("meanvar", [P, TB, 2])
        std = sb("std", [P, TB])
        rstd = sb("rstd", [P, TB])
        nmr = sb("nmr", [P, TB])
        da = sb("da", [P, NG, T])
        region = da[:].rearrange("p g t -> p (g t)")
        used = [0]

        def piece(n):
            at, used[0] = used[0], used[0] + n
            assert used[0] <= NG * T
            return region[:, at:at + n]

        work = sb("work", [P, (NHID + NPROD) * TH])
        scan_in = sb("scan_in", [P, 2, HB, NG, NS, GC])
        third = scan_in[:].rearrange("p f b g n c -> p (f b g n c)")
        gate_w = third[:, 0:2048].rearrange("p (e f) -> p e f", e=NE)
        up_w = third[:, 2048:4096].rearrange("p (e f) -> p e f", e=NE)
        down_w = third[:, 4096:6144].rearrange("p (e f c) -> p e f c", e=NE, f=FB)
        scr = third[:, 6144:10240]

        def ring(at, n):
            return work[:, at * T:(at + n) * T].rearrange("p (k t) -> p k t", t=T)

        kmask = piece(NH * T).rearrange("p (h t) -> p h t", h=NH)
        probs = ring(0, 4)
        probsT = piece(HG * TB * T).rearrange("p (j k t) -> p j k t", j=HG, k=TB)
        vaug_flat = third[:, 10240:12288]
        vaug = vaug_flat.rearrange("p (b h r) -> p b h r", b=TB, h=NH)
        qkv = scr[:, 0:TB * 384].rearrange("p (b c) -> p b c", b=TB)
        rot = scr[:, 1536:2560].rearrange("p (b c) -> p b c", b=TB)
        rtmp = scr[:, 2560:3584].rearrange("p (k b c) -> p k b c", k=2, b=TB)
        QT = scr[:, 3584:4096]
        KT = work[:, 4 * T:5 * T]
        smax = sb("smax", [P, 8])
        nbias = sb("nbias", [P, 8])
        oT = work[:, 5 * T:6 * T]
        rsum = sb("rsum", [P, TB, HG])
        attn = work[:, 6 * T:7 * T].rearrange("p (b c) -> p b c", b=TB)
        attnT = work[:, 7 * T:8 * T]

        rt = sb("rt", [P, 8, TB, NE])
        top = sb("top", [P, TB, 8])
        topi = sb("topi", [P, TB, 8], U32)
        topf = sb("topf", [P, TB, 8])
        rs = sb("rs", [P, 4, TB])
        cT = sb("cT", [NE, T])
        xn = work[:, 7 * T:8 * T].rearrange("p (b c) -> p b c", b=TB)
        gs = ring(0, 2)
        hid = ring(2, 4).rearrange("p (e f) t -> p e f t", f=FB)
        acc = work[:, 6 * T:7 * T].rearrange("p (b c) -> p b c", b=TB)

        xT = ring(0, DB)
        yT = sb("yT", [P, DB, T + 1])
        x_mixed = sb("x_mixed", [P, TB, DI])
        x_skip = sb("x_skip", [P, TB, DI])
        x_bc = sb("x_bc", [P, TB, 2 * NS])
        dtlow = sb("dtlow", [DR + 1, T])
        delta = sb("delta", [P, TB, DI])
        sp = [scr[:, 1024 * k:1024 * (k + 1)] for k in range(4)]
        bcs = sb("bcs", [P, HB, 2, NS])
        bcq = sb("bcq", [P, HB, 2, NS])
        b_norm = sb("b_norm", [P, HB, NS])
        c_norm = sb("c_norm", [P, HB, NS, GC])
        ss = sb("ss", [P, HB * 2])
        nrm = sb("nrm", [P, HB * 2])
        rn = sb("rn", [P, HB * 2])
        du = sb("du", [P, HB, DI])
        crep = sb("crep", [P, 2, TH])
        hst = work[:, 0:NHID * TH].rearrange("p (k t) -> p k t", t=TH)
        prod = work[:, NHID * TH:].rearrange("p (k t) -> p k t", t=TH)
        yscT = sb("yscT", [P, DB, TH])
        vn = sb("vn", [P, HB, DI])
        ytmp = sb("ytmp", [P, DB, TH])
        gz = ring(0, 2)
        gy = ring(2, 2)

        loaded = ctx.enter_context(nc.semaphore("loaded"))
        prepared = ctx.enter_context(nc.semaphore("prepared"))
        prep_a = ctx.enter_context(nc.semaphore("prep_a"))
        prepared_v = ctx.enter_context(nc.semaphore("prepared_v"))
        x_loaded = signal("x_loaded", 1, unit=16)
        x_free = signal("x_free", 1)
        experts_loaded = signal("experts_loaded", behind=3, unit=16)
        out_ready = signal("out_ready", behind=1)
        stored = signal("stored", behind=1, unit=16)
        vchain = signal("vchain", 110, 16, 20)

        class Norm:

            def __init__(self, name, *n):
                self.var = signal(name + "_var", *n)
                self.std = signal(name + "_std", *n)
                self.xn = signal(name + "_xn", *n)
                self.turned = signal(name + "_turned", *n)
                self.xnT = signal(name + "_xnT", *n)

        n_att, n_moe, n_ssm = Norm("na", 1), Norm("nm", 1, 0, 1), Norm("ns", 1)
        qkv_done = signal("qkv_done", 1)
        rot_done = signal("rot_done", 1)
        qk_turned = signal("qk_turned", 1)
        kt_copied = signal("kt_copied", 1)
        qt_copied = signal("qt_copied", 1)
        kmasked = signal("kmasked", NH)
        v_zero = signal("v_zero", 1)
        v_ready = signal("v_ready", 1)
        scored = signal("scored", NH * TB)
        maxed = signal("maxed", NH * TB)
        exped = signal("exped", NH * TB)
        p_turned = signal("p_turned", NH)
        p_copied_v = signal("p_copied_v", NH)
        p_copied_a = signal("p_copied_a", NH)
        pv_done = signal("pv_done", NH // HG)
        o_copied = signal("o_copied", NH // HG)
        o_turned = signal("o_turned", NH // HG)
        o_normed = signal("o_normed", NH // HG)
        a_turned = signal("a_turned", 1)
        a_copied = signal("a_copied", 1)
        projected = signal("projected", 1)
        x1_ready = signal("x1_ready", 1)

        routed = signal("routed", 1, 0, 1)
        r_shift = signal("r_shift", 1, 0, 1)
        r_exp = signal("r_exp", 1, 0, 1)
        r_comb = signal("r_comb", 1, 0, 1)
        c_turned = signal("c_turned", 1, 0, 1)
        comb_copied = signal("comb_copied", 1, 0, 1)
        biased = signal("biased", 1, 0, 1)
        nf = NE * FB
        gated = signal("gated", nf, 0, nf)
        upped = signal("upped", nf, 0, nf)
        silued = signal("silued", nf, 0, nf)
        hidden = signal("hidden", nf, 0, nf)
        downed = signal("downed", NE, 0, NE)
        summed = signal("summed", NE, 0, NE)

        xT_done = signal("xT_done", 1)
        xT_copied = signal("xT_copied", 1)
        dt_done = signal("dt_done", 1)
        dt_copied = signal("dt_copied", 1)
        dl_done = signal("dl_done", 1)
        xmix_done = signal("xmix_done", 1)
        x_mixed_a = signal("x_mixed_a", 1)
        dl_copied = signal("dl_copied", 1)
        dl_neg = signal("dl_neg", 1)
        dl_exp = signal("dl_exp", 1)
        dl_ln = signal("dl_ln", 1)
        dl_inv = signal("dl_inv", 1)
        dl_ready = signal("dl_ready", 1)
        expanded = signal("expanded", 1)
        expanded_a = signal("expanded_a", 1)
        dl_rep = signal("dl_rep", NG)
        da_ready = signal("da_ready", NG)

        y_ready = signal("y_ready", 1, 2, 2)
        front = (2, 2, 0)
        bc_done = signal("bc_done", *front)
        ss_done = signal("ss_done", *front)
        nrm_done = signal("nrm_done", *front)
        c_ready = signal("c_ready", *front)
        b_ready = signal("b_ready", *front)
        u_done = signal("u_done", *front)
        du_done = signal("du_done", *front)
        c_rep = signal("c_rep", *front)
        c_copied = signal("c_copied", *front)
        filled_a = signal("filled_a", *front)
        filled_v = signal("filled_v", *front)
        scan = (1, 2, 1)
        in_turned = signal("in_turned", *(NG // 2 * n for n in scan))
        scanned = signal("scanned", *(NG * n for n in scan))
        prod_done = signal("prod_done", *(NG // 2 * n for n in scan))
        nsummed = signal("nsummed", NG // 4 - LAG, 2 * NG // 4, NG // 4 + LAG)
        back = (0, 2, 2)
        ysc_copied = signal("ysc_copied", *back)
        z_done = signal("z_done", *back)
        zvar = signal("zvar", *back)
        zstd = signal("zstd", *back)
        znmr = signal("znmr", *back)
        v_done = signal("v_done", *back)
        vt_done = signal("vt_done", *back)
        ytmp_done = signal("ytmp_done", 0, 2, 0)
        z2_done = signal("z2_done", behind=1)
        z2_silu = signal("z2_silu", behind=1)
        gy_done = signal("gy_done", behind=1)
        o2_done = signal("o2_done", behind=1)
        x3_ready = signal("x3_ready", behind=1)

        bank = lambda n: ps[:, n, :]
        blocks = lambda n: ps[:, n, :].rearrange("p (b c) -> p b c", b=TB)
        wide = ps[:, 5:7, :].rearrange("p k c -> p (k c)").rearrange("p (b c) -> p b c", b=TB)
        du_groups = lambda tb: du[:, tb, :].rearrange("p (g c) -> p g c", c=GC)
        repeated = lambda tb: delta[:, tb, :].rearrange(
            "p (g o c) -> p g o c", o=1, c=GC).broadcast_to([P, NG, NS, GC])
        half5 = ps[:, 5, :].rearrange("p (b c) -> p b c", b=HB)
        half6 = ps[:, 6, :].rearrange("p (b c) -> p b c", b=HB)
        n_loads = len(WEIGHTS) + 2

        block = ctx.enter_context(nc.Block())

        @block.sync
        def _(eng):
            x_t = t["x"].rearrange("b (k p) c -> b p k c", p=P)
            out_t = out.rearrange("b (k p) c -> b p k c", p=P)
            eng.dma_start(x_in[:], x_t[0]).then_inc(x_loaded.sem, 16)
            for name in WEIGHTS:
                eng.dma_start(w[name][:], t[name]).then_inc(loaded, 16)
            eng.dma_start(w_dt[0:DR, :], t["w_dt"]).then_inc(loaded, 16)
            eng.dma_start(w_dt[DR:DR + 1, :], t["b_dt"]).then_inc(loaded, 16)
            eng.dma_start(down_b[:], t["down_b"]).then_inc(stored.sem, 16)
            def load_experts():
                for dst, name in ((gate_w, "gate_w"), (up_w, "up_w"), (down_w, "down_w")):
                    eng.dma_start(dst, t[name]).then_inc(experts_loaded.sem, 16)

            load_experts()
            with eng.Fori(0, B - 1) as b:
                eng.wait_ge(x_free.sem, b + 1)
                eng.dma_start(x_in[:], x_t[b + 1]).then_inc(x_loaded.sem, 16)
                eng.wait_ge(z2_done.sem, b + 1)
                load_experts()
                eng.wait_ge(out_ready.sem, b + 1)
                eng.dma_start(out_t[b], x_out[:]).then_inc(stored.sem, 16)
            eng.wait_ge(z2_done.sem, B)
            load_experts()
            eng.wait_ge(out_ready.sem, B)
            eng.dma_start(out_t[B - 1], x_out[:]).then_inc(stored.sem, 16)
            eng.wait_ge(stored.sem, 16 * (B + 1))
            eng.wait_ge(experts_loaded.sem, 16 * 3 * (B + 1))
            x_loaded.seen[0] = x_free.n[0]
            stored.seen[2] = 1
            experts_loaded.seen[2] = 3

        @block.tensor
        def _(eng):
            def turn_norm(at, n, dst):
                eng.wait_ge(n.xn.sem, n.xn.count(at, 1))
                for tb in range(TB):
                    mm = eng.transpose(dst[:, tb, :], xn[:, tb, :], ident[:])
                mm.then_inc(n.turned.sem, n.turned.up(at))

            def attention(at):
                turn_norm(at, n_att, blocks(4))
                eng.wait_ge(n_att.xnT.sem, n_att.xnT.count(at, 1))
                for tb in range(TB):
                    mm = eng.matmul(ps[:, tb, 0:3 * DM], xnT[:, tb * P:(tb + 1) * P], w["qkv_w"][:],
                                    start=True, stop=True)
                mm.then_inc(qkv_done.sem, qkv_done.up(at))
                eng.wait_ge(rot_done.sem, rot_done.count(at, 1))
                for k in range(2):
                    for tb in range(TB):
                        mm = eng.transpose(blocks(5 + k)[:, tb, :], rot[:, tb, k * DM:(k + 1) * DM],
                                           ident[:])
                mm.then_inc(qk_turned.sem, qk_turned.up(at))

                def score(u):
                    h, qb = divmod(u, TB)
                    if qb == 0:
                        eng.wait_ge(kmasked.sem, kmasked.count(at, h + 1))
                    if u == 0:
                        eng.wait_ge(qt_copied.sem, qt_copied.count(at, 1))
                    if u >= 3:
                        eng.wait_ge(exped.sem, exped.count(at, u - 2))
                    mm = eng.matmul(bank(u % 3), QT[:, qb * P:(qb + 1) * P], kmask[:, h, :],
                                    start=True, stop=True)
                    mm.then_inc(scored.sem, scored.up(at))

                def turn(u):
                    h, qb = divmod(u, TB)
                    eng.wait_ge(exped.sem, exped.count(at, u + 1))
                    if qb == 0 and h > 0:
                        eng.wait_ge(p_copied_v.sem, p_copied_v.count(at, h))
                        eng.wait_ge(p_copied_a.sem, p_copied_a.count(at, h))
                    for kb in range(TB):
                        mm = eng.transpose(ps[:, 3 + kb, qb * P:(qb + 1) * P],
                                           probs[:, u % 4, kb * P:(kb + 1) * P], ident[:])
                    if qb == TB - 1:
                        mm.then_inc(p_turned.sem, p_turned.up(at))

                def weigh(c):
                    eng.wait_ge(p_copied_v.sem, p_copied_v.count(at, HG * (c + 1)))
                    eng.wait_ge(p_copied_a.sem, p_copied_a.count(at, HG * (c + 1)))
                    if c == 0:
                        eng.wait_ge(v_ready.sem, v_ready.count(at, 1))
                    else:
                        eng.wait_ge(o_normed.sem, o_normed.count(at, c))
                    for kb in range(TB):
                        for j in range(HG):
                            mm = eng.matmul(ps[32 * j:32 * j + 32, 7, :],
                                            vaug[:, kb, HG * c + j, :], probsT[:, j, kb, :],
                                            start=(kb == 0), stop=(kb == TB - 1))
                    mm.then_inc(pv_done.sem, pv_done.up(at))

                def turn_out(c):
                    eng.wait_ge(o_copied.sem, o_copied.count(at, c + 1))
                    for tb in range(TB):
                        mm = eng.transpose(blocks(7)[:, tb, :], oT[:, tb * P:(tb + 1) * P], ident[:])
                    mm.then_inc(o_turned.sem, o_turned.up(at))

                units = NH * TB
                for u in range(units + 8):
                    if u < units:
                        score(u)
                    if 2 <= u < units + 2:
                        turn(u - 2)
                    if u >= 19 and (u - 19) % 16 == 0:
                        weigh((u - 19) // 16)
                    if u >= 21 and (u - 21) % 16 == 0:
                        turn_out((u - 21) // 16)
                eng.wait_ge(o_normed.sem, o_normed.count(at, NH // HG))
                for tb in range(TB):
                    mm = eng.transpose(blocks(7)[:, tb, :], attn[:, tb, :], ident[:])
                mm.then_inc(a_turned.sem, a_turned.up(at))
                eng.wait_ge(a_copied.sem, a_copied.count(at, 1))
                for tb in range(TB):
                    mm = eng.matmul(blocks(6)[:, tb, :], attnT[:, tb * P:(tb + 1) * P],
                                    w["out_w"][:], start=(tb == 0), stop=(tb == TB - 1))
                mm.then_inc(projected.sem, projected.up(at))

            def mixture(at):
                turn_norm(at, n_moe, blocks(4))
                eng.wait_ge(experts_loaded.sem, experts_loaded.count(at, 3 if at.section == 0 else 6))
                eng.wait_ge(n_moe.xnT.sem, n_moe.xnT.count(at, 1))
                for tb in range(TB):
                    mm = eng.matmul(ps[:, 5, tb * NE:(tb + 1) * NE], xnT[:, tb * P:(tb + 1) * P],
                                    w["router"][:], start=(tb == 0), stop=(tb == TB - 1))
                mm.then_inc(routed.sem, routed.up(at))

                def into(u):
                    e, f = divmod(u, FB)
                    if u >= 2:
                        eng.wait_ge(silued.sem, silued.count(at, u - 1))
                    mm = eng.matmul(bank(u % 2), gate_w[:, e, f * P:(f + 1) * P], xnT[:],
                                    start=True, stop=True)
                    mm.then_inc(gated.sem, gated.up(at))
                    if u >= 2:
                        eng.wait_ge(hidden.sem, hidden.count(at, u - 1))
                    mm = eng.matmul(bank(2 + u % 2), up_w[:, e, f * P:(f + 1) * P], xnT[:],
                                    start=True, stop=True)
                    mm.then_inc(upped.sem, upped.up(at))

                def down(e):
                    eng.wait_ge(hidden.sem, hidden.count(at, FB * (e + 1)))
                    if e >= 2:
                        eng.wait_ge(summed.sem, summed.count(at, e - 1))
                    for tb in range(TB):
                        for f in range(FB):
                            mm = eng.matmul(blocks(6 + e % 2)[:, tb, :],
                                            hid[:, e % 2, f, tb * P:(tb + 1) * P],
                                            down_w[:, e, f, :], start=(tb == 0 and f == 0),
                                            stop=(tb == TB - 1 and f == FB - 1))
                    mm.then_inc(downed.sem, downed.up(at))

                for u in range(4):
                    into(u)
                eng.wait_ge(r_comb.sem, r_comb.count(at, 1))
                for tb in range(TB):
                    mm = eng.transpose(ps[0:NE, 5, tb * P:(tb + 1) * P], rt[:, 7, tb, :], ident[:])
                mm.then_inc(c_turned.sem, c_turned.up(at))
                eng.wait_ge(comb_copied.sem, comb_copied.count(at, 1))
                for tb in range(TB):
                    mm = eng.matmul(blocks(4)[:, tb, :], cT[:, tb * P:(tb + 1) * P], down_b[:],
                                    start=(tb == 0), stop=(tb == TB - 1))
                mm.then_inc(biased.sem, biased.up(at))
                for e in range(NE):
                    if e < NE - 2:
                        down(e)
                        into(2 * e + 4)
                        into(2 * e + 5)
                    else:
                        down(e)

            def ssm_inputs(at):
                turn_norm(at, n_ssm, blocks(4))
                eng.wait_ge(n_ssm.xnT.sem, n_ssm.xnT.count(at, 1))
                for h in range(DB):
                    mm = eng.matmul(bank(5 + h), w["w_in"][:, h * P:(h + 1) * P], xnT[:],
                                    start=True, stop=True)
                mm.then_inc(xT_done.sem, xT_done.up(at))
                eng.wait_ge(xT_copied.sem, xT_copied.count(at, 1))
                for h in range(DB):
                    mm = eng.matmul(ps[0:DR, 4, :], w["w_x"][:, h, 0:DR], xT[:, h, :],
                                    start=(h == 0), stop=(h == DB - 1))
                mm.then_inc(dt_done.sem, dt_done.up(at))
                eng.wait_ge(dt_copied.sem, dt_copied.count(at, 1))
                for tb in range(TB):
                    mm = eng.matmul(wide[:, tb, :], dtlow[:, tb * P:(tb + 1) * P], w_dt[:],
                                    start=(tb % 2 == 0), stop=(tb % 2 == 1))
                mm.then_inc(dl_done.sem, dl_done.up(at))
                for tb in range(TB):
                    for h in range(DB):
                        eng.matmul(ps[:, 7, tb * 32:(tb + 1) * 32], xT[:, h, tb * P:(tb + 1) * P],
                                   w["w_x"][:, h, DR:DR + 2 * NS], start=(tb == 0 and h == 0),
                                   stop=(tb == TB - 1 and h == DB - 1))
                for tb in range(TB):
                    for h in range(DB):
                        mm = eng.matmul(ps[:, tb // HB, (tb % HB) * DI:(tb % HB + 1) * DI],
                                        xT[:, h, tb * P:(tb + 1) * P], w["w_mix"][:, h, :],
                                        start=(tb % HB == 0 and h == 0),
                                        stop=(tb % HB == HB - 1 and h == DB - 1))
                mm.then_inc(xmix_done.sem, xmix_done.up(at))
                eng.wait_ge(x_mixed_a.sem, x_mixed_a.count(at, 1))
                front_x(at, 0, 0)
                front_y(at, 0, 0)
                eng.wait_ge(expanded.sem, expanded.count(at, 1))
                eng.wait_ge(expanded_a.sem, expanded_a.count(at, 1))
                for g in range(NG):
                    if g >= 4:
                        eng.wait_ge(da_ready.sem, da_ready.count(at, g - 3))
                    for tb in range(TB):
                        mm = eng.transpose(blocks(RING[g % 4])[:, tb, :], group(tb // HB, tb % HB, g),
                                           ident[:])
                    mm.then_inc(dl_rep.sem, dl_rep.up(at))
                    if g == 3:
                        front_c(at, 0, 0)

            def group(hf, tb, g):
                return scan_in[:, hf, tb, g].rearrange("p n c -> p (n c)")

            def tokens(hf, tb, shift=1):
                at = (hf * HB + tb) * P + shift
                return slice(at, at + P)

            def front_x(at, hf, kf):
                for tb in range(HB):
                    eng.matmul(ps[:, 7, tb * 32:(tb + 1) * 32], ident[:], x_bc[:, hf * HB + tb, :],
                               start=(tb == 0), stop=False)
                for tb in range(HB):
                    eng.matmul(half6[:, tb, :], ident[:], x_mixed[:, hf * HB + tb, :],
                               start=(tb == 0), stop=False)

            def front_y(at, hf, kf):
                eng.wait_ge(y_ready.sem, y_ready.count(at, kf + 1 if at.section else 1))
                for tb in range(HB):
                    for h in range(DB):
                        mm = eng.matmul(ps[:, 7, tb * 32:(tb + 1) * 32], yT[:, h, tokens(hf, tb, 0)],
                                        w["w_bc"][:, h, :], start=False,
                                        stop=(tb == HB - 1 and h == DB - 1))
                mm.then_inc(bc_done.sem, bc_done.up(at))
                for tb in range(HB):
                    for h in range(DB):
                        mm = eng.matmul(half6[:, tb, :], yT[:, h, tokens(hf, tb)], mix_y[:, h, :],
                                        start=False, stop=(tb == HB - 1 and h == DB - 1))
                mm.then_inc(u_done.sem, u_done.up(at))

            def front_c(at, hf, kf):
                eng.wait_ge(c_ready.sem, c_ready.count(at, kf + 1))
                for tb in range(HB):
                    mm = eng.transpose(ps[:, 7, TH + tb * P:TH + (tb + 1) * P],
                                       c_norm[:, tb].rearrange("p n c -> p (n c)"), ident[:])
                mm.then_inc(c_rep.sem, c_rep.up(at))

            def back_d(at, hf):
                for tb in range(HB):
                    eng.matmul(half5[:, tb, :], ident[:], x_skip[:, hf * HB + tb, :],
                               start=(tb == 0), stop=False)
                    for h in range(DB):
                        eng.matmul(half5[:, tb, :], yT[:, h, tokens(hf, tb)], mix_yd[:, h, :],
                                   start=False, stop=False)

            def back_z(at, hf, kb):
                eng.wait_ge(ysc_copied.sem, ysc_copied.count(at, kb + 1))
                for tb in range(HB):
                    for h in range(DB):
                        mm = eng.matmul(half5[:, tb, h * P:(h + 1) * P],
                                        yscT[:, h, tb * P:(tb + 1) * P], ident[:], start=False,
                                        stop=(tb == HB - 1 and h == DB - 1))
                mm.then_inc(z_done.sem, z_done.up(at))

            def back_v(at, hf, kb):
                eng.wait_ge(v_done.sem, v_done.count(at, kb + 1))
                for h in range(DB):
                    for tb in range(HB):
                        mm = eng.transpose(ps[:, 5, h * TH + tb * P:h * TH + (tb + 1) * P],
                                           vn[:, tb, h * P:(h + 1) * P], ident[:])
                mm.then_inc(vt_done.sem, vt_done.up(at))

            def sum_states(at, ks, k):
                eng.wait_ge(prod_done.sem, prod_done.count(at, NG // 2 * ks + 2 * k + 2))
                for s in range(4 * k, 4 * k + 4):
                    g = ORDER[s]
                    q, r, h = (g // NR) % 4, g % NR, g // 16
                    mm = eng.matmul(ps[32 * q:32 * q + 32, 3, h * TH:(h + 1) * TH],
                                    w["sel"][:, r, :], prod[:, s % NPROD, :],
                                    start=(r == 0), stop=(r == NR - 1))
                mm.then_inc(nsummed.sem, nsummed.up(at))

            def scan_unit(at, hf, ks, filled, kb, kf):
                other = 1 - hf
                follows = kb is not None
                for p in range(NG // 2):
                    if p == 0:
                        eng.wait_ge(filled_a.sem, filled_a.count(at, filled))
                        eng.wait_ge(filled_v.sem, filled_v.count(at, filled))
                    if p >= 4 or follows:
                        eng.wait_ge(scanned.sem, scanned.count(at, NG * ks + 2 * (p - 4) + 2))
                    for s in (2 * p, 2 * p + 1):
                        for tb in range(HB):
                            c = (s % 2) * TH + tb * P
                            mm = eng.transpose(ps[:, RING[p % 4], c:c + P], group(hf, tb, ORDER[s]),
                                               ident[:])
                    mm.then_inc(in_turned.sem, in_turned.up(at))
                    if follows and p < LAG:
                        sum_states(at, ks - 1, NG // 4 - LAG + p)
                    if p == 5 and follows:
                        eng.wait_ge(ysc_copied.sem, ysc_copied.count(at, ks + 1))
                    if p >= 5 and p % 2 == 1:
                        sum_states(at, ks, (p - 5) // 2)
                    if p == PE_X and kf is not None:
                        front_x(at, other, kf)
                    if p == PE_Z and follows:
                        back_z(at, other, kb)
                    if p == PE_V and follows:
                        back_v(at, other, kb)
                    if p == (PE_Y if follows else 3) and kf is not None:
                        front_y(at, other, kf)
                    if p == (PE_C if follows else 6) and kf is not None:
                        front_c(at, other, kf)
                    if p == PE_D:
                        if kf is None:
                            eng.wait_ge(y_ready.sem, y_ready.count(at, 1))
                        back_d(at, hf)
                if kf is None:
                    for k in range(NG // 4 - LAG, NG // 4):
                        sum_states(at, ks, k)

            def ssm_output(at):
                eng.wait_ge(y_ready.sem, y_ready.count(at, 2))
                for e in range(DB):
                    eng.matmul(bank(e), w["w_in"][:, DI + e * P:DI + (e + 1) * P], xnT[:],
                               start=True, stop=False)
                    for h in range(DB):
                        mm = eng.matmul(bank(e), w["w_zy"][:, h, e * P:(e + 1) * P], yT[:, h, 0:T],
                                        start=False, stop=(h == DB - 1))
                mm.then_inc(z2_done.sem, z2_done.up(at))
                eng.wait_ge(gy_done.sem, gy_done.count(at, 1))
                for tb in range(TB):
                    for h in range(DB):
                        mm = eng.matmul(blocks(2)[:, tb, :], gy[:, h, tb * P:(tb + 1) * P],
                                        w["w_out"][:, h, :], start=(tb == 0 and h == 0),
                                        stop=(tb == TB - 1 and h == DB - 1))
                mm.then_inc(o2_done.sem, o2_done.up(at))

            eng.wait_ge(stored.sem, 16)
            eng.wait_ge(loaded, 16 * n_loads)
            eng.wait_ge(prepared, 1)
            with eng.Fori(0, B) as b:
                at = Place(b, 0)
                attention(at)
                mixture(at)
                ssm_inputs(at)
                scan_unit(at, 0, 0, 1, None, 1)
                with eng.Fori(0, ITERS) as i:
                    turn = Place(b, 1, i)
                    scan_unit(turn, 1, 0, 0, 0, 0)
                    scan_unit(turn, 0, 1, 1, 1, 1)
                at = Place(b, 2)
                scan_unit(at, 1, 0, 0, 0, None)
                back_z(at, 1, 1)
                back_v(at, 1, 1)
                ssm_output(at)
                mixture(at)

        @block.scalar
        def _(eng):
            def root(at, n):
                eng.wait_ge(n.var.sem, n.var.count(at, 1))
                eng.activation(std[:], meanvar[:, :, 1], ACT.Sqrt, bias=eps[:]).then_inc(n.std.sem, n.std.up(at))
                eng.wait_ge(n.turned.sem, n.turned.count(at, 1))
                eng.activation(xnT[:], bank(4), ACT.Copy).then_inc(n.xnT.sem, n.xnT.up(at))

            def attention(at):
                root(at, n_att)
                eng.wait_ge(qk_turned.sem, qk_turned.count(at, 1))
                eng.activation(KT, bank(6), ACT.Copy).then_inc(kt_copied.sem, kt_copied.up(at))
                eng.activation(QT, bank(5), ACT.Copy).then_inc(qt_copied.sem, qt_copied.up(at))

                def exp(u):
                    eng.wait_ge(maxed.sem, maxed.count(at, u + 1))
                    if u >= 4 and u % TB == 0:
                        eng.wait_ge(p_turned.sem, p_turned.count(at, u // TB))
                    eng.activation(probs[:, u % 4, :], bank(u % 3), ACT.Exp,
                                                bias=nbias[:, u % 8:u % 8 + 1], scale=SCALE).then_inc(exped.sem, exped.up(at))

                def copy(h):
                    eng.wait_ge(p_turned.sem, p_turned.count(at, h + 1))
                    if h >= HG and h % HG == 0:
                        eng.wait_ge(pv_done.sem, pv_done.count(at, h // HG))
                    for kb in (2, 3):
                        ins = eng.activation(probsT[:, h % HG, kb, :], bank(3 + kb), ACT.Copy)
                    ins.then_inc(p_copied_a.sem, p_copied_a.up(at))

                def copy_out(c):
                    eng.wait_ge(pv_done.sem, pv_done.count(at, c + 1))
                    eng.activation(oT, bank(7), ACT.Copy).then_inc(o_copied.sem, o_copied.up(at))

                units = NH * TB
                for u in range(units + 8):
                    if u < units:
                        exp(u)
                    if u >= 5 and (u - 5) % TB == 0 and (u - 5) // TB < NH:
                        copy((u - 5) // TB)
                    if u >= 20 and (u - 20) % 16 == 0:
                        copy_out((u - 20) // 16)
                eng.wait_ge(a_turned.sem, a_turned.count(at, 1))
                eng.activation(attnT, bank(7), ACT.Copy).then_inc(a_copied.sem, a_copied.up(at))

            def mixture(at):
                root(at, n_moe)
                eng.wait_ge(r_shift.sem, r_shift.count(at, 1))
                eng.activation(rt[:, 1], rt[:, 0], ACT.Exp).then_inc(r_exp.sem, r_exp.up(at))

                def silu(u):
                    e, f = divmod(u, FB)
                    eng.wait_ge(gated.sem, gated.count(at, u + 1))
                    if u >= 2:
                        eng.wait_ge(hidden.sem, hidden.count(at, u - 1))
                    eng.activation(gs[:, u % 2, :], bank(u % 2), ACT.Silu,
                                                 bias=w["gate_b"][:, e, f:f + 1]).then_inc(silued.sem, silued.up(at))

                for u in range(4):
                    silu(u)
                eng.wait_ge(c_turned.sem, c_turned.count(at, 1))
                eng.activation(cT[:], ps[0:NE, 5, :], ACT.Copy).then_inc(comb_copied.sem, comb_copied.up(at))
                for u in range(4, NE * FB):
                    silu(u)

            def ssm_inputs(at):
                root(at, n_ssm)
                eng.wait_ge(xT_done.sem, xT_done.count(at, 1))
                eng.activation(
                    xT.rearrange("p h t -> p (h t)"),
                    ps[:, 5:7, :].rearrange("p h t -> p (h t)"), ACT.Copy).then_inc(xT_copied.sem, xT_copied.up(at))
                eng.wait_ge(dt_done.sem, dt_done.count(at, 1))
                eng.activation(dtlow[0:DR, :], ps[0:DR, 4, :], ACT.Copy).then_inc(dt_copied.sem, dt_copied.up(at))
                eng.wait_ge(dl_done.sem, dl_done.count(at, 1))
                eng.activation(
                    sp[0], ps[:, 5:7, :].rearrange("p h t -> p (h t)"), ACT.Copy).then_inc(dl_copied.sem, dl_copied.up(at))
                eng.wait_ge(xmix_done.sem, xmix_done.count(at, 1))
                eng.activation(x_bc[:].rearrange("p b c -> p (b c)"), ps[:, 7, 0:P], ACT.Copy)
                eng.activation(x_mixed[:].rearrange("p b c -> p (b c)"),
                               ps[:, 0:2, :].rearrange("p k c -> p (k c)"), ACT.Copy
                               ).then_inc(x_mixed_a.sem, x_mixed_a.up(at))
                eng.wait_ge(dl_neg.sem, dl_neg.count(at, 1))
                eng.activation(sp[1], sp[1], ACT.Exp).then_inc(dl_exp.sem, dl_exp.up(at))
                eng.wait_ge(dl_exp.sem, dl_exp.count(at, 1))
                eng.activation(sp[3], sp[1], ACT.Ln, bias=one[:]).then_inc(dl_ln.sem, dl_ln.up(at))
                eng.wait_ge(dl_ln.sem, dl_ln.count(at, 1))
                eng.activation(delta[:].rearrange("p b c -> p (b c)"), sp[3], ACT.Exp, scale=-1.0
                               ).then_inc(dl_inv.sem, dl_inv.up(at))
                front_root(at, 0, 0)
                eng.wait_ge(dl_ready.sem, dl_ready.count(at, 1))
                eng.activation(scan_in[:, 1, HB - 1], repeated(TB - 1), ACT.Copy
                               ).then_inc(expanded_a.sem, expanded_a.up(at))
                for g in range(NG):
                    eng.wait_ge(dl_rep.sem, dl_rep.count(at, g + 1))
                    eng.activation(da[:, g, :], bank(RING[g % 4]), ACT.Exp,
                                   scale=decay[:, g:g + 1]).then_inc(da_ready.sem, da_ready.up(at))
                    if g == 7:
                        front_c(at, 0, 0)
                fill(at, 0, 0)

            def front_root(at, hf, kf):
                eng.wait_ge(ss_done.sem, ss_done.count(at, kf + 1))
                eng.activation(nrm[:], ss[:], ACT.Sqrt).then_inc(nrm_done.sem, nrm_done.up(at))

            def front_c(at, hf, kf):
                eng.wait_ge(c_rep.sem, c_rep.count(at, kf + 1))
                eng.activation(crep[:, hf, :], ps[:, 7, TH:T], ACT.Copy).then_inc(c_copied.sem, c_copied.up(at))

            def fill(at, hf, kf):
                eng.wait_ge(du_done.sem, du_done.count(at, kf + 1))
                eng.wait_ge(b_ready.sem, b_ready.count(at, kf + 1))
                for n in range(NS):
                    ins = eng.activation(scan_in[:, hf, 0, :, n, :], du_groups(0), ACT.Copy,
                                         scale=b_norm[:, 0, n:n + 1])
                ins.then_inc(filled_a.sem, filled_a.up(at))

            def front(at, hf, kf):
                front_root(at, hf, kf)
                front_c(at, hf, kf)
                fill(at, hf, kf)

            def back(at, hf, kb, last):
                cols = slice(hf * TH + 1, (hf + 1) * TH + 1)
                if not last:
                    for h in range(DB):
                        ins = eng.activation(ytmp[:, h, :], yT[:, h, cols], ACT.Identity,
                                             bias=beta_s[:, h:h + 1], scale=1.0 - STEP)
                    ins.then_inc(ytmp_done.sem, ytmp_done.up(at))
                eng.wait_ge(nsummed.sem, nsummed.count(at, LAG + NG // 4 * kb))
                eng.activation(yscT[:].rearrange("p h t -> p (h t)"), bank(3),
                                                 ACT.Copy).then_inc(ysc_copied.sem, ysc_copied.up(at))
                eng.wait_ge(zvar.sem, zvar.count(at, kb + 1))
                eng.activation(std[:, 0:HB], meanvar[:, 0:HB, 1], ACT.Sqrt, bias=eps[:]).then_inc(zstd.sem, zstd.up(at))
                eng.wait_ge(znmr.sem, znmr.count(at, kb + 1))
                for tb in range(HB):
                    ins = eng.activation(vn[:, tb, :], half5[:, tb, :], ACT.Identity,
                                         bias=nmr[:, tb:tb + 1], scale=rstd[:, tb:tb + 1])
                ins.then_inc(v_done.sem, v_done.up(at))
                if last:
                    eng.wait_ge(vt_done.sem, vt_done.count(at, kb + 1))
                    for h in range(DB):
                        ins = eng.activation(yT[:, h, cols], ps[:, 5, h * TH:(h + 1) * TH], ACT.Identity,
                                             bias=w["beta"][:, h:h + 1], scale=w["gamma"][:, h:h + 1])
                    ins.then_inc(y_ready.sem, y_ready.up(at))

            def ssm_output(at):
                eng.wait_ge(z2_done.sem, z2_done.count(at, 1))
                eng.activation(gz.rearrange("p h t -> p (h t)"),
                                              ps[:, 0:2, :].rearrange("p h t -> p (h t)"), ACT.Silu).then_inc(z2_silu.sem, z2_silu.up(at))

            eng.wait_ge(loaded, 16 * n_loads)
            eng.activation(decay[:], w["a_log"][:], ACT.Exp).then_inc(prep_a, 1)
            eng.wait_ge(prepared, 1)
            with eng.Fori(0, B) as b:
                at = Place(b, 0)
                attention(at)
                mixture(at)
                ssm_inputs(at)
                front(at, 1, 1)
                with eng.Fori(0, ITERS) as i:
                    turn = Place(b, 1, i)
                    for hf in range(2):
                        back(turn, hf, hf, False)
                        front(turn, hf, hf)
                at = Place(b, 2)
                back(at, 0, 0, True)
                back(at, 1, 1, True)
                ssm_output(at)
                mixture(at)

        @block.vector
        def _(eng):
            def hold(eng):
                holds.append(len(holds))
                eng.memset(held[:, holds[-1]:holds[-1] + 1], 0.0)

            holds = []

            def moments(at, src, done, nb=TB):
                for tb in range(nb):
                    ins = eng.bn_stats(stats[:, tb, :], src[:, tb, :])
                ins.then_inc(vchain.sem, vchain.up(at))
                eng.wait_ge(vchain.sem, vchain.last(at))
                hold(eng)
                for tb in range(nb):
                    ins = eng.bn_aggr(meanvar[:, tb, :], stats[:, tb, :])
                ins.then_inc(done.sem, done.up(at))

            def norm(at, n, src):
                moments(at, src, n.var)
                eng.wait_ge(n.std.sem, n.std.count(at, 1))
                eng.reciprocal(rstd[:], std[:]).then_inc(vchain.sem, vchain.up(at))
                eng.wait_ge(vchain.sem, vchain.last(at))
                for tb in range(TB):
                    ins = eng.tensor_scalar(xn[:, tb, :], src[:, tb, :], meanvar[:, tb, 0:1],
                                            rstd[:, tb:tb + 1], ALU.subtract, ALU.mult)
                ins.then_inc(n.xn.sem, n.xn.up(at))

            def attention(at):
                eng.wait_ge(x_loaded.sem, x_loaded.count(at, 1))
                norm(at, n_att, x_in)
                eng.tensor_tensor(x_res[:], x_in[:],
                                  w["out_b"][:].rearrange("p (o c) -> p o c", o=1).broadcast_to([P, TB, DM]),
                                  ALU.add)
                eng.memset(smax[:], 0.0).then_inc(x_free.sem, x_free.up(at))
                eng.wait_ge(qkv_done.sem, qkv_done.count(at, 1))
                eng.tensor_tensor(
                    qkv, ps[:, 0:4, 0:3 * DM],
                    w["qkv_b"][:].rearrange("p (o c) -> p o c", o=1).broadcast_to([P, TB, 3 * DM]), ALU.add).then_inc(vchain.sem, vchain.up(at))
                eng.wait_ge(vchain.sem, vchain.last(at))
                qk = qkv[:, :, 0:2 * DM].rearrange("p b (h j two) -> p two b h j", two=2, j=4)
                even, odd = qk[:, 0], qk[:, 1]
                r = rot.rearrange("p b (h two j) -> p two b h j", two=2, j=4)
                ta = rtmp[:, 0].rearrange("p b (h j) -> p b h j", j=4)
                tc = rtmp[:, 1].rearrange("p b (h j) -> p b h j", j=4)
                angles = [w[n][:].rearrange("p b (o j) -> p b o j", o=1).broadcast_to([P, TB, 2 * NH, 4])
                          for n in ("cosine", "sine")]
                for half, (first, second, op) in enumerate(((even, odd, ALU.subtract), (odd, even, ALU.add))):
                    eng.tensor_tensor(ta, first, angles[0], ALU.mult)
                    eng.tensor_tensor(tc, second, angles[1], ALU.mult).then_inc(vchain.sem, vchain.up(at))
                    eng.wait_ge(vchain.sem, vchain.last(at))
                    ins = eng.tensor_tensor(r[:, half], ta, tc, op)
                    if half == 0:
                        ins.then_inc(vchain.sem, vchain.up(at))
                        eng.wait_ge(vchain.sem, vchain.last(at))
                ins.then_inc(rot_done.sem, rot_done.up(at))
                eng.memset(vaug_flat, 0.0).then_inc(v_zero.sem, v_zero.up(at))
                eng.wait_ge(v_zero.sem, v_zero.count(at, 1))
                eng.memset(vaug[:, :, :, HD:HD + 1], 1.0).then_inc(vchain.sem, vchain.up(at))
                eng.wait_ge(vchain.sem, vchain.last(at))
                eng.tensor_copy(
                    vaug[:, :, :, 0:HD], qkv[:, :, 2 * DM:].rearrange("p b (h c) -> p b h c", c=HD)).then_inc(v_ready.sem, v_ready.up(at))

                def rowmax(u):
                    eng.wait_ge(scored.sem, scored.count(at, u + 1))
                    eng.tensor_reduce(smax[:, u % 8:u % 8 + 1], bank(u % 3), AX, ALU.max).then_inc(vchain.sem, vchain.up(at))
                    eng.wait_ge(vchain.sem, vchain.last(at))
                    eng.tensor_scalar(nbias[:, u % 8:u % 8 + 1], smax[:, u % 8:u % 8 + 1],
                                                   -SCALE, None, ALU.mult).then_inc(maxed.sem, maxed.up(at))

                def copy(h):
                    eng.wait_ge(p_turned.sem, p_turned.count(at, h + 1))
                    if h >= HG and h % HG == 0:
                        eng.wait_ge(pv_done.sem, pv_done.count(at, h // HG))
                    for kb in (0, 1):
                        ins = eng.tensor_copy(probsT[:, h % HG, kb, :], bank(3 + kb))
                    ins.then_inc(p_copied_v.sem, p_copied_v.up(at))

                def normalise(c):
                    eng.wait_ge(o_turned.sem, o_turned.count(at, c + 1))
                    o = blocks(7).rearrange("p b (j r) -> p b j r", r=32)
                    eng.reciprocal(rsum[:], o[:, :, :, HD]).then_inc(vchain.sem, vchain.up(at))
                    eng.wait_ge(vchain.sem, vchain.last(at))
                    dst = attn[:, :, c * HG * HD:(c + 1) * HG * HD].rearrange("p b (j r) -> p b j r", r=HD)
                    eng.tensor_tensor(
                        dst, o[:, :, :, 0:HD],
                        rsum[:].rearrange("p b (j o) -> p b j o", o=1).broadcast_to([P, TB, HG, HD]),
                        ALU.mult).then_inc(o_normed.sem, o_normed.up(at))

                units = NH * TB
                for u in range(units + 8):
                    if u < units:
                        rowmax(u)
                    if u >= 5 and (u - 5) % TB == 0 and (u - 5) // TB < NH:
                        copy((u - 5) // TB)
                    if u >= 22 and (u - 22) % 16 == 0:
                        normalise((u - 22) // 16)
                eng.wait_ge(projected.sem, projected.count(at, 1))
                eng.tensor_tensor(x_res[:], blocks(6), x_res[:], ALU.add).then_inc(x1_ready.sem, x1_ready.up(at))

            def mixture(at, dst, ready):
                norm(at, n_moe, x_res)
                eng.wait_ge(routed.sem, routed.count(at, 1))
                logits = ps[:, 5, 0:TB * NE].rearrange("p (b e) -> p b e", b=TB)
                per_token = lambda v: v.rearrange("p (b o) -> p b o", o=1).broadcast_to([P, TB, NE])
                eng.tensor_reduce(rs[:, 0], logits, AX, ALU.max).then_inc(vchain.sem, vchain.up(at))
                eng.wait_ge(vchain.sem, vchain.last(at))
                eng.tensor_tensor(rt[:, 0], logits, per_token(rs[:, 0]), ALU.subtract).then_inc(r_shift.sem, r_shift.up(at))
                eng.wait_ge(r_exp.sem, r_exp.count(at, 1))
                eng.tensor_reduce(rs[:, 1], rt[:, 1], AX, ALU.add).then_inc(vchain.sem, vchain.up(at))
                eng.wait_ge(vchain.sem, vchain.last(at))
                eng.reciprocal(rs[:, 2], rs[:, 1]).then_inc(vchain.sem, vchain.up(at))
                eng.wait_ge(vchain.sem, vchain.last(at))
                eng.tensor_tensor(rt[:, 2], rt[:, 1], per_token(rs[:, 2]), ALU.mult).then_inc(vchain.sem, vchain.up(at))
                eng.wait_ge(vchain.sem, vchain.last(at))
                hold(eng)
                for tb in range(TB):
                    ins = eng.max(top[:, tb, :], rt[:, 2, tb, :])
                ins.then_inc(vchain.sem, vchain.up(at))
                eng.wait_ge(vchain.sem, vchain.last(at))
                hold(eng)
                for tb in range(TB):
                    ins = eng.max_index(topi[:, tb, :], top[:, tb, :], rt[:, 2, tb, :])
                ins.then_inc(vchain.sem, vchain.up(at))
                eng.wait_ge(vchain.sem, vchain.last(at))
                eng.tensor_copy(topf[:], topi[:]).then_inc(vchain.sem, vchain.up(at))
                eng.wait_ge(vchain.sem, vchain.last(at))
                numbers = w["experts"][:].rearrange("p (o e) -> p o e", o=1).broadcast_to([P, TB, NE])
                eng.tensor_tensor(rt[:, 3], numbers, topf[:, :, 0:1].broadcast_to([P, TB, NE]), ALU.is_equal)
                eng.tensor_tensor(
                    rt[:, 4], numbers, topf[:, :, 1:2].broadcast_to([P, TB, NE]), ALU.is_equal).then_inc(vchain.sem, vchain.up(at))
                eng.wait_ge(vchain.sem, vchain.last(at))
                eng.tensor_tensor(rt[:, 5], rt[:, 3], rt[:, 4], ALU.add).then_inc(vchain.sem, vchain.up(at))
                eng.wait_ge(vchain.sem, vchain.last(at))
                eng.tensor_tensor(rt[:, 6], rt[:, 5], rt[:, 2], ALU.mult).then_inc(vchain.sem, vchain.up(at))
                eng.wait_ge(vchain.sem, vchain.last(at))
                eng.tensor_reduce(rs[:, 3], rt[:, 6], AX, ALU.add).then_inc(vchain.sem, vchain.up(at))
                eng.wait_ge(vchain.sem, vchain.last(at))
                eng.tensor_scalar(rs[:, 1], rs[:, 3], 1e-9, None, ALU.add).then_inc(vchain.sem, vchain.up(at))
                eng.wait_ge(vchain.sem, vchain.last(at))
                eng.reciprocal(rs[:, 2], rs[:, 1]).then_inc(vchain.sem, vchain.up(at))
                eng.wait_ge(vchain.sem, vchain.last(at))
                eng.tensor_tensor(rt[:, 7], rt[:, 6], per_token(rs[:, 2]), ALU.mult).then_inc(r_comb.sem, r_comb.up(at))

                def hide(u):
                    e, f = divmod(u, FB)
                    eng.wait_ge(upped.sem, upped.count(at, u + 1))
                    eng.wait_ge(silued.sem, silued.count(at, u + 1))
                    if e >= 2 and f == 0:
                        eng.wait_ge(downed.sem, downed.count(at, e - 1))
                    eng.scalar_tensor_tensor(
                        out=hid[:, e % 2, f, :], in0=bank(2 + u % 2), scalar=w["up_b"][:, e, f:f + 1],
                        in1=gs[:, u % 2, :], op0=ALU.add, op1=ALU.mult).then_inc(hidden.sem, hidden.up(at))

                def add_expert(e):
                    eng.wait_ge(downed.sem, downed.count(at, e + 1))
                    to = dst if e == NE - 1 else acc
                    for tb in range(TB):
                        ins = eng.scalar_tensor_tensor(
                            out=to[:, tb, :], in0=blocks(6 + e % 2)[:, tb, :],
                            scalar=rt[:, 7, tb, e:e + 1], in1=acc[:, tb, :], op0=ALU.mult, op1=ALU.add)
                    ins.then_inc(summed.sem, summed.up(at))
                    if e == NE - 1:
                        return ins
                    eng.wait_ge(summed.sem, summed.count(at, e + 1))

                for u in range(4):
                    hide(u)
                eng.wait_ge(biased.sem, biased.count(at, 1))
                eng.tensor_tensor(acc, blocks(4), x_res[:], ALU.add).then_inc(vchain.sem, vchain.up(at))
                eng.wait_ge(vchain.sem, vchain.last(at))
                for e in range(NE):
                    if e == NE - 1 and ready is not None:
                        eng.wait_ge(stored.sem, stored.count(at, 1))
                    add_expert(e)
                    if e < NE - 2:
                        hide(2 * e + 4)
                        hide(2 * e + 5)
                eng.wait_ge(summed.sem, summed.count(at, NE))
                if ready is not None:
                    eng.memset(rs[:, 0], 0.0).then_inc(ready.sem, ready.up(at))

            def ssm_inputs(at):
                norm(at, n_ssm, x_res)
                eng.memset(yT[:], 0.0).then_inc(y_ready.sem, y_ready.up(at))
                eng.wait_ge(dl_copied.sem, dl_copied.count(at, 1))
                eng.scalar_tensor_tensor(out=sp[1], in0=sp[0], scalar=-1.0, in1=sp[0],
                                         op0=ALU.mult, op1=ALU.min).then_inc(dl_neg.sem, dl_neg.up(at))
                eng.wait_ge(dl_exp.sem, dl_exp.count(at, 1))
                eng.tensor_scalar(sp[2], sp[1], 1.0, None, ALU.add).then_inc(vchain.sem, vchain.up(at))
                eng.wait_ge(vchain.sem, vchain.last(at))
                eng.scalar_tensor_tensor(out=sp[2], in0=sp[2], scalar=-1.0, in1=sp[1],
                                         op0=ALU.add, op1=ALU.subtract).then_inc(vchain.sem, vchain.up(at))
                front_bc(at, 0, 0)
                eng.wait_ge(dl_inv.sem, dl_inv.count(at, 1))
                flat = delta[:].rearrange("p b c -> p (b c)")
                eng.tensor_tensor(sp[2], sp[2], flat, ALU.mult).then_inc(vchain.sem, vchain.up(at))
                eng.wait_ge(vchain.sem, vchain.last(at))
                eng.tensor_tensor(sp[3], sp[3], sp[2], ALU.subtract).then_inc(vchain.sem, vchain.up(at))
                eng.wait_ge(vchain.sem, vchain.last(at))
                eng.scalar_tensor_tensor(out=flat, in0=sp[0], scalar=0.0, in1=sp[3],
                                         op0=ALU.max, op1=ALU.add).then_inc(dl_ready.sem, dl_ready.up(at))
                eng.wait_ge(dl_ready.sem, dl_ready.count(at, 1))
                for tb in range(TB - 1):
                    ins = eng.tensor_copy(scan_in[:, tb // HB, tb % HB], repeated(tb))
                ins.then_inc(expanded.sem, expanded.up(at))
                front_norm(at, 0, 0)
                front_du(at, 0, 0)
                eng.wait_ge(x_mixed_a.sem, x_mixed_a.count(at, 1))
                eng.tensor_tensor(x_skip[:], x_mixed[:],
                                  w["skip"][:].rearrange("p (o c) -> p o c", o=1).broadcast_to([P, TB, DI]),
                                  ALU.mult).then_inc(vchain.sem, vchain.up(at))
                eng.wait_ge(dl_rep.sem, dl_rep.count(at, NG))

            def front_bc(at, hf, kf):
                eng.wait_ge(bc_done.sem, bc_done.count(at, kf + 1))
                eng.tensor_copy(bcs[:].rearrange("p b k n -> p (b k n)"),
                                                 ps[:, 7, 0:HB * 2 * NS]).then_inc(vchain.sem, vchain.up(at))
                eng.wait_ge(vchain.sem, vchain.last(at))
                eng.tensor_tensor(bcq[:], bcs[:], bcs[:], ALU.mult).then_inc(vchain.sem, vchain.up(at))
                eng.wait_ge(vchain.sem, vchain.last(at))
                eng.tensor_reduce(ss[:], bcq[:].rearrange("p b k n -> p (b k) n"),
                                                 AX, ALU.add).then_inc(ss_done.sem, ss_done.up(at))

            def front_norm(at, hf, kf):
                eng.wait_ge(nrm_done.sem, nrm_done.count(at, kf + 1))
                eng.tensor_scalar(rn[:], nrm[:], EPS, None, ALU.max).then_inc(vchain.sem, vchain.up(at))
                eng.wait_ge(vchain.sem, vchain.last(at))
                eng.reciprocal(rn[:], rn[:]).then_inc(vchain.sem, vchain.up(at))
                eng.wait_ge(vchain.sem, vchain.last(at))
                r = rn[:].rearrange("p (b k) -> p k b", k=2)
                eng.tensor_tensor(
                    c_norm[:], bcs[:, :, 1, :].rearrange("p b (n o) -> p b n o", o=1).broadcast_to([P, HB, NS, GC]),
                    r[:, 1].rearrange("p (b o q) -> p b o q", o=1, q=1).broadcast_to([P, HB, NS, GC]),
                    ALU.mult).then_inc(c_ready.sem, c_ready.up(at))
                eng.tensor_tensor(
                    b_norm[:], bcs[:, :, 0, :],
                    r[:, 0].rearrange("p (b o) -> p b o", o=1).broadcast_to([P, HB, NS]), ALU.mult).then_inc(b_ready.sem, b_ready.up(at))

            def front_du(at, hf, kf):
                eng.wait_ge(u_done.sem, u_done.count(at, kf + 1))
                eng.tensor_tensor(du[:], half6, delta[:, hf * HB:(hf + 1) * HB, :],
                                                 ALU.mult).then_inc(du_done.sem, du_done.up(at))

            def fill(at, hf, kf, ns):
                if ns[0] == 0:
                    eng.wait_ge(du_done.sem, du_done.count(at, kf + 1))
                    eng.wait_ge(b_ready.sem, b_ready.count(at, kf + 1))
                for n in ns:
                    ins = eng.tensor_scalar(scan_in[:, hf, 1, :, n, :], du_groups(1),
                                            b_norm[:, 1, n:n + 1], None, ALU.mult)
                if ns[-1] == NS - 1:
                    ins.then_inc(filled_v.sem, filled_v.up(at))

            def back_var(at, hf, kb):
                eng.wait_ge(z_done.sem, z_done.count(at, kb + 1))
                moments(at, half5, zvar, HB)

            def back_norm(at, hf, kb):
                eng.wait_ge(zstd.sem, zstd.count(at, kb + 1))
                eng.reciprocal(rstd[:, 0:HB], std[:, 0:HB]).then_inc(vchain.sem, vchain.up(at))
                eng.wait_ge(vchain.sem, vchain.last(at))
                eng.scalar_tensor_tensor(
                    out=nmr[:, 0:HB], in0=meanvar[:, 0:HB, 0], scalar=-1.0, in1=rstd[:, 0:HB],
                    op0=ALU.mult, op1=ALU.mult).then_inc(znmr.sem, znmr.up(at))

            def back_y(at, hf, kb):
                eng.wait_ge(vt_done.sem, vt_done.count(at, kb + 1))
                eng.wait_ge(ytmp_done.sem, ytmp_done.count(at, kb + 1))
                for h in range(DB):
                    ins = eng.scalar_tensor_tensor(
                        out=yT[:, h, hf * TH + 1:(hf + 1) * TH + 1], in0=ps[:, 5, h * TH:(h + 1) * TH],
                        scalar=gamma_s[:, h:h + 1], in1=ytmp[:, h, :], op0=ALU.mult, op1=ALU.add)
                ins.then_inc(y_ready.sem, y_ready.up(at))

            def scan_unit(at, hf, ks, kb, kf):
                other = 1 - hf
                follows = kb is not None
                for s in range(NG):
                    if s % 2 == 0:
                        eng.wait_ge(in_turned.sem, in_turned.count(at, NG // 2 * ks + s // 2 + 1))
                        if s >= NHID or follows:
                            eng.wait_ge(prod_done.sem, prod_done.count(at, NG // 2 * ks + (s - NHID) // 2 + 1))
                    eng.tensor_tensor_scan(
                        hst[:, s % NHID, :], da[:, ORDER[s], hf * TH:(hf + 1) * TH],
                        ps[:, RING[s // 2 % 4], (s % 2) * TH:(s % 2 + 1) * TH],
                        0.0 if hf == 0 else hend[:, s:s + 1], ALU.mult, ALU.add
                    ).then_inc(scanned.sem, scanned.up(at))
                    if hf == 0 and s % NHID == NHID - 1:
                        eng.wait_ge(scanned.sem, scanned.count(at, NG * ks + s + 1))
                        eng.tensor_copy(hend[:, s - NHID + 1:s + 1], hst[:, :, TH - 1]
                                        ).then_inc(vchain.sem, vchain.up(at))
                        eng.wait_ge(vchain.sem, vchain.last(at))
                    if follows:
                        if s == DVE_VAR:
                            back_var(at, other, kb)
                        if s == DVE_NORM:
                            back_norm(at, other, kb)
                        if s == DVE_Y and kf is not None:
                            back_y(at, other, kb)
                    if kf is not None:
                        if s == (DVE_BC if follows else 8):
                            front_bc(at, other, kf)
                        if s == (DVE_BCN if follows else 11):
                            front_norm(at, other, kf)
                        if s == (DVE_DU if follows else 14):
                            front_du(at, other, kf)
                        n = 2 * (s - DVE_FILL)
                        if 0 <= n < NS:
                            fill(at, other, kf, (n, n + 1))

            def ssm_output(at):
                eng.wait_ge(z2_silu.sem, z2_silu.count(at, 1))
                eng.tensor_tensor(gy, gz, yT[:, :, 1:T + 1], ALU.mult).then_inc(gy_done.sem, gy_done.up(at))
                eng.wait_ge(o2_done.sem, o2_done.count(at, 1))
                eng.tensor_tensor(x_res[:], blocks(2), x_res[:], ALU.add).then_inc(x3_ready.sem, x3_ready.up(at))
                eng.wait_ge(x3_ready.sem, x3_ready.count(at, 1))

            eng.memset(eps[:], EPS)
            eng.memset(one[:], 1.0)
            eng.memset(dtlow[:], 1.0)
            eng.wait_ge(loaded, 16 * n_loads)
            eng.tensor_scalar(gamma_s[:], w["gamma"][:], STEP, None, ALU.mult)
            eng.tensor_scalar(beta_s[:], w["beta"][:], STEP, None, ALU.mult)
            eng.wait_ge(prep_a, 1)
            eng.tensor_scalar(decay[:], decay[:], -1.0, None, ALU.mult)
            ins = eng.tensor_scalar(mix_y[:], w["w_mix"][:], -1.0, None, ALU.mult)
            ins.then_inc(prepared_v, 1)
            eng.wait_ge(prepared_v, 1)
            for h in range(DB):
                ins = eng.tensor_tensor(mix_y[:, h, h * P:(h + 1) * P], mix_y[:, h, h * P:(h + 1) * P],
                                        ident[:], ALU.add)
            ins.then_inc(prepared_v, 1)
            eng.wait_ge(prepared_v, 2)
            for h in range(DB):
                ins = eng.tensor_tensor(mix_yd[:, h, :], mix_y[:, h, :], w["skip"][:], ALU.mult)
            ins.then_inc(prepared, 1)
            eng.wait_ge(prepared, 1)
            with eng.Fori(0, B) as b:
                at = Place(b, 0)
                attention(at)
                eng.wait_ge(x1_ready.sem, x1_ready.count(at, 1))
                mixture(at, x_res, None)
                ssm_inputs(at)
                fill(at, 0, 0, tuple(range(NS)))
                scan_unit(at, 0, 0, None, 1)
                hold(eng)
                with eng.Fori(0, ITERS) as i:
                    turn = Place(b, 1, i)
                    scan_unit(turn, 1, 0, 0, 0)
                    scan_unit(turn, 0, 1, 1, 1)
                at = Place(b, 2)
                scan_unit(at, 1, 0, 0, None)
                back_var(at, 1, 1)
                back_norm(at, 1, 1)
                ssm_output(at)
                mixture(at, x_out, out_ready)

        @block.gpsimd
        def _(eng):
            def attention(at):
                eng.wait_ge(kt_copied.sem, kt_copied.count(at, 1))
                for h in range(NH):
                    eng.tensor_tensor(
                        kmask[:, h, :], KT, w["headmask"][:, h:h + 1].broadcast_to([P, T]), ALU.mult).then_inc(kmasked.sem, kmasked.up(at))

            def scan_unit(at, hf, ks, ready, carried):
                sums = NG // 4 * ks + (LAG if carried else 0)
                for p in range(NG // 2):
                    eng.wait_ge(scanned.sem, scanned.count(at, NG * ks + 2 * p + 2))
                    if p == 0:
                        eng.wait_ge(c_copied.sem, c_copied.count(at, ready))
                    if p % 2 == 0 and (p >= NPROD // 2 or carried):
                        eng.wait_ge(nsummed.sem, nsummed.count(at, sums + p // 2 - 1))
                    s = 2 * p % NHID
                    eng.tensor_tensor(
                        prod[:, s:s + 2, :], hst[:, s:s + 2, :],
                        crep[:, hf:hf + 1, :].broadcast_to([P, 2, TH]), ALU.mult).then_inc(prod_done.sem, prod_done.up(at))

            eng.wait_ge(loaded, 16 * n_loads)
            with eng.Fori(0, B) as b:
                at = Place(b, 0)
                attention(at)
                scan_unit(at, 0, 0, 1, False)
                with eng.Fori(0, ITERS) as i:
                    turn = Place(b, 1, i)
                    scan_unit(turn, 1, 0, 0, True)
                    scan_unit(turn, 0, 1, 1, True)
                scan_unit(Place(b, 2), 1, 0, 0, True)

        for name, s in sems:
            assert tuple(s.seen) == tuple(s.n), (name, s.seen, s.n)


def _rows(a):
    return np.ascontiguousarray(a.reshape(-1, P, a.shape[-1]).transpose(1, 0, 2))


def kernel(**inputs):
    import concourse.bacc as bacc
    from concourse.bass_utils import run_bass_kernel_spmd

    a = {k: np.asarray(v) for k, v in inputs.items()}
    b, f = (lambda n: a["L0_attn_b_" + n]), (lambda n: a["L0_ffn_" + n])
    wide = lambda v: np.ascontiguousarray(np.broadcast_to(v, (P, v.shape[0])))

    freqs = np.float32(10000.0) ** (np.arange(0, HD, 2, dtype=np.float32) / np.float32(HD))
    angles = np.arange(T, dtype=np.float32)[:, None] * freqs[None, :].astype(np.float32)
    cosine = np.cos(angles.astype(np.float64)).astype(np.float32)
    sine = np.sin(angles.astype(np.float64)).astype(np.float32)
    lanes = np.arange(P)
    sel = np.zeros((P, NR, 32), np.float32)
    for r in range(NR):
        sel[lanes, r, GC * r + lanes % GC] = 1.0

    arrays = {
        "x": a["L0_attn_a_x"],
        "ident": np.eye(P, dtype=np.float32), "sel": sel,
        "cosine": _rows(cosine), "sine": _rows(sine),
        "headmask": (lanes[:, None] // HD == np.arange(NH)[None, :]).astype(np.float32),
        "experts": wide(np.arange(NE, dtype=np.float32)),
        "qkv_w": a["L0_attn_a_qkv_w"], "qkv_b": wide(a["L0_attn_a_qkv_b"]),
        "out_w": a["L0_attn_a_out_w"], "out_b": wide(a["L0_attn_a_out_b"]),
        "w_in": b("W_in").T, "w_x": _rows(b("W_x").T),
        "a_log": b("A_log").reshape(NG, GC, NS).transpose(2, 1, 0).reshape(P, NG),
        "w_bc": _rows(b("W_bc").T), "w_zy": _rows(b("W_zy").T), "w_mix": _rows(b("W_mix").T),
        "skip": wide(b("D")), "gamma": b("ln_gamma").reshape(DB, P).T,
        "beta": b("ln_beta").reshape(DB, P).T, "w_out": _rows(b("W_out").T),
        "router": f("router_w").T,
        "gate_w": f("gate_w").transpose(1, 0, 2), "up_w": f("up_w").transpose(1, 0, 2),
        "gate_b": f("gate_b").reshape(NE, FB, P).transpose(2, 0, 1),
        "up_b": f("up_b").reshape(NE, FB, P).transpose(2, 0, 1),
        "down_w": f("down_w").reshape(NE, FB, P, DM).transpose(2, 0, 1, 3),
        "w_dt": b("W_dt").T, "b_dt": b("b_dt").reshape(1, DI), "down_b": f("down_b"),
    }
    nc = bacc.Bacc("TRN2", target_bir_lowering=False, num_devices=1)
    in_map, tensors = {}, {}
    for name, v in arrays.items():
        v = np.ascontiguousarray(v)
        in_map["in_" + name] = v
        tensors[name] = nc.dram_tensor("in_" + name, v.shape, F32, kind="ExternalInput").ap()
    out = nc.dram_tensor("out", (B, T, DM), F32, kind="ExternalOutput").ap()
    hybrid_kernel(nc, tensors, out)
    r = run_bass_kernel_spmd(nc, [in_map], core_ids=[0])
    return r.results[0]["out"]
```

```python
from contextlib import ExitStack

import numpy as np
import concourse.bass as bass
from concourse import mybir

P = 128
F32 = mybir.dt.float32
BF16 = mybir.dt.bfloat16
U32 = mybir.dt.uint32
ALU = mybir.AluOpType
ACT = mybir.ActivationFunctionType
AX = mybir.AxisListType.X

B, T, DM = 16, 512, 128
TB = T // P
NH, HD = 16, 8
HG = 4
SCALE = HD ** -0.5
PARTS = 3
SLOTS = PARTS * PARTS
QR = SLOTS * HD
BIAS = 96
K_SLOTS = ((5, 7), (1, 8), (2, 4))
QUAD = 4
NE, DF = 8, 256
FB = DF // P
DI, NS, DR = 256, 16, 8
DB = DI // P
GC = 8
NG = DI // GC
NR = 32 // GC
ITERS, STEP, EPS = 8, 0.99, 1e-5
TH = T // 2
HB = TH // P
RING = (0, 1, 2, 4)
NHID, NPROD = 8, 8
PE_X, PE_Z, PE_V, PE_Y, PE_C, PE_D = 3, 3, 7, 9, 11, 15
DVE_VAR, DVE_NORM, DVE_Y, DVE_BC, DVE_BCN, DVE_DU, DVE_FILL = 7, 9, 12, 16, 18, 19, 22
EXPAND = 4
FIRST_C = 15
AHEAD = 2
MAX_AT = 3
LAG = 2
ORDER = [16 * h + NR * q + r for h in range(DB) for r in range(NR) for q in range(4)]


class Place:

    def __init__(self, seq, section, turn=0):
        self.seq, self.section, self.turn = seq, section, turn


class Signal:

    def __init__(self, sem, before, turn, behind, unit=1):
        self.sem, self.n, self.unit = sem, (before, turn, behind), unit
        self.seen = [0, 0, 0]
        self.total = before + ITERS * turn + behind

    def up(self, at):
        self.seen[at.section] += 1
        return self.unit

    def count(self, at, k):
        before, turn, _ = self.n
        skipped = (0, before, before + ITERS * turn)[at.section]
        value = at.seq * (self.total * self.unit) + (skipped + k) * self.unit
        return value + at.turn * (turn * self.unit) if at.section == 1 else value

    def last(self, at):
        return self.count(at, self.seen[at.section])


def hybrid_kernel(nc, t, out):
    with ExitStack() as ctx:
        sems = []

        def sb(name, shape, dt=F32):
            return ctx.enter_context(nc.sbuf_tensor(name, shape, dt))

        def signal(name, before=0, turn=0, behind=0, unit=1):
            s = Signal(ctx.enter_context(nc.semaphore(name)), before, turn, behind, unit)
            sems.append((name, s))
            return s

        ps = ctx.enter_context(nc.psum_tensor("ps", [P, 8, 512], F32))

        WEIGHTS = {
            "ident": [P, P], "sel": [P, NR, 32], "cosine": [P, TB, 4], "sine": [P, TB, 4],
            "experts": [P, NE],
            "qkv_w": [P, 3 * DM], "qkv_b": [P, 3 * DM], "out_w": [P, DM], "out_b": [P, DM],
            "w_in": [P, 2 * DI], "w_x": [P, DB, DR + 2 * NS], "a_log": [P, NG],
            "w_bc": [P, DB, 2 * NS], "w_zy": [P, DB, DI], "w_mix": [P, DB, DI],
            "skip": [P, DI], "gamma": [P, DB], "beta": [P, DB], "w_out": [P, DB, DM],
            "router": [P, NE], "gate_b": [P, NE, FB],
            "up_b": [P, NE, FB],
        }
        w = {name: sb("w_" + name, shape) for name, shape in WEIGHTS.items()}
        w_dt = sb("w_dt", [DR + 1, DI])
        down_b = sb("down_b", [NE, DM])
        ident = w["ident"]
        ident_b = sb("ident_b", [P, P], BF16)

        eps = sb("eps", [P, 1])
        one = sb("one", [P, 1])
        held = sb("held", [P, 32])
        gamma_s = sb("gamma_s", [P, DB])
        beta_s = sb("beta_s", [P, DB])
        decay = sb("decay", [P, NG])
        mix_y = sb("mix_y", [P, DB, DI])
        hend = sb("hend", [P, NG])
        mix_yd = sb("mix_yd", [P, DB, DI])

        x_in = sb("x_in", [P, TB, DM])
        x_res = sb("x_res", [P, TB, DM])
        x_out = sb("x_out", [P, TB, DM])
        xnT = sb("xnT", [P, T])
        stats = sb("stats", [P, TB, 6])
        meanvar = sb("meanvar", [P, TB, 2])
        std = sb("std", [P, TB])
        rstd = sb("rstd", [P, TB])
        nmr = sb("nmr", [P, TB])
        da = sb("da", [P, NG, T])
        region = da[:].rearrange("p g t -> p (g t)")
        used = [0]

        def piece(n):
            at, used[0] = used[0], used[0] + n
            assert used[0] <= NG * T
            return region[:, at:at + n]

        work = sb("work", [P, (NHID + NPROD) * TH])
        scan_in = sb("scan_in", [P, 2, HB, NG, NS, GC])
        third = scan_in[:].rearrange("p f b g n c -> p (f b g n c)")
        gate_w = third[:, 0:2048].rearrange("p (e f) -> p e f", e=NE)
        up_w = third[:, 2048:4096].rearrange("p (e f) -> p e f", e=NE)
        down_w = third[:, 4096:6144].rearrange("p (e f c) -> p e f c", e=NE, f=FB)
        scr = third[:, 6144:10240]

        def ring(at, n):
            return work[:, at * T:(at + n) * T].rearrange("p (k t) -> p k t", t=T)

        slots = piece(2 * TB * NH * QR // 2).bitcast(BF16).rearrange(
            "p (k b h s c) -> p k b h s c", k=2, b=TB, h=NH, s=SLOTS)
        heads_flat = piece(QUAD * 2 * T // 2)
        heads = heads_flat.bitcast(BF16).rearrange("p (h k t) -> p h k t", h=QUAD, k=2)
        probsT = piece(HG * TB * T).rearrange("p (j k t) -> p j k t", j=HG, k=TB)
        vaug_flat = third[:, 10240:12288]
        vaug = vaug_flat.rearrange("p (b h r) -> p b h r", b=TB, h=NH)
        qkv = scr[:, 0:TB * 384].rearrange("p (b c) -> p b c", b=TB)
        rot = scr[:, 1536:2560].rearrange("p (b c) -> p b c", b=TB)
        rtmp = scr[:, 2560:3584].rearrange("p (k b c) -> p k b c", k=2, b=TB)
        left = ring(0, 2).rearrange("p k t -> p (k t)")
        smax = sb("smax", [P, 2, TB])
        smax_b = sb("smax_b", [P, 2, TB, 2], BF16)
        oT = work[:, 5 * T:6 * T]
        rsum = sb("rsum", [P, TB, HG])
        attn = work[:, 6 * T:7 * T].rearrange("p (b c) -> p b c", b=TB)
        attnT = work[:, 7 * T:8 * T]

        rt = sb("rt", [P, 8, TB, NE])
        top = sb("top", [P, TB, 8])
        topi = sb("topi", [P, TB, 8], U32)
        topf = sb("topf", [P, TB, 8])
        rs = sb("rs", [P, 4, TB])
        cT = sb("cT", [NE, T])
        xn = work[:, 7 * T:8 * T].rearrange("p (b c) -> p b c", b=TB)
        gs = ring(0, 2)
        hid = ring(2, 4).rearrange("p (e f) t -> p e f t", f=FB)
        acc = work[:, 6 * T:7 * T].rearrange("p (b c) -> p b c", b=TB)

        xT = ring(0, DB)
        yT = sb("yT", [P, DB, T + 1])
        x_mixed = sb("x_mixed", [P, TB, DI])
        x_skip = sb("x_skip", [P, TB, DI])
        x_bc = sb("x_bc", [P, TB, 2 * NS])
        dtlow = sb("dtlow", [DR + 1, T])
        delta = sb("delta", [P, TB, DI])
        sp = [scr[:, 1024 * k:1024 * (k + 1)] for k in range(4)]
        bcs = sb("bcs", [P, HB, 2, NS])
        bcq = sb("bcq", [P, HB, 2, NS])
        b_norm = sb("b_norm", [P, HB, NS])
        c_norm = sb("c_norm", [P, HB, NS, GC])
        ss = sb("ss", [P, HB * 2])
        nrm = sb("nrm", [P, HB * 2])
        rn = sb("rn", [P, HB * 2])
        du = sb("du", [P, HB, DI])
        crep = sb("crep", [P, 2, TH])
        hst = work[:, 0:NHID * TH].rearrange("p (k t) -> p k t", t=TH)
        prod = work[:, NHID * TH:].rearrange("p (k t) -> p k t", t=TH)
        yscT = sb("yscT", [P, DB, TH])
        vn = sb("vn", [P, HB, DI])
        ytmp = sb("ytmp", [P, DB, TH])
        gz = ring(0, 2)
        gy = ring(2, 2)

        loaded = ctx.enter_context(nc.semaphore("loaded"))
        prepared = ctx.enter_context(nc.semaphore("prepared"))
        prep_a = ctx.enter_context(nc.semaphore("prep_a"))
        prepared_v = ctx.enter_context(nc.semaphore("prepared_v"))
        x_loaded = signal("x_loaded", 1, unit=16)
        x_free = signal("x_free", 1)
        experts_loaded = signal("experts_loaded", behind=3, unit=16)
        out_ready = signal("out_ready", behind=1)
        stored = signal("stored", behind=1, unit=16)
        vchain = signal("vchain", 63, 16, 20)

        class Norm:

            def __init__(self, name, *n):
                self.var = signal(name + "_var", *n)
                self.std = signal(name + "_std", *n)
                self.xn = signal(name + "_xn", *n)
                self.turned = signal(name + "_turned", *n)
                self.xnT = signal(name + "_xnT", *n)

        n_att, n_moe, n_ssm = Norm("na", 1), Norm("nm", 1, 0, 1), Norm("ns", 1)
        qkv_done = signal("qkv_done", 1)
        rot_done = signal("rot_done", 1)
        heads_zero = signal("heads_zero", 1)
        part_done = signal("part_done", PARTS)
        repeated_a = signal("repeated_a", PARTS)
        repeated_v = signal("repeated_v", 1)
        qk_turned = signal("qk_turned", NH)
        qk_copied = signal("qk_copied", NH)
        v_zero = signal("v_zero", 1)
        v_ready = signal("v_ready", 1)
        scored = signal("scored", NH * TB)
        maxed = signal("maxed", NH * TB)
        max_parts = signal("max_parts", NH)
        max_turned = signal("max_turned", NH)
        max_copied = signal("max_copied", NH)
        rescored = signal("rescored", NH * TB)
        exped = signal("exped", NH * TB)
        weighed = signal("weighed", NH)
        o_copied = signal("o_copied", NH // HG)
        o_turned = signal("o_turned", NH // HG)
        o_normed = signal("o_normed", NH // HG)
        a_turned = signal("a_turned", 1)
        a_copied = signal("a_copied", 1)
        projected = signal("projected", 1)
        x1_ready = signal("x1_ready", 1)

        routed = signal("routed", 1, 0, 1)
        r_shift = signal("r_shift", 1, 0, 1)
        r_exp = signal("r_exp", 1, 0, 1)
        r_comb = signal("r_comb", 1, 0, 1)
        c_turned = signal("c_turned", 1, 0, 1)
        comb_copied = signal("comb_copied", 1, 0, 1)
        biased = signal("biased", 1, 0, 1)
        nf = NE * FB
        gated = signal("gated", nf, 0, nf)
        upped = signal("upped", nf, 0, nf)
        silued = signal("silued", nf, 0, nf)
        hidden = signal("hidden", nf, 0, nf)
        downed = signal("downed", NE, 0, NE)
        summed = signal("summed", NE, 0, NE)

        xT_done = signal("xT_done", 1)
        xT_copied = signal("xT_copied", 1)
        dt_done = signal("dt_done", 1)
        dt_copied = signal("dt_copied", 1)
        dl_done = signal("dl_done", 1)
        xmix_done = signal("xmix_done", 1)
        x_mixed_a = signal("x_mixed_a", 1)
        dl_abs = signal("dl_abs", 1)
        dl_relu = signal("dl_relu", 1)
        dl_exp = signal("dl_exp", 1)
        dl_ln = signal("dl_ln", 1)
        dl_ready = signal("dl_ready", 1)
        expanded = signal("expanded", EXPAND)
        dl_rep = signal("dl_rep", NG)
        da_ready = signal("da_ready", NG)

        y_ready = signal("y_ready", 1, 2, 2)
        front = (2, 2, 0)
        bc_done = signal("bc_done", *front)
        ss_done = signal("ss_done", *front)
        nrm_done = signal("nrm_done", *front)
        c_ready = signal("c_ready", *front)
        b_ready = signal("b_ready", *front)
        u_done = signal("u_done", *front)
        du_done = signal("du_done", *front)
        c_rep = signal("c_rep", *front)
        c_copied = signal("c_copied", *front)
        filled_a = signal("filled_a", *front)
        filled_v = signal("filled_v", *front)
        scan = (1, 2, 1)
        in_turned = signal("in_turned", *(NG // 2 * n for n in scan))
        scanned = signal("scanned", *(NG * n for n in scan))
        prod_done = signal("prod_done", *(NG // 2 * n for n in scan))
        nsummed = signal("nsummed", NG // 4 - LAG, 2 * NG // 4, NG // 4 + LAG)
        back = (0, 2, 2)
        ysc_copied = signal("ysc_copied", *back)
        z_done = signal("z_done", *back)
        zvar = signal("zvar", *back)
        zstd = signal("zstd", *back)
        znmr = signal("znmr", *back)
        v_done = signal("v_done", *back)
        vt_done = signal("vt_done", *back)
        ytmp_done = signal("ytmp_done", 0, 2, 0)
        z2_done = signal("z2_done", behind=1)
        z2_silu = signal("z2_silu", behind=1)
        gy_done = signal("gy_done", behind=1)
        o2_done = signal("o2_done", behind=1)
        x3_ready = signal("x3_ready", behind=1)

        bank = lambda n: ps[:, n, :]
        blocks = lambda n: ps[:, n, :].rearrange("p (b c) -> p b c", b=TB)
        wide = ps[:, 5:7, :].rearrange("p k c -> p (k c)").rearrange("p (b c) -> p b c", b=TB)
        du_groups = lambda tb: du[:, tb, :].rearrange("p (g c) -> p g c", c=GC)
        ge = NG // EXPAND
        chunk = lambda e: scan_in[:, :, :, ge * e:ge * (e + 1)].rearrange(
            "p f b g n c -> p (f b) g n c")
        repeated = lambda e: delta[:, :, ge * GC * e:ge * GC * (e + 1)].rearrange(
            "p b (g o c) -> p b g o c", o=1, c=GC).broadcast_to([P, TB, ge, NS, GC])
        turned = ps[0:QR, 5, :].bitcast(BF16).rearrange("p (k t) -> p k t", k=2)
        qk_slots = slots.rearrange("p k b h s c -> p k (b h) s c")
        half5 = ps[:, 5, :].rearrange("p (b c) -> p b c", b=HB)
        half6 = ps[:, 6, :].rearrange("p (b c) -> p b c", b=HB)
        n_loads = len(WEIGHTS) + 2

        block = ctx.enter_context(nc.Block())

        @block.sync
        def _(eng):
            x_t = t["x"].rearrange("b (k p) c -> b p k c", p=P)
            out_t = out.rearrange("b (k p) c -> b p k c", p=P)
            eng.dma_start(x_in[:], x_t[0]).then_inc(x_loaded.sem, 16)
            for name in WEIGHTS:
                eng.dma_start(w[name][:], t[name]).then_inc(loaded, 16)
            eng.dma_start(w_dt[0:DR, :], t["w_dt"]).then_inc(loaded, 16)
            eng.dma_start(w_dt[DR:DR + 1, :], t["b_dt"]).then_inc(loaded, 16)
            eng.dma_start(down_b[:], t["down_b"]).then_inc(stored.sem, 16)
            def load_experts():
                for dst, name in ((gate_w, "gate_w"), (up_w, "up_w"), (down_w, "down_w")):
                    eng.dma_start(dst, t[name]).then_inc(experts_loaded.sem, 16)

            load_experts()
            with eng.Fori(0, B - 1) as b:
                eng.wait_ge(x_free.sem, b + 1)
                eng.dma_start(x_in[:], x_t[b + 1]).then_inc(x_loaded.sem, 16)
                eng.wait_ge(z2_done.sem, b + 1)
                load_experts()
                eng.wait_ge(out_ready.sem, b + 1)
                eng.dma_start(out_t[b], x_out[:]).then_inc(stored.sem, 16)
            eng.wait_ge(z2_done.sem, B)
            load_experts()
            eng.wait_ge(out_ready.sem, B)
            eng.dma_start(out_t[B - 1], x_out[:]).then_inc(stored.sem, 16)
            eng.wait_ge(stored.sem, 16 * (B + 1))
            eng.wait_ge(experts_loaded.sem, 16 * 3 * (B + 1))
            x_loaded.seen[0] = x_free.n[0]
            stored.seen[2] = 1
            experts_loaded.seen[2] = 3

        @block.tensor
        def _(eng):
            def turn_norm(at, n, dst):
                eng.wait_ge(n.xn.sem, n.xn.count(at, 1))
                for tb in range(TB):
                    mm = eng.transpose(dst[:, tb, :], xn[:, tb, :], ident[:])
                mm.then_inc(n.turned.sem, n.turned.up(at))

            def attention(at):
                turn_norm(at, n_att, blocks(4))
                eng.wait_ge(n_att.xnT.sem, n_att.xnT.count(at, 1))
                for tb in range(TB):
                    mm = eng.matmul(ps[:, tb, 0:3 * DM], xnT[:, tb * P:(tb + 1) * P], w["qkv_w"][:],
                                    start=True, stop=True)
                mm.then_inc(qkv_done.sem, qkv_done.up(at))

                def turn_head(h):
                    if h == 0:
                        eng.wait_ge(repeated_a.sem, repeated_a.count(at, PARTS))
                        eng.wait_ge(repeated_v.sem, repeated_v.count(at, 1))
                    else:
                        eng.wait_ge(qk_copied.sem, qk_copied.count(at, h))
                    for k in range(2):
                        for tb in range(TB):
                            mm = eng.transpose(
                                turned[:, k, tb * P:(tb + 1) * P],
                                slots[:, k, tb, h].rearrange("p s c -> p (s c)"), ident_b[:])
                    mm.then_inc(qk_turned.sem, qk_turned.up(at))

                def score(h, qb):
                    u = TB * h + qb
                    if qb == 0:
                        eng.wait_ge(qk_copied.sem, qk_copied.count(at, h + 1))
                    if u >= 3:
                        eng.wait_ge(maxed.sem, maxed.count(at, u - 2))
                    q, k = heads[0:BIAS, h % QUAD, 0], heads[0:BIAS, h % QUAD, 1]
                    mm = eng.matmul(bank(u % 3), q[:, qb * P:(qb + 1) * P], k,
                                    start=True, stop=True)
                    mm.then_inc(scored.sem, scored.up(at))

                def turn_max(h):
                    eng.wait_ge(max_parts.sem, max_parts.count(at, h + 1))
                    if h > 0:
                        eng.wait_ge(max_copied.sem, max_copied.count(at, h))
                    for tb in range(TB):
                        mm = eng.matmul(ps[BIAS:BIAS + 2, 6, tb * P:(tb + 1) * P],
                                        smax_b[:, h % 2, tb, :], ident_b[:],
                                        start=(tb == 0), stop=(tb == TB - 1))
                    mm.then_inc(max_turned.sem, max_turned.up(at))

                def rescore(h, kb):
                    u = TB * h + kb
                    if kb == 0:
                        eng.wait_ge(max_copied.sem, max_copied.count(at, h + 1))
                    if u >= 2:
                        eng.wait_ge(exped.sem, exped.count(at, u - 1))
                    q, k = heads[0:BIAS + 2, h % QUAD, 0], heads[0:BIAS + 2, h % QUAD, 1]
                    mm = eng.matmul(bank(3 + u % 2), k[:, kb * P:(kb + 1) * P], q,
                                    start=True, stop=True)
                    mm.then_inc(rescored.sem, rescored.up(at))

                def weigh(c, kb):
                    eng.wait_ge(exped.sem, exped.count(at, TB * (HG * c + HG - 1) + kb + 1))
                    if c == 0 and kb == 0:
                        eng.wait_ge(v_ready.sem, v_ready.count(at, 1))
                    if c > 0 and kb == 0:
                        eng.wait_ge(o_normed.sem, o_normed.count(at, c))
                    for j in range(HG):
                        mm = eng.matmul(ps[32 * j:32 * j + 32, 7, :],
                                        vaug[:, kb, HG * c + j, :], probsT[:, j, kb, :],
                                        start=(kb == 0), stop=(kb == TB - 1))
                    mm.then_inc(weighed.sem, weighed.up(at))

                def turn_out(c):
                    eng.wait_ge(o_copied.sem, o_copied.count(at, c + 1))
                    for tb in range(TB):
                        mm = eng.transpose(blocks(7)[:, tb, :], oT[:, tb * P:(tb + 1) * P], ident[:])
                    mm.then_inc(o_turned.sem, o_turned.up(at))

                turn_head(0)
                turn_head(1)
                for h in range(NH + AHEAD + 2):
                    behind = h - AHEAD
                    for b in range(TB):
                        if h < NH:
                            score(h, b)
                        if b == MAX_AT - 1 and 1 <= h <= NH:
                            turn_max(h - 1)
                        if behind >= HG and behind % HG == 0:
                            weigh(behind // HG - 1, b)
                        if 0 <= behind < NH:
                            rescore(behind, b)
                    if h + 2 < NH:
                        turn_head(h + 2)
                    if behind > HG and behind % HG == 1:
                        turn_out(behind // HG - 1)
                eng.wait_ge(o_normed.sem, o_normed.count(at, NH // HG))
                for tb in range(TB):
                    mm = eng.transpose(blocks(7)[:, tb, :], attn[:, tb, :], ident[:])
                mm.then_inc(a_turned.sem, a_turned.up(at))
                eng.wait_ge(a_copied.sem, a_copied.count(at, 1))
                for tb in range(TB):
                    mm = eng.matmul(blocks(6)[:, tb, :], attnT[:, tb * P:(tb + 1) * P],
                                    w["out_w"][:], start=(tb == 0), stop=(tb == TB - 1))
                mm.then_inc(projected.sem, projected.up(at))

            def mixture(at):
                turn_norm(at, n_moe, blocks(4))
                eng.wait_ge(experts_loaded.sem, experts_loaded.count(at, 3 if at.section == 0 else 6))
                eng.wait_ge(n_moe.xnT.sem, n_moe.xnT.count(at, 1))
                for tb in range(TB):
                    mm = eng.matmul(ps[:, 5, tb * NE:(tb + 1) * NE], xnT[:, tb * P:(tb + 1) * P],
                                    w["router"][:], start=(tb == 0), stop=(tb == TB - 1))
                mm.then_inc(routed.sem, routed.up(at))

                def into(u):
                    e, f = divmod(u, FB)
                    if u >= 2:
                        eng.wait_ge(silued.sem, silued.count(at, u - 1))
                    mm = eng.matmul(bank(u % 2), gate_w[:, e, f * P:(f + 1) * P], xnT[:],
                                    start=True, stop=True)
                    mm.then_inc(gated.sem, gated.up(at))
                    if u >= 2:
                        eng.wait_ge(hidden.sem, hidden.count(at, u - 1))
                    mm = eng.matmul(bank(2 + u % 2), up_w[:, e, f * P:(f + 1) * P], xnT[:],
                                    start=True, stop=True)
                    mm.then_inc(upped.sem, upped.up(at))

                def down(e):
                    eng.wait_ge(hidden.sem, hidden.count(at, FB * (e + 1)))
                    if e >= 2:
                        eng.wait_ge(summed.sem, summed.count(at, e - 1))
                    for tb in range(TB):
                        for f in range(FB):
                            mm = eng.matmul(blocks(6 + e % 2)[:, tb, :],
                                            hid[:, e % 2, f, tb * P:(tb + 1) * P],
                                            down_w[:, e, f, :], start=(tb == 0 and f == 0),
                                            stop=(tb == TB - 1 and f == FB - 1))
                    mm.then_inc(downed.sem, downed.up(at))

                for u in range(4):
                    into(u)
                eng.wait_ge(r_comb.sem, r_comb.count(at, 1))
                for tb in range(TB):
                    mm = eng.transpose(ps[0:NE, 5, tb * P:(tb + 1) * P], rt[:, 7, tb, :], ident[:])
                mm.then_inc(c_turned.sem, c_turned.up(at))
                eng.wait_ge(comb_copied.sem, comb_copied.count(at, 1))
                for tb in range(TB):
                    mm = eng.matmul(blocks(4)[:, tb, :], cT[:, tb * P:(tb + 1) * P], down_b[:],
                                    start=(tb == 0), stop=(tb == TB - 1))
                mm.then_inc(biased.sem, biased.up(at))
                for e in range(NE):
                    if e < NE - 2:
                        down(e)
                        into(2 * e + 4)
                        into(2 * e + 5)
                    else:
                        down(e)

            def ssm_inputs(at):
                turn_norm(at, n_ssm, blocks(4))
                eng.wait_ge(n_ssm.xnT.sem, n_ssm.xnT.count(at, 1))
                for h in range(DB):
                    mm = eng.matmul(bank(5 + h), w["w_in"][:, h * P:(h + 1) * P], xnT[:],
                                    start=True, stop=True)
                mm.then_inc(xT_done.sem, xT_done.up(at))
                eng.wait_ge(xT_copied.sem, xT_copied.count(at, 1))
                for h in range(DB):
                    mm = eng.matmul(ps[0:DR, 4, :], w["w_x"][:, h, 0:DR], xT[:, h, :],
                                    start=(h == 0), stop=(h == DB - 1))
                mm.then_inc(dt_done.sem, dt_done.up(at))
                eng.wait_ge(dt_copied.sem, dt_copied.count(at, 1))
                for tb in range(TB):
                    mm = eng.matmul(wide[:, tb, :], dtlow[:, tb * P:(tb + 1) * P], w_dt[:],
                                    start=(tb % 2 == 0), stop=(tb % 2 == 1))
                mm.then_inc(dl_done.sem, dl_done.up(at))
                for tb in range(TB):
                    for h in range(DB):
                        eng.matmul(ps[:, 7, tb * 32:(tb + 1) * 32], xT[:, h, tb * P:(tb + 1) * P],
                                   w["w_x"][:, h, DR:DR + 2 * NS], start=(tb == 0 and h == 0),
                                   stop=(tb == TB - 1 and h == DB - 1))
                for tb in range(TB):
                    for h in range(DB):
                        mm = eng.matmul(ps[:, tb // HB, (tb % HB) * DI:(tb % HB + 1) * DI],
                                        xT[:, h, tb * P:(tb + 1) * P], w["w_mix"][:, h, :],
                                        start=(tb % HB == 0 and h == 0),
                                        stop=(tb % HB == HB - 1 and h == DB - 1))
                mm.then_inc(xmix_done.sem, xmix_done.up(at))
                eng.wait_ge(x_mixed_a.sem, x_mixed_a.count(at, 1))
                eng.wait_ge(dl_relu.sem, dl_relu.count(at, 1))
                front_x(at, 0, 0)
                front_y(at, 0, 0)
                for g in range(NG):
                    if g % (NG // EXPAND) == 0:
                        eng.wait_ge(expanded.sem, expanded.count(at, g * EXPAND // NG + 1))
                    if g >= 4:
                        eng.wait_ge(da_ready.sem, da_ready.count(at, g - 3))
                    for tb in range(TB):
                        mm = eng.transpose(blocks(RING[g % 4])[:, tb, :], group(tb // HB, tb % HB, g),
                                           ident[:])
                    mm.then_inc(dl_rep.sem, dl_rep.up(at))
                    if g == FIRST_C:
                        front_c(at, 0, 0)
                eng.wait_ge(da_ready.sem, da_ready.count(at, NG))

            def group(hf, tb, g):
                return scan_in[:, hf, tb, g].rearrange("p n c -> p (n c)")

            def tokens(hf, tb, shift=1):
                at = (hf * HB + tb) * P + shift
                return slice(at, at + P)

            def front_x(at, hf, kf):
                for tb in range(HB):
                    eng.matmul(ps[:, 7, tb * 32:(tb + 1) * 32], ident[:], x_bc[:, hf * HB + tb, :],
                               start=(tb == 0), stop=False)
                for tb in range(HB):
                    eng.matmul(half6[:, tb, :], ident[:], x_mixed[:, hf * HB + tb, :],
                               start=(tb == 0), stop=False)

            def front_y(at, hf, kf):
                eng.wait_ge(y_ready.sem, y_ready.count(at, kf + 1 if at.section else 1))
                for tb in range(HB):
                    for h in range(DB):
                        mm = eng.matmul(ps[:, 7, tb * 32:(tb + 1) * 32], yT[:, h, tokens(hf, tb, 0)],
                                        w["w_bc"][:, h, :], start=False,
                                        stop=(tb == HB - 1 and h == DB - 1))
                mm.then_inc(bc_done.sem, bc_done.up(at))
                for tb in range(HB):
                    for h in range(DB):
                        mm = eng.matmul(half6[:, tb, :], yT[:, h, tokens(hf, tb)], mix_y[:, h, :],
                                        start=False, stop=(tb == HB - 1 and h == DB - 1))
                mm.then_inc(u_done.sem, u_done.up(at))

            def front_c(at, hf, kf):
                eng.wait_ge(c_ready.sem, c_ready.count(at, kf + 1))
                for tb in range(HB):
                    mm = eng.transpose(ps[:, 7, TH + tb * P:TH + (tb + 1) * P],
                                       c_norm[:, tb].rearrange("p n c -> p (n c)"), ident[:])
                mm.then_inc(c_rep.sem, c_rep.up(at))

            def back_d(at, hf):
                for tb in range(HB):
                    eng.matmul(half5[:, tb, :], ident[:], x_skip[:, hf * HB + tb, :],
                               start=(tb == 0), stop=False)
                    for h in range(DB):
                        eng.matmul(half5[:, tb, :], yT[:, h, tokens(hf, tb)], mix_yd[:, h, :],
                                   start=False, stop=False)

            def back_z(at, hf, kb):
                eng.wait_ge(ysc_copied.sem, ysc_copied.count(at, kb + 1))
                for tb in range(HB):
                    for h in range(DB):
                        mm = eng.matmul(half5[:, tb, h * P:(h + 1) * P],
                                        yscT[:, h, tb * P:(tb + 1) * P], ident[:], start=False,
                                        stop=(tb == HB - 1 and h == DB - 1))
                mm.then_inc(z_done.sem, z_done.up(at))

            def back_v(at, hf, kb):
                eng.wait_ge(v_done.sem, v_done.count(at, kb + 1))
                for h in range(DB):
                    for tb in range(HB):
                        mm = eng.transpose(ps[:, 5, h * TH + tb * P:h * TH + (tb + 1) * P],
                                           vn[:, tb, h * P:(h + 1) * P], ident[:])
                mm.then_inc(vt_done.sem, vt_done.up(at))

            def sum_states(at, ks, k):
                eng.wait_ge(prod_done.sem, prod_done.count(at, NG // 2 * ks + 2 * k + 2))
                for s in range(4 * k, 4 * k + 4):
                    g = ORDER[s]
                    q, r, h = (g // NR) % 4, g % NR, g // 16
                    mm = eng.matmul(ps[32 * q:32 * q + 32, 3, h * TH:(h + 1) * TH],
                                    w["sel"][:, r, :], prod[:, s % NPROD, :],
                                    start=(r == 0), stop=(r == NR - 1))
                mm.then_inc(nsummed.sem, nsummed.up(at))

            def scan_unit(at, hf, ks, filled, kb, kf):
                other = 1 - hf
                follows = kb is not None
                for p in range(NG // 2):
                    if p == 0:
                        eng.wait_ge(filled_a.sem, filled_a.count(at, filled))
                        eng.wait_ge(filled_v.sem, filled_v.count(at, filled))
                    if p >= 4 or follows:
                        eng.wait_ge(scanned.sem, scanned.count(at, NG * ks + 2 * (p - 4) + 2))
                    for s in (2 * p, 2 * p + 1):
                        for tb in range(HB):
                            c = (s % 2) * TH + tb * P
                            mm = eng.transpose(ps[:, RING[p % 4], c:c + P], group(hf, tb, ORDER[s]),
                                               ident[:])
                    mm.then_inc(in_turned.sem, in_turned.up(at))
                    if follows and p < LAG:
                        sum_states(at, ks - 1, NG // 4 - LAG + p)
                    if p == 5 and follows:
                        eng.wait_ge(ysc_copied.sem, ysc_copied.count(at, ks + 1))
                    if p >= 5 and p % 2 == 1:
                        sum_states(at, ks, (p - 5) // 2)
                    if p == PE_X and kf is not None:
                        front_x(at, other, kf)
                    if p == PE_Z and follows:
                        back_z(at, other, kb)
                    if p == PE_V and follows:
                        back_v(at, other, kb)
                    if p == (PE_Y if follows else 3) and kf is not None:
                        front_y(at, other, kf)
                    if p == (PE_C if follows else 6) and kf is not None:
                        front_c(at, other, kf)
                    if p == PE_D:
                        if kf is None:
                            eng.wait_ge(y_ready.sem, y_ready.count(at, 1))
                        back_d(at, hf)
                if kf is None:
                    for k in range(NG // 4 - LAG, NG // 4):
                        sum_states(at, ks, k)

            def ssm_output(at):
                eng.wait_ge(y_ready.sem, y_ready.count(at, 2))
                for e in range(DB):
                    eng.matmul(bank(e), w["w_in"][:, DI + e * P:DI + (e + 1) * P], xnT[:],
                               start=True, stop=False)
                    for h in range(DB):
                        mm = eng.matmul(bank(e), w["w_zy"][:, h, e * P:(e + 1) * P], yT[:, h, 0:T],
                                        start=False, stop=(h == DB - 1))
                mm.then_inc(z2_done.sem, z2_done.up(at))
                eng.wait_ge(gy_done.sem, gy_done.count(at, 1))
                for tb in range(TB):
                    for h in range(DB):
                        mm = eng.matmul(blocks(2)[:, tb, :], gy[:, h, tb * P:(tb + 1) * P],
                                        w["w_out"][:, h, :], start=(tb == 0 and h == 0),
                                        stop=(tb == TB - 1 and h == DB - 1))
                mm.then_inc(o2_done.sem, o2_done.up(at))

            eng.wait_ge(stored.sem, 16)
            eng.wait_ge(loaded, 16 * n_loads)
            eng.wait_ge(prepared, 1)
            with eng.Fori(0, B) as b:
                at = Place(b, 0)
                attention(at)
                mixture(at)
                ssm_inputs(at)
                scan_unit(at, 0, 0, 1, None, 1)
                with eng.Fori(0, ITERS) as i:
                    turn = Place(b, 1, i)
                    scan_unit(turn, 1, 0, 0, 0, 0)
                    scan_unit(turn, 0, 1, 1, 1, 1)
                at = Place(b, 2)
                scan_unit(at, 1, 0, 0, 0, None)
                back_z(at, 1, 1)
                back_v(at, 1, 1)
                ssm_output(at)
                mixture(at)

        @block.scalar
        def _(eng):
            def root(at, n):
                eng.wait_ge(n.var.sem, n.var.count(at, 1))
                eng.activation(std[:], meanvar[:, :, 1], ACT.Sqrt, bias=eps[:]).then_inc(n.std.sem, n.std.up(at))
                eng.wait_ge(n.turned.sem, n.turned.count(at, 1))
                eng.activation(xnT[:], bank(4), ACT.Copy).then_inc(n.xnT.sem, n.xnT.up(at))

            def attention(at):
                root(at, n_att)
                for part in range(PARTS):
                    eng.wait_ge(part_done.sem, part_done.count(at, part + 1))
                    s = PARTS * part
                    eng.activation(qk_slots[:, 0, :, s + 1:s + 3, :],
                                   qk_slots[:, 0, :, s:s + 1, :].broadcast_to([P, TB * NH, 2, HD]),
                                   ACT.Copy).then_inc(repeated_a.sem, repeated_a.up(at))

                def copy_head(h):
                    eng.wait_ge(qk_turned.sem, qk_turned.count(at, h + 1))
                    if h == 0:
                        eng.wait_ge(heads_zero.sem, heads_zero.count(at, 1))
                    if h >= QUAD:
                        eng.wait_ge(rescored.sem, rescored.count(at, TB * (h - QUAD + 1)))
                    eng.activation(heads[0:QR, h % QUAD], turned, ACT.Copy
                                   ).then_inc(qk_copied.sem, qk_copied.up(at))

                def exp(h, kb):
                    eng.wait_ge(rescored.sem, rescored.count(at, TB * h + kb + 1))
                    if h >= HG and h % HG == 0:
                        eng.wait_ge(weighed.sem, weighed.count(at, h - HG + kb + 1))
                    eng.activation(probsT[:, h % HG, kb, :], bank(3 + (TB * h + kb) % 2), ACT.Exp,
                                   scale=SCALE).then_inc(exped.sem, exped.up(at))

                def copy_out(c):
                    eng.wait_ge(weighed.sem, weighed.count(at, TB * (c + 1)))
                    eng.activation(oT, bank(7), ACT.Copy).then_inc(o_copied.sem, o_copied.up(at))

                copy_head(0)
                copy_head(1)
                for h in range(NH + AHEAD + 2):
                    behind = h - AHEAD
                    for b in range(TB):
                        if 0 <= behind < NH:
                            exp(behind, b)
                    if behind >= HG and behind % HG == 0:
                        copy_out(behind // HG - 1)
                    if h + 2 < NH:
                        copy_head(h + 2)
                eng.wait_ge(a_turned.sem, a_turned.count(at, 1))
                eng.activation(attnT, bank(7), ACT.Copy).then_inc(a_copied.sem, a_copied.up(at))

            def mixture(at):
                root(at, n_moe)
                eng.wait_ge(r_shift.sem, r_shift.count(at, 1))
                eng.activation(rt[:, 1], rt[:, 0], ACT.Exp).then_inc(r_exp.sem, r_exp.up(at))

                def silu(u):
                    e, f = divmod(u, FB)
                    eng.wait_ge(gated.sem, gated.count(at, u + 1))
                    if u >= 2:
                        eng.wait_ge(hidden.sem, hidden.count(at, u - 1))
                    eng.activation(gs[:, u % 2, :], bank(u % 2), ACT.Silu,
                                                 bias=w["gate_b"][:, e, f:f + 1]).then_inc(silued.sem, silued.up(at))

                for u in range(4):
                    silu(u)
                eng.wait_ge(c_turned.sem, c_turned.count(at, 1))
                eng.activation(cT[:], ps[0:NE, 5, :], ACT.Copy).then_inc(comb_copied.sem, comb_copied.up(at))
                for u in range(4, NE * FB):
                    silu(u)

            def ssm_inputs(at):
                root(at, n_ssm)
                eng.wait_ge(xT_done.sem, xT_done.count(at, 1))
                eng.activation(
                    xT.rearrange("p h t -> p (h t)"),
                    ps[:, 5:7, :].rearrange("p h t -> p (h t)"), ACT.Copy).then_inc(xT_copied.sem, xT_copied.up(at))
                eng.wait_ge(dt_done.sem, dt_done.count(at, 1))
                eng.activation(dtlow[0:DR, :], ps[0:DR, 4, :], ACT.Copy).then_inc(dt_copied.sem, dt_copied.up(at))
                eng.wait_ge(dl_done.sem, dl_done.count(at, 1))
                eng.activation(sp[1], ps[:, 5:7, :].rearrange("p h t -> p (h t)"), ACT.Abs
                               ).then_inc(dl_abs.sem, dl_abs.up(at))
                eng.wait_ge(dl_abs.sem, dl_abs.count(at, 1))
                eng.activation(sp[1], sp[1], ACT.Exp, scale=-1.0).then_inc(dl_exp.sem, dl_exp.up(at))
                eng.wait_ge(dl_exp.sem, dl_exp.count(at, 1))
                eng.activation(sp[3], sp[1], ACT.Ln, bias=one[:]).then_inc(dl_ln.sem, dl_ln.up(at))
                eng.wait_ge(xmix_done.sem, xmix_done.count(at, 1))
                eng.activation(x_bc[:].rearrange("p b c -> p (b c)"), ps[:, 7, 0:P], ACT.Copy)
                eng.activation(x_mixed[:].rearrange("p b c -> p (b c)"),
                               ps[:, 0:2, :].rearrange("p k c -> p (k c)"), ACT.Copy
                               ).then_inc(x_mixed_a.sem, x_mixed_a.up(at))
                front_root(at, 0, 0)
                for g in range(NG):
                    eng.wait_ge(dl_rep.sem, dl_rep.count(at, g + 1))
                    eng.activation(da[:, g, :], bank(RING[g % 4]), ACT.Exp,
                                   scale=decay[:, g:g + 1]).then_inc(da_ready.sem, da_ready.up(at))
                    if g == FIRST_C + 4:
                        front_c(at, 0, 0)

            def front_root(at, hf, kf):
                eng.wait_ge(ss_done.sem, ss_done.count(at, kf + 1))
                eng.activation(nrm[:], ss[:], ACT.Sqrt).then_inc(nrm_done.sem, nrm_done.up(at))

            def front_c(at, hf, kf):
                eng.wait_ge(c_rep.sem, c_rep.count(at, kf + 1))
                eng.activation(crep[:, hf, :], ps[:, 7, TH:T], ACT.Copy).then_inc(c_copied.sem, c_copied.up(at))

            def fill(at, hf, kf):
                eng.wait_ge(du_done.sem, du_done.count(at, kf + 1))
                eng.wait_ge(b_ready.sem, b_ready.count(at, kf + 1))
                for n in range(NS):
                    ins = eng.activation(scan_in[:, hf, 0, :, n, :], du_groups(0), ACT.Copy,
                                         scale=b_norm[:, 0, n:n + 1])
                ins.then_inc(filled_a.sem, filled_a.up(at))

            def front(at, hf, kf):
                front_root(at, hf, kf)
                front_c(at, hf, kf)
                fill(at, hf, kf)

            def back(at, hf, kb, last):
                cols = slice(hf * TH + 1, (hf + 1) * TH + 1)
                if not last:
                    for h in range(DB):
                        ins = eng.activation(ytmp[:, h, :], yT[:, h, cols], ACT.Identity,
                                             bias=beta_s[:, h:h + 1], scale=1.0 - STEP)
                    ins.then_inc(ytmp_done.sem, ytmp_done.up(at))
                eng.wait_ge(nsummed.sem, nsummed.count(at, LAG + NG // 4 * kb))
                eng.activation(yscT[:].rearrange("p h t -> p (h t)"), bank(3),
                                                 ACT.Copy).then_inc(ysc_copied.sem, ysc_copied.up(at))
                eng.wait_ge(zvar.sem, zvar.count(at, kb + 1))
                eng.activation(std[:, 0:HB], meanvar[:, 0:HB, 1], ACT.Sqrt, bias=eps[:]).then_inc(zstd.sem, zstd.up(at))
                eng.wait_ge(znmr.sem, znmr.count(at, kb + 1))
                for tb in range(HB):
                    ins = eng.activation(vn[:, tb, :], half5[:, tb, :], ACT.Identity,
                                         bias=nmr[:, tb:tb + 1], scale=rstd[:, tb:tb + 1])
                ins.then_inc(v_done.sem, v_done.up(at))
                if last:
                    eng.wait_ge(vt_done.sem, vt_done.count(at, kb + 1))
                    for h in range(DB):
                        ins = eng.activation(yT[:, h, cols], ps[:, 5, h * TH:(h + 1) * TH], ACT.Identity,
                                             bias=w["beta"][:, h:h + 1], scale=w["gamma"][:, h:h + 1])
                    ins.then_inc(y_ready.sem, y_ready.up(at))

            def ssm_output(at):
                eng.wait_ge(z2_done.sem, z2_done.count(at, 1))
                eng.activation(gz.rearrange("p h t -> p (h t)"),
                                              ps[:, 0:2, :].rearrange("p h t -> p (h t)"), ACT.Silu).then_inc(z2_silu.sem, z2_silu.up(at))

            eng.wait_ge(loaded, 16 * n_loads)
            eng.activation(decay[:], w["a_log"][:], ACT.Exp).then_inc(prep_a, 1)
            eng.wait_ge(prepared, 1)
            with eng.Fori(0, B) as b:
                at = Place(b, 0)
                attention(at)
                mixture(at)
                ssm_inputs(at)
                front(at, 1, 1)
                with eng.Fori(0, ITERS) as i:
                    turn = Place(b, 1, i)
                    for hf in range(2):
                        back(turn, hf, hf, False)
                        front(turn, hf, hf)
                at = Place(b, 2)
                back(at, 0, 0, True)
                back(at, 1, 1, True)
                ssm_output(at)
                mixture(at)

        @block.vector
        def _(eng):
            def hold(eng):
                holds.append(len(holds))
                eng.memset(held[:, holds[-1]:holds[-1] + 1], 0.0)

            holds = []

            def moments(at, src, done, nb=TB):
                for tb in range(nb):
                    ins = eng.bn_stats(stats[:, tb, :], src[:, tb, :])
                ins.then_inc(vchain.sem, vchain.up(at))
                eng.wait_ge(vchain.sem, vchain.last(at))
                hold(eng)
                for tb in range(nb):
                    ins = eng.bn_aggr(meanvar[:, tb, :], stats[:, tb, :])
                ins.then_inc(done.sem, done.up(at))

            def norm(at, n, src):
                moments(at, src, n.var)
                eng.wait_ge(n.std.sem, n.std.count(at, 1))
                eng.reciprocal(rstd[:], std[:]).then_inc(vchain.sem, vchain.up(at))
                eng.wait_ge(vchain.sem, vchain.last(at))
                for tb in range(TB):
                    ins = eng.tensor_scalar(xn[:, tb, :], src[:, tb, :], meanvar[:, tb, 0:1],
                                            rstd[:, tb:tb + 1], ALU.subtract, ALU.mult)
                ins.then_inc(n.xn.sem, n.xn.up(at))

            def attention(at):
                eng.wait_ge(x_loaded.sem, x_loaded.count(at, 1))
                norm(at, n_att, x_in)
                eng.tensor_tensor(x_res[:], x_in[:],
                                  w["out_b"][:].rearrange("p (o c) -> p o c", o=1).broadcast_to([P, TB, DM]),
                                  ALU.add)
                eng.memset(smax[:], 0.0).then_inc(x_free.sem, x_free.up(at))
                eng.memset(heads_flat[64:BIAS], 0.0)
                eng.memset(heads[BIAS:BIAS + 2, :, 1], -1.0).then_inc(heads_zero.sem, heads_zero.up(at))
                eng.memset(vaug_flat, 0.0).then_inc(v_zero.sem, v_zero.up(at))
                eng.wait_ge(qkv_done.sem, qkv_done.count(at, 1))
                eng.tensor_tensor(
                    qkv, ps[:, 0:4, 0:3 * DM],
                    w["qkv_b"][:].rearrange("p (o c) -> p o c", o=1).broadcast_to([P, TB, 3 * DM]), ALU.add).then_inc(vchain.sem, vchain.up(at))
                eng.wait_ge(vchain.sem, vchain.last(at))
                qk = qkv[:, :, 0:2 * DM].rearrange("p b (h j two) -> p two b h j", two=2, j=4)
                even, odd = qk[:, 0], qk[:, 1]
                r = rot.rearrange("p b (h two j) -> p two b h j", two=2, j=4)
                ta = rtmp[:, 0].rearrange("p b (h j) -> p b h j", j=4)
                tc = rtmp[:, 1].rearrange("p b (h j) -> p b h j", j=4)
                angles = [w[n][:].rearrange("p b (o j) -> p b o j", o=1).broadcast_to([P, TB, 2 * NH, 4])
                          for n in ("cosine", "sine")]
                for half, (first, second, op) in enumerate(((even, odd, ALU.subtract), (odd, even, ALU.add))):
                    eng.tensor_tensor(ta, first, angles[0], ALU.mult)
                    eng.tensor_tensor(tc, second, angles[1], ALU.mult).then_inc(vchain.sem, vchain.up(at))
                    eng.wait_ge(vchain.sem, vchain.last(at))
                    ins = eng.tensor_tensor(r[:, half], ta, tc, op)
                    if half == 0:
                        ins.then_inc(vchain.sem, vchain.up(at))
                        eng.wait_ge(vchain.sem, vchain.last(at))
                ins.then_inc(rot_done.sem, rot_done.up(at))
                first = [qk_slots[:, :, :, PARTS * n, :] for n in range(PARTS)]
                full = rot.rearrange("p b (k h c) -> p k b h c", k=2, c=HD)
                rest = left.rearrange("p (k n c) -> p k n c", k=2, c=HD)
                eng.wait_ge(rot_done.sem, rot_done.count(at, 1))
                eng.tensor_copy(slots[:, :, :, :, 0, :], full).then_inc(part_done.sem, part_done.up(at))
                eng.wait_ge(part_done.sem, part_done.count(at, 1))
                eng.tensor_tensor(left.rearrange("p (k b h c) -> p k b h c", k=2, b=TB, c=HD), full,
                                  slots[:, :, :, :, 0, :], ALU.subtract).then_inc(vchain.sem, vchain.up(at))
                eng.wait_ge(vchain.sem, vchain.last(at))
                eng.tensor_copy(first[1], rest).then_inc(part_done.sem, part_done.up(at))
                eng.wait_ge(part_done.sem, part_done.count(at, 2))
                eng.tensor_tensor(first[2], rest, first[1], ALU.subtract).then_inc(part_done.sem, part_done.up(at))
                for part, (low, high) in enumerate(K_SLOTS):
                    if part == PARTS - 1:
                        eng.wait_ge(part_done.sem, part_done.count(at, PARTS))
                    ins = eng.tensor_copy(
                        qk_slots[:, 1, :, low:high + 1:high - low, :],
                        qk_slots[:, 1, :, PARTS * part:PARTS * part + 1, :].broadcast_to([P, TB * NH, 2, HD]))
                ins.then_inc(repeated_v.sem, repeated_v.up(at))
                eng.wait_ge(v_zero.sem, v_zero.count(at, 1))
                eng.memset(vaug[:, :, :, HD:HD + 1], 1.0).then_inc(vchain.sem, vchain.up(at))
                eng.wait_ge(vchain.sem, vchain.last(at))
                eng.tensor_copy(
                    vaug[:, :, :, 0:HD], qkv[:, :, 2 * DM:].rearrange("p b (h c) -> p b h c", c=HD)).then_inc(v_ready.sem, v_ready.up(at))

                def rowmax(h, qb):
                    u = TB * h + qb
                    eng.wait_ge(scored.sem, scored.count(at, u + 1))
                    eng.tensor_reduce(smax[:, h % 2, qb:qb + 1], bank(u % 3), AX, ALU.max
                                      ).then_inc(maxed.sem, maxed.up(at))

                def split_max(h):
                    eng.wait_ge(maxed.sem, maxed.count(at, TB * (h + 1)))
                    high = smax_b[:, h % 2, :, 0]
                    eng.tensor_copy(high, smax[:, h % 2, :]).then_inc(vchain.sem, vchain.up(at))
                    eng.wait_ge(vchain.sem, vchain.last(at))
                    eng.tensor_tensor(smax_b[:, h % 2, :, 1], smax[:, h % 2, :], high, ALU.subtract
                                      ).then_inc(max_parts.sem, max_parts.up(at))

                def copy_max(h):
                    eng.wait_ge(max_turned.sem, max_turned.count(at, h + 1))
                    eng.tensor_copy(heads[BIAS:BIAS + 2, h % QUAD, 0], ps[BIAS:BIAS + 2, 6, :]
                                    ).then_inc(max_copied.sem, max_copied.up(at))

                def normalise(c):
                    eng.wait_ge(o_turned.sem, o_turned.count(at, c + 1))
                    o = blocks(7).rearrange("p b (j r) -> p b j r", r=32)
                    eng.reciprocal(rsum[:], o[:, :, :, HD]).then_inc(vchain.sem, vchain.up(at))
                    eng.wait_ge(vchain.sem, vchain.last(at))
                    dst = attn[:, :, c * HG * HD:(c + 1) * HG * HD].rearrange("p b (j r) -> p b j r", r=HD)
                    eng.tensor_tensor(
                        dst, o[:, :, :, 0:HD],
                        rsum[:].rearrange("p b (j o) -> p b j o", o=1).broadcast_to([P, TB, HG, HD]),
                        ALU.mult).then_inc(o_normed.sem, o_normed.up(at))

                for h in range(NH + AHEAD + 2):
                    behind = h - AHEAD
                    for qb in range(TB):
                        if qb == MAX_AT and 1 <= h <= NH:
                            copy_max(h - 1)
                        if h < NH:
                            rowmax(h, qb)
                    if h < NH:
                        split_max(h)
                    if behind > HG and behind % HG == 1:
                        normalise(behind // HG - 1)
                eng.wait_ge(projected.sem, projected.count(at, 1))
                eng.tensor_tensor(x_res[:], blocks(6), x_res[:], ALU.add).then_inc(x1_ready.sem, x1_ready.up(at))

            def mixture(at, dst, ready):
                norm(at, n_moe, x_res)
                eng.wait_ge(routed.sem, routed.count(at, 1))
                logits = ps[:, 5, 0:TB * NE].rearrange("p (b e) -> p b e", b=TB)
                per_token = lambda v: v.rearrange("p (b o) -> p b o", o=1).broadcast_to([P, TB, NE])
                eng.tensor_reduce(rs[:, 0], logits, AX, ALU.max).then_inc(vchain.sem, vchain.up(at))
                eng.wait_ge(vchain.sem, vchain.last(at))
                eng.tensor_tensor(rt[:, 0], logits, per_token(rs[:, 0]), ALU.subtract).then_inc(r_shift.sem, r_shift.up(at))
                eng.wait_ge(r_exp.sem, r_exp.count(at, 1))
                eng.tensor_reduce(rs[:, 1], rt[:, 1], AX, ALU.add).then_inc(vchain.sem, vchain.up(at))
                eng.wait_ge(vchain.sem, vchain.last(at))
                eng.reciprocal(rs[:, 2], rs[:, 1]).then_inc(vchain.sem, vchain.up(at))
                eng.wait_ge(vchain.sem, vchain.last(at))
                eng.tensor_tensor(rt[:, 2], rt[:, 1], per_token(rs[:, 2]), ALU.mult).then_inc(vchain.sem, vchain.up(at))
                eng.wait_ge(vchain.sem, vchain.last(at))
                hold(eng)
                for tb in range(TB):
                    ins = eng.max(top[:, tb, :], rt[:, 2, tb, :])
                ins.then_inc(vchain.sem, vchain.up(at))
                eng.wait_ge(vchain.sem, vchain.last(at))
                hold(eng)
                for tb in range(TB):
                    ins = eng.max_index(topi[:, tb, :], top[:, tb, :], rt[:, 2, tb, :])
                ins.then_inc(vchain.sem, vchain.up(at))
                eng.wait_ge(vchain.sem, vchain.last(at))
                eng.tensor_copy(topf[:], topi[:]).then_inc(vchain.sem, vchain.up(at))
                eng.wait_ge(vchain.sem, vchain.last(at))
                numbers = w["experts"][:].rearrange("p (o e) -> p o e", o=1).broadcast_to([P, TB, NE])
                eng.tensor_tensor(rt[:, 3], numbers, topf[:, :, 0:1].broadcast_to([P, TB, NE]), ALU.is_equal)
                eng.tensor_tensor(
                    rt[:, 4], numbers, topf[:, :, 1:2].broadcast_to([P, TB, NE]), ALU.is_equal).then_inc(vchain.sem, vchain.up(at))
                eng.wait_ge(vchain.sem, vchain.last(at))
                eng.tensor_tensor(rt[:, 5], rt[:, 3], rt[:, 4], ALU.add).then_inc(vchain.sem, vchain.up(at))
                eng.wait_ge(vchain.sem, vchain.last(at))
                eng.tensor_tensor(rt[:, 6], rt[:, 5], rt[:, 2], ALU.mult).then_inc(vchain.sem, vchain.up(at))
                eng.wait_ge(vchain.sem, vchain.last(at))
                eng.tensor_reduce(rs[:, 3], rt[:, 6], AX, ALU.add).then_inc(vchain.sem, vchain.up(at))
                eng.wait_ge(vchain.sem, vchain.last(at))
                eng.tensor_scalar(rs[:, 1], rs[:, 3], 1e-9, None, ALU.add).then_inc(vchain.sem, vchain.up(at))
                eng.wait_ge(vchain.sem, vchain.last(at))
                eng.reciprocal(rs[:, 2], rs[:, 1]).then_inc(vchain.sem, vchain.up(at))
                eng.wait_ge(vchain.sem, vchain.last(at))
                eng.tensor_tensor(rt[:, 7], rt[:, 6], per_token(rs[:, 2]), ALU.mult).then_inc(r_comb.sem, r_comb.up(at))

                def hide(u):
                    e, f = divmod(u, FB)
                    eng.wait_ge(upped.sem, upped.count(at, u + 1))
                    eng.wait_ge(silued.sem, silued.count(at, u + 1))
                    if e >= 2 and f == 0:
                        eng.wait_ge(downed.sem, downed.count(at, e - 1))
                    eng.scalar_tensor_tensor(
                        out=hid[:, e % 2, f, :], in0=bank(2 + u % 2), scalar=w["up_b"][:, e, f:f + 1],
                        in1=gs[:, u % 2, :], op0=ALU.add, op1=ALU.mult).then_inc(hidden.sem, hidden.up(at))

                def add_expert(e):
                    eng.wait_ge(downed.sem, downed.count(at, e + 1))
                    to = dst if e == NE - 1 else acc
                    for tb in range(TB):
                        ins = eng.scalar_tensor_tensor(
                            out=to[:, tb, :], in0=blocks(6 + e % 2)[:, tb, :],
                            scalar=rt[:, 7, tb, e:e + 1], in1=acc[:, tb, :], op0=ALU.mult, op1=ALU.add)
                    ins.then_inc(summed.sem, summed.up(at))
                    if e == NE - 1:
                        return ins
                    eng.wait_ge(summed.sem, summed.count(at, e + 1))

                for u in range(4):
                    hide(u)
                eng.wait_ge(biased.sem, biased.count(at, 1))
                eng.tensor_tensor(acc, blocks(4), x_res[:], ALU.add).then_inc(vchain.sem, vchain.up(at))
                eng.wait_ge(vchain.sem, vchain.last(at))
                for e in range(NE):
                    if e == NE - 1 and ready is not None:
                        eng.wait_ge(stored.sem, stored.count(at, 1))
                    add_expert(e)
                    if e < NE - 2:
                        hide(2 * e + 4)
                        hide(2 * e + 5)
                eng.wait_ge(summed.sem, summed.count(at, NE))
                if ready is not None:
                    eng.memset(rs[:, 0], 0.0).then_inc(ready.sem, ready.up(at))

            def ssm_inputs(at):
                norm(at, n_ssm, x_res)
                eng.memset(yT[:], 0.0).then_inc(y_ready.sem, y_ready.up(at))
                eng.wait_ge(dl_abs.sem, dl_abs.count(at, 1))
                eng.tensor_scalar(sp[0], ps[:, 5:7, :].rearrange("p h t -> p (h t)"), 0.0, None, ALU.max
                                  ).then_inc(dl_relu.sem, dl_relu.up(at))
                eng.wait_ge(dl_exp.sem, dl_exp.count(at, 1))
                eng.tensor_scalar(sp[2], sp[1], 1.0, None, ALU.add)
                flat = delta[:].rearrange("p b c -> p (b c)")
                eng.tensor_scalar(flat, sp[1], -0.5, 1.0, ALU.mult, ALU.add
                                  ).then_inc(vchain.sem, vchain.up(at))
                eng.wait_ge(vchain.sem, vchain.last(at))
                eng.scalar_tensor_tensor(out=sp[2], in0=sp[2], scalar=-1.0, in1=sp[1],
                                         op0=ALU.add, op1=ALU.subtract).then_inc(vchain.sem, vchain.up(at))
                eng.wait_ge(vchain.sem, vchain.last(at))
                eng.tensor_tensor(sp[2], sp[2], flat, ALU.mult).then_inc(vchain.sem, vchain.up(at))
                eng.wait_ge(vchain.sem, vchain.last(at))
                eng.tensor_tensor(sp[2], sp[0], sp[2], ALU.subtract).then_inc(vchain.sem, vchain.up(at))
                eng.wait_ge(vchain.sem, vchain.last(at))
                eng.wait_ge(dl_ln.sem, dl_ln.count(at, 1))
                eng.tensor_tensor(flat, sp[2], sp[3], ALU.add).then_inc(dl_ready.sem, dl_ready.up(at))
                eng.wait_ge(dl_ready.sem, dl_ready.count(at, 1))
                for e in range(EXPAND):
                    eng.tensor_copy(chunk(e), repeated(e)).then_inc(expanded.sem, expanded.up(at))
                    if e == 0:
                        front_bc(at, 0, 0)
                front_norm(at, 0, 0)
                front_du(at, 0, 0)
                for e in range(EXPAND):
                    eng.wait_ge(dl_rep.sem, dl_rep.count(at, ge * (e + 1)))
                    if e == 0:
                        eng.wait_ge(du_done.sem, du_done.count(at, 1))
                        eng.wait_ge(b_ready.sem, b_ready.count(at, 1))
                    for tb in range(HB):
                        ins = eng.tensor_tensor(
                            scan_in[:, 0, tb, ge * e:ge * (e + 1)],
                            du[:, tb, ge * GC * e:ge * GC * (e + 1)].rearrange(
                                "p (g o c) -> p g o c", o=1, c=GC).broadcast_to([P, ge, NS, GC]),
                            b_norm[:, tb, :].rearrange("p (o n q) -> p o n q", o=1, q=1
                                                       ).broadcast_to([P, ge, NS, GC]), ALU.mult)
                    if e >= EXPAND - 2:
                        filled = (filled_a, filled_v)[e % 2]
                        ins.then_inc(filled.sem, filled.up(at))
                eng.wait_ge(x_mixed_a.sem, x_mixed_a.count(at, 1))
                eng.tensor_tensor(x_skip[:], x_mixed[:],
                                  w["skip"][:].rearrange("p (o c) -> p o c", o=1).broadcast_to([P, TB, DI]),
                                  ALU.mult).then_inc(vchain.sem, vchain.up(at))

            def front_bc(at, hf, kf):
                eng.wait_ge(bc_done.sem, bc_done.count(at, kf + 1))
                eng.tensor_copy(bcs[:].rearrange("p b k n -> p (b k n)"),
                                                 ps[:, 7, 0:HB * 2 * NS]).then_inc(vchain.sem, vchain.up(at))
                eng.wait_ge(vchain.sem, vchain.last(at))
                eng.tensor_tensor(bcq[:], bcs[:], bcs[:], ALU.mult).then_inc(vchain.sem, vchain.up(at))
                eng.wait_ge(vchain.sem, vchain.last(at))
                eng.tensor_reduce(ss[:], bcq[:].rearrange("p b k n -> p (b k) n"),
                                                 AX, ALU.add).then_inc(ss_done.sem, ss_done.up(at))

            def front_norm(at, hf, kf):
                eng.wait_ge(nrm_done.sem, nrm_done.count(at, kf + 1))
                eng.tensor_scalar(rn[:], nrm[:], EPS, None, ALU.max).then_inc(vchain.sem, vchain.up(at))
                eng.wait_ge(vchain.sem, vchain.last(at))
                eng.reciprocal(rn[:], rn[:]).then_inc(vchain.sem, vchain.up(at))
                eng.wait_ge(vchain.sem, vchain.last(at))
                r = rn[:].rearrange("p (b k) -> p k b", k=2)
                eng.tensor_tensor(
                    c_norm[:], bcs[:, :, 1, :].rearrange("p b (n o) -> p b n o", o=1).broadcast_to([P, HB, NS, GC]),
                    r[:, 1].rearrange("p (b o q) -> p b o q", o=1, q=1).broadcast_to([P, HB, NS, GC]),
                    ALU.mult).then_inc(c_ready.sem, c_ready.up(at))
                eng.tensor_tensor(
                    b_norm[:], bcs[:, :, 0, :],
                    r[:, 0].rearrange("p (b o) -> p b o", o=1).broadcast_to([P, HB, NS]), ALU.mult).then_inc(b_ready.sem, b_ready.up(at))

            def front_du(at, hf, kf):
                eng.wait_ge(u_done.sem, u_done.count(at, kf + 1))
                eng.tensor_tensor(du[:], half6, delta[:, hf * HB:(hf + 1) * HB, :],
                                                 ALU.mult).then_inc(du_done.sem, du_done.up(at))

            def fill(at, hf, kf, ns):
                if ns[0] == 0:
                    eng.wait_ge(du_done.sem, du_done.count(at, kf + 1))
                    eng.wait_ge(b_ready.sem, b_ready.count(at, kf + 1))
                for n in ns:
                    ins = eng.tensor_scalar(scan_in[:, hf, 1, :, n, :], du_groups(1),
                                            b_norm[:, 1, n:n + 1], None, ALU.mult)
                if ns[-1] == NS - 1:
                    ins.then_inc(filled_v.sem, filled_v.up(at))

            def back_var(at, hf, kb):
                eng.wait_ge(z_done.sem, z_done.count(at, kb + 1))
                moments(at, half5, zvar, HB)

            def back_norm(at, hf, kb):
                eng.wait_ge(zstd.sem, zstd.count(at, kb + 1))
                eng.reciprocal(rstd[:, 0:HB], std[:, 0:HB]).then_inc(vchain.sem, vchain.up(at))
                eng.wait_ge(vchain.sem, vchain.last(at))
                eng.scalar_tensor_tensor(
                    out=nmr[:, 0:HB], in0=meanvar[:, 0:HB, 0], scalar=-1.0, in1=rstd[:, 0:HB],
                    op0=ALU.mult, op1=ALU.mult).then_inc(znmr.sem, znmr.up(at))

            def back_y(at, hf, kb):
                eng.wait_ge(vt_done.sem, vt_done.count(at, kb + 1))
                eng.wait_ge(ytmp_done.sem, ytmp_done.count(at, kb + 1))
                for h in range(DB):
                    ins = eng.scalar_tensor_tensor(
                        out=yT[:, h, hf * TH + 1:(hf + 1) * TH + 1], in0=ps[:, 5, h * TH:(h + 1) * TH],
                        scalar=gamma_s[:, h:h + 1], in1=ytmp[:, h, :], op0=ALU.mult, op1=ALU.add)
                ins.then_inc(y_ready.sem, y_ready.up(at))

            def scan_unit(at, hf, ks, kb, kf):
                other = 1 - hf
                follows = kb is not None
                for s in range(NG):
                    if s % 2 == 0:
                        eng.wait_ge(in_turned.sem, in_turned.count(at, NG // 2 * ks + s // 2 + 1))
                        if s >= NHID or follows:
                            eng.wait_ge(prod_done.sem, prod_done.count(at, NG // 2 * ks + (s - NHID) // 2 + 1))
                    eng.tensor_tensor_scan(
                        hst[:, s % NHID, :], da[:, ORDER[s], hf * TH:(hf + 1) * TH],
                        ps[:, RING[s // 2 % 4], (s % 2) * TH:(s % 2 + 1) * TH],
                        0.0 if hf == 0 else hend[:, s:s + 1], ALU.mult, ALU.add
                    ).then_inc(scanned.sem, scanned.up(at))
                    if hf == 0 and s % NHID == NHID - 1:
                        eng.wait_ge(scanned.sem, scanned.count(at, NG * ks + s + 1))
                        eng.tensor_copy(hend[:, s - NHID + 1:s + 1], hst[:, :, TH - 1]
                                        ).then_inc(vchain.sem, vchain.up(at))
                        eng.wait_ge(vchain.sem, vchain.last(at))
                    if follows:
                        if s == DVE_VAR:
                            back_var(at, other, kb)
                        if s == DVE_NORM:
                            back_norm(at, other, kb)
                        if s == DVE_Y and kf is not None:
                            back_y(at, other, kb)
                    if kf is not None:
                        if s == (DVE_BC if follows else 8):
                            front_bc(at, other, kf)
                        if s == (DVE_BCN if follows else 11):
                            front_norm(at, other, kf)
                        if s == (DVE_DU if follows else 14):
                            front_du(at, other, kf)
                        n = 2 * (s - DVE_FILL)
                        if 0 <= n < NS:
                            fill(at, other, kf, (n, n + 1))

            def ssm_output(at):
                eng.wait_ge(z2_silu.sem, z2_silu.count(at, 1))
                eng.tensor_tensor(gy, gz, yT[:, :, 1:T + 1], ALU.mult).then_inc(gy_done.sem, gy_done.up(at))
                eng.wait_ge(o2_done.sem, o2_done.count(at, 1))
                eng.tensor_tensor(x_res[:], blocks(2), x_res[:], ALU.add).then_inc(x3_ready.sem, x3_ready.up(at))
                eng.wait_ge(x3_ready.sem, x3_ready.count(at, 1))

            eng.memset(eps[:], EPS)
            eng.memset(one[:], 1.0)
            eng.memset(dtlow[:], 1.0)
            eng.wait_ge(loaded, 16 * n_loads)
            eng.tensor_scalar(gamma_s[:], w["gamma"][:], STEP, None, ALU.mult)
            eng.tensor_scalar(beta_s[:], w["beta"][:], STEP, None, ALU.mult)
            eng.tensor_copy(ident_b[:], ident[:])
            eng.wait_ge(prep_a, 1)
            eng.tensor_scalar(decay[:], decay[:], -1.0, None, ALU.mult)
            ins = eng.tensor_scalar(mix_y[:], w["w_mix"][:], -1.0, None, ALU.mult)
            ins.then_inc(prepared_v, 1)
            eng.wait_ge(prepared_v, 1)
            for h in range(DB):
                ins = eng.tensor_tensor(mix_y[:, h, h * P:(h + 1) * P], mix_y[:, h, h * P:(h + 1) * P],
                                        ident[:], ALU.add)
            ins.then_inc(prepared_v, 1)
            eng.wait_ge(prepared_v, 2)
            for h in range(DB):
                ins = eng.tensor_tensor(mix_yd[:, h, :], mix_y[:, h, :], w["skip"][:], ALU.mult)
            ins.then_inc(prepared, 1)
            eng.wait_ge(prepared, 1)
            with eng.Fori(0, B) as b:
                at = Place(b, 0)
                attention(at)
                eng.wait_ge(x1_ready.sem, x1_ready.count(at, 1))
                mixture(at, x_res, None)
                ssm_inputs(at)
                scan_unit(at, 0, 0, None, 1)
                hold(eng)
                with eng.Fori(0, ITERS) as i:
                    turn = Place(b, 1, i)
                    scan_unit(turn, 1, 0, 0, 0)
                    scan_unit(turn, 0, 1, 1, 1)
                at = Place(b, 2)
                scan_unit(at, 1, 0, 0, None)
                back_var(at, 1, 1)
                back_norm(at, 1, 1)
                ssm_output(at)
                mixture(at, x_out, out_ready)

        @block.gpsimd
        def _(eng):
            def scan_unit(at, hf, ks, ready, carried):
                sums = NG // 4 * ks + (LAG if carried else 0)
                for p in range(NG // 2):
                    eng.wait_ge(scanned.sem, scanned.count(at, NG * ks + 2 * p + 2))
                    if p == 0:
                        eng.wait_ge(c_copied.sem, c_copied.count(at, ready))
                    if p % 2 == 0 and (p >= NPROD // 2 or carried):
                        eng.wait_ge(nsummed.sem, nsummed.count(at, sums + p // 2 - 1))
                    s = 2 * p % NHID
                    eng.tensor_tensor(
                        prod[:, s:s + 2, :], hst[:, s:s + 2, :],
                        crep[:, hf:hf + 1, :].broadcast_to([P, 2, TH]), ALU.mult).then_inc(prod_done.sem, prod_done.up(at))

            eng.wait_ge(loaded, 16 * n_loads)
            with eng.Fori(0, B) as b:
                at = Place(b, 0)
                scan_unit(at, 0, 0, 1, False)
                with eng.Fori(0, ITERS) as i:
                    turn = Place(b, 1, i)
                    scan_unit(turn, 1, 0, 0, True)
                    scan_unit(turn, 0, 1, 1, True)
                scan_unit(Place(b, 2), 1, 0, 0, True)

        for name, s in sems:
            assert tuple(s.seen) == tuple(s.n), (name, s.seen, s.n)


def _rows(a):
    return np.ascontiguousarray(a.reshape(-1, P, a.shape[-1]).transpose(1, 0, 2))


def kernel(**inputs):
    import concourse.bacc as bacc
    from concourse.bass_utils import run_bass_kernel_spmd

    a = {k: np.asarray(v) for k, v in inputs.items()}
    b, f = (lambda n: a["L0_attn_b_" + n]), (lambda n: a["L0_ffn_" + n])
    wide = lambda v: np.ascontiguousarray(np.broadcast_to(v, (P, v.shape[0])))

    freqs = np.float32(10000.0) ** (np.arange(0, HD, 2, dtype=np.float32) / np.float32(HD))
    angles = np.arange(T, dtype=np.float32)[:, None] * freqs[None, :].astype(np.float32)
    cosine = np.cos(angles.astype(np.float64)).astype(np.float32)
    sine = np.sin(angles.astype(np.float64)).astype(np.float32)
    lanes = np.arange(P)
    sel = np.zeros((P, NR, 32), np.float32)
    for r in range(NR):
        sel[lanes, r, GC * r + lanes % GC] = 1.0

    arrays = {
        "x": a["L0_attn_a_x"],
        "ident": np.eye(P, dtype=np.float32), "sel": sel,
        "cosine": _rows(cosine), "sine": _rows(sine),
        "experts": wide(np.arange(NE, dtype=np.float32)),
        "qkv_w": a["L0_attn_a_qkv_w"], "qkv_b": wide(a["L0_attn_a_qkv_b"]),
        "out_w": a["L0_attn_a_out_w"], "out_b": wide(a["L0_attn_a_out_b"]),
        "w_in": b("W_in").T, "w_x": _rows(b("W_x").T),
        "a_log": b("A_log").reshape(NG, GC, NS).transpose(2, 1, 0).reshape(P, NG),
        "w_bc": _rows(b("W_bc").T), "w_zy": _rows(b("W_zy").T), "w_mix": _rows(b("W_mix").T),
        "skip": wide(b("D")), "gamma": b("ln_gamma").reshape(DB, P).T,
        "beta": b("ln_beta").reshape(DB, P).T, "w_out": _rows(b("W_out").T),
        "router": f("router_w").T,
        "gate_w": f("gate_w").transpose(1, 0, 2), "up_w": f("up_w").transpose(1, 0, 2),
        "gate_b": f("gate_b").reshape(NE, FB, P).transpose(2, 0, 1),
        "up_b": f("up_b").reshape(NE, FB, P).transpose(2, 0, 1),
        "down_w": f("down_w").reshape(NE, FB, P, DM).transpose(2, 0, 1, 3),
        "w_dt": b("W_dt").T, "b_dt": b("b_dt").reshape(1, DI), "down_b": f("down_b"),
    }
    nc = bacc.Bacc("TRN2", target_bir_lowering=False, num_devices=1)
    in_map, tensors = {}, {}
    for name, v in arrays.items():
        v = np.ascontiguousarray(v)
        in_map["in_" + name] = v
        tensors[name] = nc.dram_tensor("in_" + name, v.shape, F32, kind="ExternalInput").ap()
    out = nc.dram_tensor("out", (B, T, DM), F32, kind="ExternalOutput").ap()
    hybrid_kernel(nc, tensors, out)
    r = run_bass_kernel_spmd(nc, [in_map], core_ids=[0])
    return r.results[0]["out"]
```

```python
from contextlib import ExitStack

import numpy as np
import concourse.bass as bass
from concourse import mybir

P = 128
F32 = mybir.dt.float32
BF16 = mybir.dt.bfloat16
U32 = mybir.dt.uint32
ALU = mybir.AluOpType
ACT = mybir.ActivationFunctionType
AX = mybir.AxisListType.X

B, T, DM = 16, 512, 128
TB = T // P
NH, HD = 16, 8
HG = 4
SCALE = HD ** -0.5
PARTS = 3
SLOTS = PARTS * PARTS
QR = SLOTS * HD
BIAS = 96
K_SLOTS = ((5, 7), (1, 8), (2, 4))
QUAD = 4
NE, DF = 8, 256
FB = DF // P
DI, NS, DR = 256, 16, 8
DB = DI // P
GC = 8
NG = DI // GC
NR = 32 // GC
ITERS, STEP, EPS = 8, 0.99, 1e-5
TH = T // 2
HB = TH // P
RING = (0, 1, 2, 4)
NHID, NPROD = 8, 8
PE_X, PE_Z, PE_V, PE_Y, PE_C, PE_D = 3, 3, 7, 9, 10, 15
DVE_VAR, DVE_NORM, DVE_Y, DVE_BC, DVE_BCN, DVE_DU, DVE_FILL = 7, 8, 12, 17, 18, 18, 23
ACT_FILL = 4
EXPAND = 8
FIRST_C = 15
AHEAD = 2
MAX_AT = 3
PE_START, ACT_START = (1, 2, 3), (4, 7)
DVE_START = ((1,), (2,), (3,), (4, 5), (6,), (7,), (8,), (9,))
LAG = 2
ORDER = [16 * h + NR * q + r for h in range(DB) for r in range(NR) for q in range(4)]


class Place:

    def __init__(self, seq, section, turn=0):
        self.seq, self.section, self.turn = seq, section, turn


class Signal:

    def __init__(self, sem, before, turn, behind, unit=1):
        self.sem, self.n, self.unit = sem, (before, turn, behind), unit
        self.seen = [0, 0, 0]
        self.total = before + ITERS * turn + behind

    def up(self, at):
        self.seen[at.section] += 1
        return self.unit

    def count(self, at, k):
        before, turn, _ = self.n
        skipped = (0, before, before + ITERS * turn)[at.section]
        value = at.seq * (self.total * self.unit) + (skipped + k) * self.unit
        return value + at.turn * (turn * self.unit) if at.section == 1 else value

    def last(self, at):
        return self.count(at, self.seen[at.section])


def hybrid_kernel(nc, t, out):
    with ExitStack() as ctx:
        sems = []

        def sb(name, shape, dt=F32):
            return ctx.enter_context(nc.sbuf_tensor(name, shape, dt))

        def signal(name, before=0, turn=0, behind=0, unit=1):
            s = Signal(ctx.enter_context(nc.semaphore(name)), before, turn, behind, unit)
            sems.append((name, s))
            return s

        ps = ctx.enter_context(nc.psum_tensor("ps", [P, 8, 512], F32))

        WEIGHTS = {
            "ident": [P, P], "sel": [P, NR, 32], "cosine": [P, TB, 4], "sine": [P, TB, 4],
            "experts": [P, NE],
            "qkv_w": [P, 3 * DM], "qkv_b": [P, 3 * DM], "out_w": [P, DM], "out_b": [P, DM],
            "w_in": [P, 2 * DI], "w_x": [P, DB, DR + 2 * NS], "a_log": [P, NG],
            "w_bc": [P, DB, 2 * NS], "w_zy": [P, DB, DI], "w_mix": [P, DB, DI],
            "skip": [P, DI], "gamma": [P, DB], "beta": [P, DB], "w_out": [P, DB, DM],
            "router": [P, NE], "gate_b": [P, NE, FB],
            "up_b": [P, NE, FB],
        }
        w = {name: sb("w_" + name, shape) for name, shape in WEIGHTS.items()}
        w_dt = sb("w_dt", [DR + 1, DI])
        down_b = sb("down_b", [NE, DM])
        ident = w["ident"]
        ident_b = sb("ident_b", [P, P], BF16)

        eps = sb("eps", [P, 1])
        one = sb("one", [P, 1])
        held = sb("held", [P, 32])
        gamma_s = sb("gamma_s", [P, DB])
        beta_s = sb("beta_s", [P, DB])
        decay = sb("decay", [P, NG])
        mix_y = sb("mix_y", [P, DB, DI])
        hend = sb("hend", [P, NG])
        mix_yd = sb("mix_yd", [P, DB, DI])

        x_in = sb("x_in", [P, TB, DM])
        x_res = sb("x_res", [P, TB, DM])
        x_out = sb("x_out", [P, TB, DM])
        xnT = sb("xnT", [P, T])
        stats = sb("stats", [P, TB, 6])
        meanvar = sb("meanvar", [P, TB, 2])
        std = sb("std", [P, TB])
        rstd = sb("rstd", [P, TB])
        nmr = sb("nmr", [P, TB])
        da = sb("da", [P, NG, T])
        region = da[:].rearrange("p g t -> p (g t)")
        used = [0]

        def piece(n):
            at, used[0] = used[0], used[0] + n
            assert used[0] <= NG * T
            return region[:, at:at + n]

        work = sb("work", [P, (NHID + NPROD) * TH])
        scan_in = sb("scan_in", [P, 2, HB, NG, NS, GC])
        third = scan_in[:].rearrange("p f b g n c -> p (f b g n c)")
        gate_w = third[:, 0:2048].rearrange("p (e f) -> p e f", e=NE)
        up_w = third[:, 2048:4096].rearrange("p (e f) -> p e f", e=NE)
        down_w = third[:, 4096:6144].rearrange("p (e f c) -> p e f c", e=NE, f=FB)
        scr = third[:, 6144:10240]

        def ring(at, n):
            return work[:, at * T:(at + n) * T].rearrange("p (k t) -> p k t", t=T)

        slots = piece(2 * TB * NH * QR // 2).bitcast(BF16).rearrange(
            "p (k b h s c) -> p k b h s c", k=2, b=TB, h=NH, s=SLOTS)
        heads_flat = piece(QUAD * 2 * T // 2)
        heads = heads_flat.bitcast(BF16).rearrange("p (h k t) -> p h k t", h=QUAD, k=2)
        left = piece(2 * TB * DM)
        xnT_next = piece(T)
        probsT = piece(HG * TB * T).rearrange("p (j k t) -> p j k t", j=HG, k=TB)
        vaug_flat = third[:, 10240:12288]
        vaug = vaug_flat.rearrange("p (b h r) -> p b h r", b=TB, h=NH)
        qkv = scr[:, 0:TB * 384].rearrange("p (b c) -> p b c", b=TB)
        rot = scr[:, 1536:2560].rearrange("p (b c) -> p b c", b=TB)
        rtmp = scr[:, 2560:3584].rearrange("p (k b c) -> p k b c", k=2, b=TB)
        smax = sb("smax", [P, 2, TB])
        smax_b = sb("smax_b", [P, 2, TB, 2], BF16)
        oT = work[:, 5 * T:6 * T]
        rsum = sb("rsum", [P, TB, HG])
        attn = work[:, 6 * T:7 * T].rearrange("p (b c) -> p b c", b=TB)
        attnT = work[:, 7 * T:8 * T]

        rt = sb("rt", [P, 8, TB, NE])
        top = sb("top", [P, TB, 8])
        topi = sb("topi", [P, TB, 8], U32)
        topf = sb("topf", [P, TB, 8])
        rs = sb("rs", [P, 4, TB])
        cT = sb("cT", [NE, T])
        xn = work[:, 7 * T:8 * T].rearrange("p (b c) -> p b c", b=TB)
        gs = ring(0, 2)
        hid = ring(2, 4).rearrange("p (e f) t -> p e f t", f=FB)
        acc = work[:, 6 * T:7 * T].rearrange("p (b c) -> p b c", b=TB)

        xT = ring(0, DB)
        yT = sb("yT", [P, DB, T + 1])
        x_mixed = sb("x_mixed", [P, TB, DI])
        x_skip = sb("x_skip", [P, TB, DI])
        x_bc = sb("x_bc", [P, TB, 2 * NS])
        dtlow = sb("dtlow", [DR + 1, T])
        delta = sb("delta", [P, TB, DI])
        sp = [scr[:, 1024 * k:1024 * (k + 1)] for k in range(4)]
        bcs = sb("bcs", [P, HB, 2, NS])
        bcq = sb("bcq", [P, HB, 2, NS])
        b_norm = sb("b_norm", [P, HB, NS])
        c_norm = sb("c_norm", [P, HB, NS, GC])
        ss = sb("ss", [P, HB * 2])
        nrm = sb("nrm", [P, HB * 2])
        rn = sb("rn", [P, HB * 2])
        du = sb("du", [P, HB, DI])
        crep = sb("crep", [P, 2, TH])
        hst = work[:, 0:NHID * TH].rearrange("p (k t) -> p k t", t=TH)
        prod = work[:, NHID * TH:].rearrange("p (k t) -> p k t", t=TH)
        yscT = sb("yscT", [P, DB, TH])
        vn = sb("vn", [P, HB, DI])
        ytmp = sb("ytmp", [P, DB, TH])
        gz = ring(0, 2)
        gy = ring(2, 2)

        loaded = ctx.enter_context(nc.semaphore("loaded"))
        prepared = ctx.enter_context(nc.semaphore("prepared"))
        prep_a = ctx.enter_context(nc.semaphore("prep_a"))
        prepared_v = ctx.enter_context(nc.semaphore("prepared_v"))
        x_loaded = signal("x_loaded", 1, unit=16)
        x_free = signal("x_free", 1)
        experts_loaded = signal("experts_loaded", behind=3, unit=16)
        out_ready = signal("out_ready", behind=1)
        stored = signal("stored", behind=1, unit=16)
        vchain = signal("vchain", 55, 16, 20)

        class Norm:

            def __init__(self, name, *n):
                self.var = signal(name + "_var", *n)
                self.std = signal(name + "_std", *n)
                self.xn = signal(name + "_xn", *(TB * k for k in n))
                self.turned = signal(name + "_turned", *n)
                self.xnT = signal(name + "_xnT", *n)

        nchain = signal("nchain", 7)
        n_att, n_moe, n_ssm = Norm("na", 1), Norm("nm", 1, 0, 1), Norm("ns", 1)
        qkv_done = signal("qkv_done", 2)
        qkv_taken = signal("qkv_taken", 2)
        rot_done = signal("rot_done", 1)
        heads_zero = signal("heads_zero", 1)
        part_done = signal("part_done", PARTS)
        repeated_a = signal("repeated_a", PARTS)
        repeated_v = signal("repeated_v", 1)
        qk_turned = signal("qk_turned", NH)
        qk_copied = signal("qk_copied", NH)
        v_zero = signal("v_zero", 1)
        v_ready = signal("v_ready", 1)
        scored = signal("scored", NH * TB)
        maxed = signal("maxed", NH * TB)
        max_parts = signal("max_parts", NH)
        max_turned = signal("max_turned", NH)
        max_copied = signal("max_copied", NH)
        rescored = signal("rescored", NH * TB)
        exped = signal("exped", NH * TB)
        weighed = signal("weighed", NH)
        o_copied = signal("o_copied", NH // HG)
        o_turned = signal("o_turned", NH // HG)
        o_normed = signal("o_normed", NH // HG)
        a_turned = signal("a_turned", 1)
        a_copied = signal("a_copied", 1)
        projected = signal("projected", 1)
        x1_ready = signal("x1_ready", 1)

        routed = signal("routed", 1, 0, 1)
        r_shift = signal("r_shift", 1, 0, 1)
        r_exp = signal("r_exp", 1, 0, 1)
        r_comb = signal("r_comb", 1, 0, 1)
        c_turned = signal("c_turned", 1, 0, 1)
        comb_copied = signal("comb_copied", 1, 0, 1)
        biased = signal("biased", 1, 0, 1)
        nf = NE * FB
        gated = signal("gated", nf, 0, nf)
        upped = signal("upped", nf, 0, nf)
        silued = signal("silued", nf, 0, nf)
        hidden = signal("hidden", nf, 0, nf)
        downed = signal("downed", NE, 0, NE)
        summed = signal("summed", NE, 0, NE)

        xT_done = signal("xT_done", DB)
        xT_copied = signal("xT_copied", DB)
        dt_done = signal("dt_done", 1)
        dt_copied = signal("dt_copied", 1)
        dl_done = signal("dl_done", 1)
        xmix_done = signal("xmix_done", 1)
        x_mixed_a = signal("x_mixed_a", 1)
        dl_abs = signal("dl_abs", 1)
        dl_relu = signal("dl_relu", 1)
        dl_exp = signal("dl_exp", 1)
        dl_ln = signal("dl_ln", 1)
        dl_ready = signal("dl_ready", 1)
        expanded = signal("expanded", EXPAND)
        dl_rep = signal("dl_rep", NG)
        da_ready = signal("da_ready", NG)

        y_ready = signal("y_ready", 1, 2, 2)
        front = (2, 2, 0)
        bc_done = signal("bc_done", *front)
        ss_done = signal("ss_done", *front)
        nrm_done = signal("nrm_done", *front)
        c_ready = signal("c_ready", *front)
        b_ready = signal("b_ready", *front)
        u_done = signal("u_done", *front)
        du_done = signal("du_done", *front)
        c_rep = signal("c_rep", *front)
        c_copied = signal("c_copied", *front)
        filled_a = signal("filled_a", *front)
        filled_v = signal("filled_v", *front)
        scan = (1, 2, 1)
        in_turned = signal("in_turned", *(NG // 2 * n for n in scan))
        scanned = signal("scanned", *(NG * n for n in scan))
        prod_done = signal("prod_done", *(NG // 2 * n for n in scan))
        nsummed = signal("nsummed", NG // 4 - LAG, 2 * NG // 4, NG // 4 + LAG)
        back = (0, 2, 2)
        ysc_copied = signal("ysc_copied", *back)
        z_done = signal("z_done", *back)
        zvar = signal("zvar", *back)
        zstd = signal("zstd", *back)
        znmr = signal("znmr", *back)
        v_done = signal("v_done", *back)
        vt_done = signal("vt_done", *back)
        ytmp_done = signal("ytmp_done", 0, 2, 0)
        z2_done = signal("z2_done", behind=DB)
        z2_silu = signal("z2_silu", behind=DB)
        gy_done = signal("gy_done", behind=DB)
        o2_done = signal("o2_done", behind=1)
        x3_ready = signal("x3_ready", behind=1)

        bank = lambda n: ps[:, n, :]
        blocks = lambda n: ps[:, n, :].rearrange("p (b c) -> p b c", b=TB)
        wide = ps[:, 5:7, :].rearrange("p k c -> p (k c)").rearrange("p (b c) -> p b c", b=TB)
        du_groups = lambda tb: du[:, tb, :].rearrange("p (g c) -> p g c", c=GC)
        ge = NG // EXPAND
        chunk = lambda e: scan_in[:, :, :, ge * e:ge * (e + 1)].rearrange(
            "p f b g n c -> p (f b) g n c")
        repeated = lambda e: delta[:, :, ge * GC * e:ge * GC * (e + 1)].rearrange(
            "p b (g o c) -> p b g o c", o=1, c=GC).broadcast_to([P, TB, ge, NS, GC])
        turned = ps[0:QR, 5, :].bitcast(BF16).rearrange("p (k t) -> p k t", k=2)
        qk_slots = slots.rearrange("p k b h s c -> p k (b h) s c")
        half5 = ps[:, 5, :].rearrange("p (b c) -> p b c", b=HB)
        half6 = ps[:, 6, :].rearrange("p (b c) -> p b c", b=HB)
        n_loads = len(WEIGHTS) + 2

        block = ctx.enter_context(nc.Block())

        def begin_with(start, steps):
            seen = [list(s.seen) for _, s in sems]
            for step in range(steps):
                start(Place(0, 0), step)
            for (_, s), before in zip(sems, seen):
                s.seen[:] = before

        @block.sync
        def _(eng):
            x_t = t["x"].rearrange("b (k p) c -> b p k c", p=P)
            out_t = out.rearrange("b (k p) c -> b p k c", p=P)
            eng.dma_start(x_in[:], x_t[0]).then_inc(x_loaded.sem, 16)
            for name in WEIGHTS:
                eng.dma_start(w[name][:], t[name]).then_inc(loaded, 16)
            eng.dma_start(w_dt[0:DR, :], t["w_dt"]).then_inc(loaded, 16)
            eng.dma_start(w_dt[DR:DR + 1, :], t["b_dt"]).then_inc(loaded, 16)
            eng.dma_start(down_b[:], t["down_b"]).then_inc(stored.sem, 16)
            def load_experts():
                for dst, name in ((gate_w, "gate_w"), (up_w, "up_w"), (down_w, "down_w")):
                    eng.dma_start(dst, t[name]).then_inc(experts_loaded.sem, 16)

            load_experts()
            with eng.Fori(0, B - 1) as b:
                eng.wait_ge(x_free.sem, b + 1)
                eng.dma_start(x_in[:], x_t[b + 1]).then_inc(x_loaded.sem, 16)
                eng.wait_ge(z2_done.sem, DB * (b + 1))
                load_experts()
                eng.wait_ge(out_ready.sem, b + 1)
                eng.dma_start(out_t[b], x_out[:]).then_inc(stored.sem, 16)
            eng.wait_ge(x_free.sem, B)
            eng.dma_start(x_in[:], x_t[B - 1]).then_inc(x_loaded.sem, 16)
            eng.wait_ge(z2_done.sem, DB * B)
            load_experts()
            eng.wait_ge(out_ready.sem, B)
            eng.dma_start(out_t[B - 1], x_out[:]).then_inc(stored.sem, 16)
            eng.wait_ge(stored.sem, 16 * (B + 1))
            eng.wait_ge(experts_loaded.sem, 16 * 3 * (B + 1))
            x_loaded.seen[0] = x_free.n[0]
            stored.seen[2] = 1
            experts_loaded.seen[2] = 3

        @block.tensor
        def _(eng):
            def turn_norm(at, n, dst):
                for tb in range(TB):
                    eng.wait_ge(n.xn.sem, n.xn.count(at, tb + 1))
                    mm = eng.transpose(dst[:, tb, :], xn[:, tb, :], ident[:])
                mm.then_inc(n.turned.sem, n.turned.up(at))

            def start(at, step):
                if step == 0:
                    turn_norm(at, n_att, blocks(5))
                if step in (1, 2):
                    if step == 1:
                        eng.wait_ge(n_att.xnT.sem, n_att.xnT.count(at, 1))
                    else:
                        eng.wait_ge(qkv_taken.sem, qkv_taken.count(at, 1))
                    for k in range(2):
                        tb = 2 * (step - 1) + k
                        mm = eng.matmul(ps[:, 4 + k, 0:3 * DM], xnT_next[:, tb * P:(tb + 1) * P],
                                        w["qkv_w"][:], start=True, stop=True)
                    mm.then_inc(qkv_done.sem, qkv_done.up(at))

            def attention(at):

                def turn_head(h):
                    if h == 0:
                        eng.wait_ge(repeated_a.sem, repeated_a.count(at, PARTS))
                        eng.wait_ge(repeated_v.sem, repeated_v.count(at, 1))
                    else:
                        eng.wait_ge(qk_copied.sem, qk_copied.count(at, h))
                    for k in range(2):
                        for tb in range(TB):
                            mm = eng.transpose(
                                turned[:, k, tb * P:(tb + 1) * P],
                                slots[:, k, tb, h].rearrange("p s c -> p (s c)"), ident_b[:])
                    mm.then_inc(qk_turned.sem, qk_turned.up(at))

                def score(h, qb):
                    u = TB * h + qb
                    if qb == 0:
                        eng.wait_ge(qk_copied.sem, qk_copied.count(at, h + 1))
                    if u >= 3:
                        eng.wait_ge(maxed.sem, maxed.count(at, u - 2))
                    q, k = heads[0:BIAS, h % QUAD, 0], heads[0:BIAS, h % QUAD, 1]
                    mm = eng.matmul(bank(u % 3), q[:, qb * P:(qb + 1) * P], k,
                                    start=True, stop=True)
                    mm.then_inc(scored.sem, scored.up(at))

                def turn_max(h):
                    eng.wait_ge(max_parts.sem, max_parts.count(at, h + 1))
                    if h > 0:
                        eng.wait_ge(max_copied.sem, max_copied.count(at, h))
                    for tb in range(TB):
                        mm = eng.matmul(ps[BIAS:BIAS + 2, 6, tb * P:(tb + 1) * P],
                                        smax_b[:, h % 2, tb, :], ident_b[:],
                                        start=(tb == 0), stop=(tb == TB - 1))
                    mm.then_inc(max_turned.sem, max_turned.up(at))

                def rescore(h, kb):
                    u = TB * h + kb
                    if kb == 0:
                        eng.wait_ge(max_copied.sem, max_copied.count(at, h + 1))
                    if u >= 2:
                        eng.wait_ge(exped.sem, exped.count(at, u - 1))
                    q, k = heads[0:BIAS + 2, h % QUAD, 0], heads[0:BIAS + 2, h % QUAD, 1]
                    mm = eng.matmul(bank(3 + u % 2), k[:, kb * P:(kb + 1) * P], q,
                                    start=True, stop=True)
                    mm.then_inc(rescored.sem, rescored.up(at))

                def weigh(c, kb):
                    eng.wait_ge(exped.sem, exped.count(at, TB * (HG * c + HG - 1) + kb + 1))
                    if c == 0 and kb == 0:
                        eng.wait_ge(v_ready.sem, v_ready.count(at, 1))
                    if c > 0 and kb == 0:
                        eng.wait_ge(o_normed.sem, o_normed.count(at, c))
                    for j in range(HG):
                        mm = eng.matmul(ps[32 * j:32 * j + 32, 7, :],
                                        vaug[:, kb, HG * c + j, :], probsT[:, j, kb, :],
                                        start=(kb == 0), stop=(kb == TB - 1))
                    mm.then_inc(weighed.sem, weighed.up(at))

                def turn_out(c):
                    eng.wait_ge(o_copied.sem, o_copied.count(at, c + 1))
                    for tb in range(TB):
                        mm = eng.transpose(blocks(7)[:, tb, :], oT[:, tb * P:(tb + 1) * P], ident[:])
                    mm.then_inc(o_turned.sem, o_turned.up(at))

                turn_head(0)
                turn_head(1)
                for h in range(NH + AHEAD + 2):
                    behind = h - AHEAD
                    for b in range(TB):
                        if h < NH:
                            score(h, b)
                        if b == MAX_AT - 1 and 1 <= h <= NH:
                            turn_max(h - 1)
                        if behind >= HG and behind % HG == 0:
                            weigh(behind // HG - 1, b)
                        if 0 <= behind < NH:
                            rescore(behind, b)
                    if h + 2 < NH:
                        turn_head(h + 2)
                    if behind > HG and behind % HG == 1:
                        turn_out(behind // HG - 1)
                eng.wait_ge(o_normed.sem, o_normed.count(at, NH // HG))
                for tb in range(TB):
                    mm = eng.transpose(blocks(7)[:, tb, :], attn[:, tb, :], ident[:])
                mm.then_inc(a_turned.sem, a_turned.up(at))
                eng.wait_ge(a_copied.sem, a_copied.count(at, 1))
                for tb in range(TB):
                    mm = eng.matmul(blocks(6)[:, tb, :], attnT[:, tb * P:(tb + 1) * P],
                                    w["out_w"][:], start=(tb == 0), stop=(tb == TB - 1))
                mm.then_inc(projected.sem, projected.up(at))

            def mixture(at, coming=None):
                turn_norm(at, n_moe, blocks(4))
                eng.wait_ge(experts_loaded.sem, experts_loaded.count(at, 3 if at.section == 0 else 6))
                eng.wait_ge(n_moe.xnT.sem, n_moe.xnT.count(at, 1))
                for tb in range(TB):
                    mm = eng.matmul(ps[:, 5, tb * NE:(tb + 1) * NE], xnT[:, tb * P:(tb + 1) * P],
                                    w["router"][:], start=(tb == 0), stop=(tb == TB - 1))
                mm.then_inc(routed.sem, routed.up(at))

                def into(u):
                    e, f = divmod(u, FB)
                    if u >= 2:
                        eng.wait_ge(silued.sem, silued.count(at, u - 1))
                    mm = eng.matmul(bank(u % 2), gate_w[:, e, f * P:(f + 1) * P], xnT[:],
                                    start=True, stop=True)
                    mm.then_inc(gated.sem, gated.up(at))
                    if u >= 2:
                        eng.wait_ge(hidden.sem, hidden.count(at, u - 1))
                    mm = eng.matmul(bank(2 + u % 2), up_w[:, e, f * P:(f + 1) * P], xnT[:],
                                    start=True, stop=True)
                    mm.then_inc(upped.sem, upped.up(at))

                def down(e):
                    eng.wait_ge(hidden.sem, hidden.count(at, FB * (e + 1)))
                    if e >= 2:
                        eng.wait_ge(summed.sem, summed.count(at, e - 1))
                    for tb in range(TB):
                        for f in range(FB):
                            mm = eng.matmul(blocks(6 + e % 2)[:, tb, :],
                                            hid[:, e % 2, f, tb * P:(tb + 1) * P],
                                            down_w[:, e, f, :], start=(tb == 0 and f == 0),
                                            stop=(tb == TB - 1 and f == FB - 1))
                    mm.then_inc(downed.sem, downed.up(at))

                for u in range(4):
                    into(u)
                eng.wait_ge(r_comb.sem, r_comb.count(at, 1))
                for tb in range(TB):
                    mm = eng.transpose(ps[0:NE, 5, tb * P:(tb + 1) * P], rt[:, 7, tb, :], ident[:])
                mm.then_inc(c_turned.sem, c_turned.up(at))
                eng.wait_ge(comb_copied.sem, comb_copied.count(at, 1))
                for tb in range(TB):
                    mm = eng.matmul(blocks(4)[:, tb, :], cT[:, tb * P:(tb + 1) * P], down_b[:],
                                    start=(tb == 0), stop=(tb == TB - 1))
                mm.then_inc(biased.sem, biased.up(at))
                for e in range(NE):
                    down(e)
                    if e < NE - 2:
                        into(2 * e + 4)
                        into(2 * e + 5)
                    if coming is not None and e in PE_START:
                        start(coming, PE_START.index(e))

            def ssm_inputs(at):
                turn_norm(at, n_ssm, blocks(4))
                eng.wait_ge(n_ssm.xnT.sem, n_ssm.xnT.count(at, 1))
                for h in range(DB):
                    mm = eng.matmul(bank(5 + h), w["w_in"][:, h * P:(h + 1) * P], xnT[:],
                                    start=True, stop=True)
                    mm.then_inc(xT_done.sem, xT_done.up(at))
                for h in range(DB):
                    eng.wait_ge(xT_copied.sem, xT_copied.count(at, h + 1))
                    mm = eng.matmul(ps[0:DR, 4, :], w["w_x"][:, h, 0:DR], xT[:, h, :],
                                    start=(h == 0), stop=(h == DB - 1))
                mm.then_inc(dt_done.sem, dt_done.up(at))
                eng.wait_ge(dt_copied.sem, dt_copied.count(at, 1))
                for tb in range(TB):
                    mm = eng.matmul(wide[:, tb, :], dtlow[:, tb * P:(tb + 1) * P], w_dt[:],
                                    start=(tb % 2 == 0), stop=(tb % 2 == 1))
                mm.then_inc(dl_done.sem, dl_done.up(at))
                for tb in range(TB):
                    for h in range(DB):
                        eng.matmul(ps[:, 7, tb * 32:(tb + 1) * 32], xT[:, h, tb * P:(tb + 1) * P],
                                   w["w_x"][:, h, DR:DR + 2 * NS], start=(tb == 0 and h == 0),
                                   stop=(tb == TB - 1 and h == DB - 1))
                for tb in range(TB):
                    for h in range(DB):
                        mm = eng.matmul(ps[:, tb // HB, (tb % HB) * DI:(tb % HB + 1) * DI],
                                        xT[:, h, tb * P:(tb + 1) * P], w["w_mix"][:, h, :],
                                        start=(tb % HB == 0 and h == 0),
                                        stop=(tb % HB == HB - 1 and h == DB - 1))
                mm.then_inc(xmix_done.sem, xmix_done.up(at))
                eng.wait_ge(x_mixed_a.sem, x_mixed_a.count(at, 1))
                eng.wait_ge(dl_relu.sem, dl_relu.count(at, 1))
                front_x(at, 0, 0)
                front_y(at, 0, 0)
                for g in range(NG):
                    if g % (NG // EXPAND) == 0:
                        eng.wait_ge(expanded.sem, expanded.count(at, g * EXPAND // NG + 1))
                    if g >= 4:
                        eng.wait_ge(da_ready.sem, da_ready.count(at, g - 3))
                    for tb in range(TB):
                        mm = eng.transpose(blocks(RING[g % 4])[:, tb, :], group(tb // HB, tb % HB, g),
                                           ident[:])
                    mm.then_inc(dl_rep.sem, dl_rep.up(at))
                    if g == FIRST_C:
                        front_c(at, 0, 0)
                eng.wait_ge(da_ready.sem, da_ready.count(at, NG))

            def group(hf, tb, g):
                return scan_in[:, hf, tb, g].rearrange("p n c -> p (n c)")

            def tokens(hf, tb, shift=1):
                at = (hf * HB + tb) * P + shift
                return slice(at, at + P)

            def front_x(at, hf, kf):
                for tb in range(HB):
                    eng.matmul(ps[:, 7, tb * 32:(tb + 1) * 32], ident[:], x_bc[:, hf * HB + tb, :],
                               start=(tb == 0), stop=False)
                for tb in range(HB):
                    eng.matmul(half6[:, tb, :], ident[:], x_mixed[:, hf * HB + tb, :],
                               start=(tb == 0), stop=False)

            def front_y(at, hf, kf):
                eng.wait_ge(y_ready.sem, y_ready.count(at, kf + 1 if at.section else 1))
                for tb in range(HB):
                    for h in range(DB):
                        mm = eng.matmul(ps[:, 7, tb * 32:(tb + 1) * 32], yT[:, h, tokens(hf, tb, 0)],
                                        w["w_bc"][:, h, :], start=False,
                                        stop=(tb == HB - 1 and h == DB - 1))
                mm.then_inc(bc_done.sem, bc_done.up(at))
                for tb in range(HB):
                    for h in range(DB):
                        mm = eng.matmul(half6[:, tb, :], yT[:, h, tokens(hf, tb)], mix_y[:, h, :],
                                        start=False, stop=(tb == HB - 1 and h == DB - 1))
                mm.then_inc(u_done.sem, u_done.up(at))

            def front_c(at, hf, kf):
                eng.wait_ge(c_ready.sem, c_ready.count(at, kf + 1))
                for tb in range(HB):
                    mm = eng.transpose(ps[:, 7, TH + tb * P:TH + (tb + 1) * P],
                                       c_norm[:, tb].rearrange("p n c -> p (n c)"), ident[:])
                mm.then_inc(c_rep.sem, c_rep.up(at))

            def back_d(at, hf):
                for tb in range(HB):
                    eng.matmul(half5[:, tb, :], ident[:], x_skip[:, hf * HB + tb, :],
                               start=(tb == 0), stop=False)
                    for h in range(DB):
                        eng.matmul(half5[:, tb, :], yT[:, h, tokens(hf, tb)], mix_yd[:, h, :],
                                   start=False, stop=False)

            def back_z(at, hf, kb):
                eng.wait_ge(ysc_copied.sem, ysc_copied.count(at, kb + 1))
                for tb in range(HB):
                    for h in range(DB):
                        mm = eng.matmul(half5[:, tb, h * P:(h + 1) * P],
                                        yscT[:, h, tb * P:(tb + 1) * P], ident[:], start=False,
                                        stop=(tb == HB - 1 and h == DB - 1))
                mm.then_inc(z_done.sem, z_done.up(at))

            def back_v(at, hf, kb):
                eng.wait_ge(v_done.sem, v_done.count(at, kb + 1))
                for h in range(DB):
                    for tb in range(HB):
                        mm = eng.transpose(ps[:, 5, h * TH + tb * P:h * TH + (tb + 1) * P],
                                           vn[:, tb, h * P:(h + 1) * P], ident[:])
                mm.then_inc(vt_done.sem, vt_done.up(at))

            def sum_states(at, ks, k):
                eng.wait_ge(prod_done.sem, prod_done.count(at, NG // 2 * ks + 2 * k + 2))
                for s in range(4 * k, 4 * k + 4):
                    g = ORDER[s]
                    q, r, h = (g // NR) % 4, g % NR, g // 16
                    mm = eng.matmul(ps[32 * q:32 * q + 32, 3, h * TH:(h + 1) * TH],
                                    w["sel"][:, r, :], prod[:, s % NPROD, :],
                                    start=(r == 0), stop=(r == NR - 1))
                mm.then_inc(nsummed.sem, nsummed.up(at))

            def scan_unit(at, hf, ks, filled, kb, kf):
                other = 1 - hf
                follows = kb is not None
                for p in range(NG // 2):
                    if p == 0:
                        eng.wait_ge(filled_a.sem, filled_a.count(at, filled))
                        eng.wait_ge(filled_v.sem, filled_v.count(at, filled))
                    if p >= 4 or follows:
                        eng.wait_ge(scanned.sem, scanned.count(at, NG * ks + 2 * (p - 4) + 2))
                    for s in (2 * p, 2 * p + 1):
                        for tb in range(HB):
                            c = (s % 2) * TH + tb * P
                            mm = eng.transpose(ps[:, RING[p % 4], c:c + P], group(hf, tb, ORDER[s]),
                                               ident[:])
                    mm.then_inc(in_turned.sem, in_turned.up(at))
                    if follows and p < LAG:
                        sum_states(at, ks - 1, NG // 4 - LAG + p)
                    if p == 5 and follows:
                        eng.wait_ge(ysc_copied.sem, ysc_copied.count(at, ks + 1))
                    if p >= 5 and p % 2 == 1:
                        sum_states(at, ks, (p - 5) // 2)
                    if p == PE_X and kf is not None:
                        front_x(at, other, kf)
                    if p == PE_Z and follows:
                        back_z(at, other, kb)
                    if p == PE_V and follows:
                        back_v(at, other, kb)
                    if p == (PE_Y if follows else 3) and kf is not None:
                        front_y(at, other, kf)
                    if p == (PE_C if follows else 6) and kf is not None:
                        front_c(at, other, kf)
                    if p == PE_D:
                        if kf is None:
                            eng.wait_ge(y_ready.sem, y_ready.count(at, 1))
                            for e in range(DB):
                                gate_y(0, e)
                        back_d(at, hf)
                    if kf is None and p == PE_D - 3:
                        gate_x()
                if kf is None:
                    for k in range(NG // 4 - LAG, NG // 4):
                        sum_states(at, ks, k)

            def gate_y(hf, e):
                for h in range(DB):
                    mm = eng.matmul(ps[:, 6 + e, hf * TH:(hf + 1) * TH],
                                    w["w_zy"][:, h, e * P:(e + 1) * P],
                                    yT[:, h, hf * TH:(hf + 1) * TH],
                                    start=False, stop=(hf == 1 and h == DB - 1))
                return mm

            def gate_x():
                for e in range(DB):
                    eng.matmul(bank(6 + e), w["w_in"][:, DI + e * P:DI + (e + 1) * P], xnT[:],
                               start=True, stop=False)

            def ssm_output(at):
                eng.wait_ge(y_ready.sem, y_ready.count(at, 2))
                for e in range(DB):
                    gate_y(1, e).then_inc(z2_done.sem, z2_done.up(at))
                for h in range(DB):
                    eng.wait_ge(gy_done.sem, gy_done.count(at, h + 1))
                    for tb in range(TB):
                        mm = eng.matmul(blocks(2)[:, tb, :], gy[:, h, tb * P:(tb + 1) * P],
                                        w["w_out"][:, h, :], start=(tb == 0 and h == 0),
                                        stop=(tb == TB - 1 and h == DB - 1))
                mm.then_inc(o2_done.sem, o2_done.up(at))

            eng.wait_ge(stored.sem, 16)
            eng.wait_ge(loaded, 16 * n_loads)
            eng.wait_ge(prepared, 1)
            begin_with(start, len(PE_START))
            with eng.Fori(0, B) as b:
                at = Place(b, 0)
                attention(at)
                mixture(at)
                ssm_inputs(at)
                scan_unit(at, 0, 0, 1, None, 1)
                with eng.Fori(0, ITERS) as i:
                    turn = Place(b, 1, i)
                    scan_unit(turn, 1, 0, 0, 0, 0)
                    scan_unit(turn, 0, 1, 1, 1, 1)
                at = Place(b, 2)
                scan_unit(at, 1, 0, 0, 0, None)
                back_z(at, 1, 1)
                back_v(at, 1, 1)
                ssm_output(at)
                mixture(at, Place(b + 1, 0))

        @block.scalar
        def _(eng):
            def root(at, n):
                eng.wait_ge(n.var.sem, n.var.count(at, 1))
                eng.activation(std[:], meanvar[:, :, 1], ACT.Sqrt, bias=eps[:]
                    ).then_inc(n.std.sem, n.std.up(at))

            def copy_turned(at, n, dst, src):
                eng.wait_ge(n.turned.sem, n.turned.count(at, 1))
                eng.activation(dst, src, ACT.Copy).then_inc(n.xnT.sem, n.xnT.up(at))

            def start(at, step):
                if step == 0:
                    root(at, n_att)
                if step == 1:
                    copy_turned(at, n_att, xnT_next, bank(5))
                if step >= 2:
                    part = step - 2
                    eng.wait_ge(part_done.sem, part_done.count(at, part + 1))
                    s = PARTS * part
                    eng.activation(qk_slots[:, 0, :, s + 1:s + 3, :],
                                   qk_slots[:, 0, :, s:s + 1, :].broadcast_to([P, TB * NH, 2, HD]),
                                   ACT.Copy).then_inc(repeated_a.sem, repeated_a.up(at))

            def attention(at):
                def copy_head(h):
                    eng.wait_ge(qk_turned.sem, qk_turned.count(at, h + 1))
                    if h == 0:
                        eng.wait_ge(heads_zero.sem, heads_zero.count(at, 1))
                    if h >= QUAD:
                        eng.wait_ge(rescored.sem, rescored.count(at, TB * (h - QUAD + 1)))
                    eng.activation(heads[0:QR, h % QUAD], turned, ACT.Copy
                                   ).then_inc(qk_copied.sem, qk_copied.up(at))

                def copy_max(h):
                    eng.wait_ge(max_turned.sem, max_turned.count(at, h + 1))
                    eng.activation(heads[BIAS:BIAS + 2, h % QUAD, 0], ps[BIAS:BIAS + 2, 6, :],
                                   ACT.Copy).then_inc(max_copied.sem, max_copied.up(at))

                def exp(h, kb):
                    eng.wait_ge(rescored.sem, rescored.count(at, TB * h + kb + 1))
                    if h >= HG and h % HG == 0:
                        eng.wait_ge(weighed.sem, weighed.count(at, h - HG + kb + 1))
                    eng.activation(probsT[:, h % HG, kb, :], bank(3 + (TB * h + kb) % 2), ACT.Exp,
                                   scale=SCALE).then_inc(exped.sem, exped.up(at))

                def copy_out(c):
                    eng.wait_ge(weighed.sem, weighed.count(at, TB * (c + 1)))
                    eng.activation(oT, bank(7), ACT.Copy).then_inc(o_copied.sem, o_copied.up(at))

                copy_head(0)
                copy_head(1)
                for h in range(NH + AHEAD + 2):
                    behind = h - AHEAD
                    for b in range(TB):
                        if b == MAX_AT and 1 <= h <= NH and h % 2 == 0:
                            copy_max(h - 1)
                        if 0 <= behind < NH:
                            exp(behind, b)
                    if behind >= HG and behind % HG == 0:
                        copy_out(behind // HG - 1)
                    if h + 2 < NH:
                        copy_head(h + 2)
                eng.wait_ge(a_turned.sem, a_turned.count(at, 1))
                eng.activation(attnT, bank(7), ACT.Copy).then_inc(a_copied.sem, a_copied.up(at))

            def mixture(at, coming=None):
                root(at, n_moe)
                copy_turned(at, n_moe, xnT[:], bank(4))
                eng.wait_ge(r_shift.sem, r_shift.count(at, 1))
                eng.activation(rt[:, 1], rt[:, 0], ACT.Exp).then_inc(r_exp.sem, r_exp.up(at))

                def silu(u):
                    e, f = divmod(u, FB)
                    eng.wait_ge(gated.sem, gated.count(at, u + 1))
                    if u >= 2:
                        eng.wait_ge(hidden.sem, hidden.count(at, u - 1))
                    eng.activation(gs[:, u % 2, :], bank(u % 2), ACT.Silu,
                                                 bias=w["gate_b"][:, e, f:f + 1]
                                                     ).then_inc(silued.sem, silued.up(at))

                for u in range(4):
                    silu(u)
                eng.wait_ge(c_turned.sem, c_turned.count(at, 1))
                eng.activation(cT[:], ps[0:NE, 5, :], ACT.Copy
                    ).then_inc(comb_copied.sem, comb_copied.up(at))
                for u in range(4, NE * FB):
                    silu(u)
                    if coming is not None and u in ACT_START:
                        start(coming, ACT_START.index(u))
                if coming is not None:
                    for step in range(len(ACT_START), 2 + PARTS):
                        start(coming, step)

            def ssm_inputs(at):
                root(at, n_ssm)
                copy_turned(at, n_ssm, xnT[:], bank(4))
                for h in range(DB):
                    eng.wait_ge(xT_done.sem, xT_done.count(at, h + 1))
                    eng.activation(xT[:, h, :], bank(5 + h), ACT.Copy
                        ).then_inc(xT_copied.sem, xT_copied.up(at))
                eng.wait_ge(dt_done.sem, dt_done.count(at, 1))
                eng.activation(dtlow[0:DR, :], ps[0:DR, 4, :], ACT.Copy
                    ).then_inc(dt_copied.sem, dt_copied.up(at))
                eng.wait_ge(dl_done.sem, dl_done.count(at, 1))
                eng.activation(sp[1], ps[:, 5:7, :].rearrange("p h t -> p (h t)"), ACT.Abs
                               ).then_inc(dl_abs.sem, dl_abs.up(at))
                eng.wait_ge(dl_abs.sem, dl_abs.count(at, 1))
                eng.activation(sp[1], sp[1], ACT.Exp, scale=-1.0).then_inc(dl_exp.sem, dl_exp.up(at))
                eng.wait_ge(dl_exp.sem, dl_exp.count(at, 1))
                eng.activation(sp[3], sp[1], ACT.Ln, bias=one[:]).then_inc(dl_ln.sem, dl_ln.up(at))
                eng.wait_ge(xmix_done.sem, xmix_done.count(at, 1))
                eng.activation(x_bc[:].rearrange("p b c -> p (b c)"), ps[:, 7, 0:P], ACT.Copy)
                eng.activation(x_mixed[:].rearrange("p b c -> p (b c)"),
                               ps[:, 0:2, :].rearrange("p k c -> p (k c)"), ACT.Copy
                               ).then_inc(x_mixed_a.sem, x_mixed_a.up(at))
                front_root(at, 0, 0)
                for g in range(NG):
                    eng.wait_ge(dl_rep.sem, dl_rep.count(at, g + 1))
                    eng.activation(da[:, g, :], bank(RING[g % 4]), ACT.Exp,
                                   scale=decay[:, g:g + 1]).then_inc(da_ready.sem, da_ready.up(at))
                    if g == FIRST_C + 4:
                        front_c(at, 0, 0)

            def front_root(at, hf, kf):
                eng.wait_ge(ss_done.sem, ss_done.count(at, kf + 1))
                eng.activation(nrm[:], ss[:], ACT.Sqrt).then_inc(nrm_done.sem, nrm_done.up(at))

            def front_c(at, hf, kf):
                eng.wait_ge(c_rep.sem, c_rep.count(at, kf + 1))
                eng.activation(crep[:, hf, :], ps[:, 7, TH:T], ACT.Copy
                    ).then_inc(c_copied.sem, c_copied.up(at))

            def fill(at, hf, kf):
                eng.wait_ge(du_done.sem, du_done.count(at, kf + 1))
                eng.wait_ge(b_ready.sem, b_ready.count(at, kf + 1))
                for n in range(NS):
                    ins = eng.activation(scan_in[:, hf, 0, :, n, :], du_groups(0), ACT.Copy,
                                         scale=b_norm[:, 0, n:n + 1])
                for n in range(NS - ACT_FILL, NS):
                    ins = eng.activation(scan_in[:, hf, 1, :, n, :], du_groups(1), ACT.Copy,
                                         scale=b_norm[:, 1, n:n + 1])
                ins.then_inc(filled_a.sem, filled_a.up(at))

            def front(at, hf, kf):
                front_root(at, hf, kf)
                front_c(at, hf, kf)
                fill(at, hf, kf)

            def back(at, hf, kb, last):
                cols = slice(hf * TH + 1, (hf + 1) * TH + 1)
                if not last:
                    for h in range(DB):
                        ins = eng.activation(ytmp[:, h, :], yT[:, h, cols], ACT.Identity,
                                             bias=beta_s[:, h:h + 1], scale=1.0 - STEP)
                    ins.then_inc(ytmp_done.sem, ytmp_done.up(at))
                eng.wait_ge(nsummed.sem, nsummed.count(at, LAG + NG // 4 * kb))
                eng.activation(yscT[:].rearrange("p h t -> p (h t)"), bank(3),
                                                 ACT.Copy).then_inc(ysc_copied.sem, ysc_copied.up(at))
                eng.wait_ge(zvar.sem, zvar.count(at, kb + 1))
                eng.activation(std[:, 0:HB], meanvar[:, 0:HB, 1], ACT.Sqrt, bias=eps[:]
                    ).then_inc(zstd.sem, zstd.up(at))
                eng.wait_ge(znmr.sem, znmr.count(at, kb + 1))
                for tb in range(HB):
                    ins = eng.activation(vn[:, tb, :], half5[:, tb, :], ACT.Identity,
                                         bias=nmr[:, tb:tb + 1], scale=rstd[:, tb:tb + 1])
                ins.then_inc(v_done.sem, v_done.up(at))
                if last:
                    eng.wait_ge(vt_done.sem, vt_done.count(at, kb + 1))
                    for h in range(DB):
                        ins = eng.activation(yT[:, h, cols], ps[:, 5, h * TH:(h + 1) * TH], ACT.Identity,
                                             bias=w["beta"][:, h:h + 1], scale=w["gamma"][:, h:h + 1])
                    ins.then_inc(y_ready.sem, y_ready.up(at))

            def ssm_output(at):
                for e in range(DB):
                    eng.wait_ge(z2_done.sem, z2_done.count(at, e + 1))
                    eng.activation(gz[:, e, :], bank(6 + e), ACT.Silu
                                   ).then_inc(z2_silu.sem, z2_silu.up(at))

            eng.wait_ge(loaded, 16 * n_loads)
            eng.activation(decay[:], w["a_log"][:], ACT.Exp).then_inc(prep_a, 1)
            eng.wait_ge(prepared, 1)
            begin_with(start, 2 + PARTS)
            with eng.Fori(0, B) as b:
                at = Place(b, 0)
                attention(at)
                mixture(at)
                ssm_inputs(at)
                front(at, 1, 1)
                with eng.Fori(0, ITERS) as i:
                    turn = Place(b, 1, i)
                    for hf in range(2):
                        back(turn, hf, hf, False)
                        front(turn, hf, hf)
                at = Place(b, 2)
                back(at, 0, 0, True)
                back(at, 1, 1, True)
                ssm_output(at)
                mixture(at, Place(b + 1, 0))

        @block.vector
        def _(eng):
            def hold(eng):
                holds.append(len(holds))
                eng.memset(held[:, holds[-1]:holds[-1] + 1], 0.0)

            holds = []

            def moments(at, src, done, nb=TB, vchain=vchain):
                for tb in range(nb):
                    ins = eng.bn_stats(stats[:, tb, :], src[:, tb, :])
                ins.then_inc(vchain.sem, vchain.up(at))
                eng.wait_ge(vchain.sem, vchain.last(at))
                hold(eng)
                for tb in range(nb):
                    ins = eng.bn_aggr(meanvar[:, tb, :], stats[:, tb, :])
                ins.then_inc(done.sem, done.up(at))

            def norm(at, n, src):
                moments(at, src, n.var)
                scale(at, n, src, vchain)

            def scale(at, n, src, chain):
                eng.wait_ge(n.std.sem, n.std.count(at, 1))
                eng.reciprocal(rstd[:], std[:]).then_inc(chain.sem, chain.up(at))
                eng.wait_ge(chain.sem, chain.last(at))
                for tb in range(TB):
                    eng.tensor_scalar(xn[:, tb, :], src[:, tb, :], meanvar[:, tb, 0:1],
                                      rstd[:, tb:tb + 1], ALU.subtract, ALU.mult
                                      ).then_inc(n.xn.sem, n.xn.up(at))

            def start(at, step):
                if step == 0:
                    eng.wait_ge(x_loaded.sem, x_loaded.count(at, 1))
                    moments(at, x_in, n_att.var, TB, nchain)
                    eng.memset(vaug_flat, 0.0).then_inc(v_zero.sem, v_zero.up(at))
                if step == 1:
                    scale(at, n_att, x_in, nchain)
                if step == 2:
                    eng.tensor_tensor(x_res[:], x_in[:],
                                      w["out_b"][:].rearrange("p (o c) -> p o c", o=1).broadcast_to([P, TB, DM]),
                                      ALU.add)
                    eng.memset(smax[:], 0.0).then_inc(x_free.sem, x_free.up(at))
                    eng.memset(heads_flat[64:BIAS], 0.0)
                    eng.memset(heads[BIAS:BIAS + 2, :, 1], -1.0
                        ).then_inc(heads_zero.sem, heads_zero.up(at))
                if step in (3, 4):
                    k = step - 3
                    eng.wait_ge(qkv_done.sem, qkv_done.count(at, k + 1))
                    eng.tensor_tensor(
                        qkv[:, 2 * k:2 * k + 2], ps[:, 4:6, 0:3 * DM],
                        w["qkv_b"][:].rearrange("p (o c) -> p o c", o=1).broadcast_to([P, 2, 3 * DM]),
                        ALU.add).then_inc(qkv_taken.sem, qkv_taken.up(at))
                if step == 5:
                    eng.wait_ge(qkv_taken.sem, qkv_taken.count(at, 2))
                    qk = qkv[:, :, 0:2 * DM].rearrange("p b (h j two) -> p two b h j", two=2, j=4)
                    even, odd = qk[:, 0], qk[:, 1]
                    r = rot.rearrange("p b (h two j) -> p two b h j", two=2, j=4)
                    ta = rtmp[:, 0].rearrange("p b (h j) -> p b h j", j=4)
                    tc = rtmp[:, 1].rearrange("p b (h j) -> p b h j", j=4)
                    angles = [w[n][:].rearrange("p b (o j) -> p b o j", o=1).broadcast_to([P, TB, 2 * NH, 4])
                              for n in ("cosine", "sine")]
                    for half, (first, second, op) in enumerate(((even, odd, ALU.subtract), (odd, even, ALU.add))):
                        eng.tensor_tensor(ta, first, angles[0], ALU.mult)
                        eng.tensor_tensor(tc, second, angles[1], ALU.mult
                            ).then_inc(nchain.sem, nchain.up(at))
                        eng.wait_ge(nchain.sem, nchain.last(at))
                        ins = eng.tensor_tensor(r[:, half], ta, tc, op)
                        if half == 0:
                            ins.then_inc(nchain.sem, nchain.up(at))
                            eng.wait_ge(nchain.sem, nchain.last(at))
                    ins.then_inc(rot_done.sem, rot_done.up(at))
                first = [qk_slots[:, :, :, PARTS * n, :] for n in range(PARTS)]
                full = rot.rearrange("p b (k h c) -> p k b h c", k=2, c=HD)
                rest = left.rearrange("p (k n c) -> p k n c", k=2, c=HD)
                if step == 6:
                    eng.wait_ge(rot_done.sem, rot_done.count(at, 1))
                    eng.tensor_copy(slots[:, :, :, :, 0, :], full
                        ).then_inc(part_done.sem, part_done.up(at))
                    eng.wait_ge(part_done.sem, part_done.count(at, 1))
                    eng.tensor_tensor(left.rearrange("p (k b h c) -> p k b h c", k=2, b=TB, c=HD), full,
                                      slots[:, :, :, :, 0, :], ALU.subtract
                                          ).then_inc(nchain.sem, nchain.up(at))
                    eng.wait_ge(nchain.sem, nchain.last(at))
                if step == 7:
                    eng.tensor_copy(first[1], rest).then_inc(part_done.sem, part_done.up(at))
                    eng.wait_ge(part_done.sem, part_done.count(at, 2))
                    eng.tensor_tensor(first[2], rest, first[1], ALU.subtract
                        ).then_inc(part_done.sem, part_done.up(at))
                if step == 8:
                    for part, (low, high) in enumerate(K_SLOTS):
                        if part == PARTS - 1:
                            eng.wait_ge(part_done.sem, part_done.count(at, PARTS))
                        ins = eng.tensor_copy(
                            qk_slots[:, 1, :, low:high + 1:high - low, :],
                            qk_slots[:, 1, :, PARTS * part:PARTS * part + 1, :].broadcast_to([P, TB * NH, 2, HD]))
                    ins.then_inc(repeated_v.sem, repeated_v.up(at))
                if step == 9:
                    eng.wait_ge(v_zero.sem, v_zero.count(at, 1))
                    eng.memset(vaug[:, :, :, HD:HD + 1], 1.0).then_inc(nchain.sem, nchain.up(at))
                    eng.wait_ge(nchain.sem, nchain.last(at))
                    eng.tensor_copy(
                        vaug[:, :, :, 0:HD], qkv[:, :, 2 * DM:].rearrange("p b (h c) -> p b h c", c=HD)
                            ).then_inc(v_ready.sem, v_ready.up(at))

            def attention(at):
                def rowmax(h, qb):
                    u = TB * h + qb
                    eng.wait_ge(scored.sem, scored.count(at, u + 1))
                    eng.tensor_reduce(smax[:, h % 2, qb:qb + 1], bank(u % 3), AX, ALU.max
                                      ).then_inc(maxed.sem, maxed.up(at))

                def split_max(h):
                    eng.wait_ge(maxed.sem, maxed.count(at, TB * (h + 1)))
                    high = smax_b[:, h % 2, :, 0]
                    eng.tensor_copy(high, smax[:, h % 2, :]).then_inc(vchain.sem, vchain.up(at))
                    eng.wait_ge(vchain.sem, vchain.last(at))
                    eng.tensor_tensor(smax_b[:, h % 2, :, 1], smax[:, h % 2, :], high, ALU.subtract
                                      ).then_inc(max_parts.sem, max_parts.up(at))

                def copy_max(h):
                    eng.wait_ge(max_turned.sem, max_turned.count(at, h + 1))
                    eng.tensor_copy(heads[BIAS:BIAS + 2, h % QUAD, 0], ps[BIAS:BIAS + 2, 6, :]
                                    ).then_inc(max_copied.sem, max_copied.up(at))

                def normalise(c):
                    eng.wait_ge(o_turned.sem, o_turned.count(at, c + 1))
                    o = blocks(7).rearrange("p b (j r) -> p b j r", r=32)
                    eng.reciprocal(rsum[:], o[:, :, :, HD]).then_inc(vchain.sem, vchain.up(at))
                    eng.wait_ge(vchain.sem, vchain.last(at))
                    dst = attn[:, :, c * HG * HD:(c + 1) * HG * HD].rearrange("p b (j r) -> p b j r", r=HD)
                    eng.tensor_tensor(
                        dst, o[:, :, :, 0:HD],
                        rsum[:].rearrange("p b (j o) -> p b j o", o=1).broadcast_to([P, TB, HG, HD]),
                        ALU.mult).then_inc(o_normed.sem, o_normed.up(at))

                for h in range(NH + AHEAD + 2):
                    behind = h - AHEAD
                    for qb in range(TB):
                        if qb == MAX_AT and 1 <= h <= NH and h % 2 == 1:
                            copy_max(h - 1)
                        if h < NH:
                            rowmax(h, qb)
                    if h < NH:
                        split_max(h)
                    if behind > HG and behind % HG == 1:
                        normalise(behind // HG - 1)
                eng.wait_ge(projected.sem, projected.count(at, 1))
                eng.tensor_tensor(x_res[:], blocks(6), x_res[:], ALU.add
                    ).then_inc(x1_ready.sem, x1_ready.up(at))

            def mixture(at, dst, ready, coming=None):
                norm(at, n_moe, x_res)
                eng.wait_ge(routed.sem, routed.count(at, 1))
                logits = ps[:, 5, 0:TB * NE].rearrange("p (b e) -> p b e", b=TB)
                per_token = lambda v: v.rearrange("p (b o) -> p b o", o=1).broadcast_to([P, TB, NE])
                eng.tensor_reduce(rs[:, 0], logits, AX, ALU.max).then_inc(vchain.sem, vchain.up(at))
                eng.wait_ge(vchain.sem, vchain.last(at))
                eng.tensor_tensor(rt[:, 0], logits, per_token(rs[:, 0]), ALU.subtract
                    ).then_inc(r_shift.sem, r_shift.up(at))
                eng.wait_ge(r_exp.sem, r_exp.count(at, 1))
                eng.tensor_reduce(rs[:, 1], rt[:, 1], AX, ALU.add).then_inc(vchain.sem, vchain.up(at))
                eng.wait_ge(vchain.sem, vchain.last(at))
                eng.reciprocal(rs[:, 2], rs[:, 1]).then_inc(vchain.sem, vchain.up(at))
                eng.wait_ge(vchain.sem, vchain.last(at))
                eng.tensor_tensor(rt[:, 2], rt[:, 1], per_token(rs[:, 2]), ALU.mult
                    ).then_inc(vchain.sem, vchain.up(at))
                eng.wait_ge(vchain.sem, vchain.last(at))
                hold(eng)
                for tb in range(TB):
                    ins = eng.max(top[:, tb, :], rt[:, 2, tb, :])
                ins.then_inc(vchain.sem, vchain.up(at))
                eng.wait_ge(vchain.sem, vchain.last(at))
                hold(eng)
                for tb in range(TB):
                    ins = eng.max_index(topi[:, tb, :], top[:, tb, :], rt[:, 2, tb, :])
                ins.then_inc(vchain.sem, vchain.up(at))
                eng.wait_ge(vchain.sem, vchain.last(at))
                eng.tensor_copy(topf[:], topi[:]).then_inc(vchain.sem, vchain.up(at))
                eng.wait_ge(vchain.sem, vchain.last(at))
                numbers = w["experts"][:].rearrange("p (o e) -> p o e", o=1).broadcast_to([P, TB, NE])
                eng.tensor_tensor(rt[:, 3], numbers, topf[:, :, 0:1].broadcast_to([P, TB, NE]), ALU.is_equal)
                eng.tensor_tensor(
                    rt[:, 4], numbers, topf[:, :, 1:2].broadcast_to([P, TB, NE]), ALU.is_equal
                        ).then_inc(vchain.sem, vchain.up(at))
                eng.wait_ge(vchain.sem, vchain.last(at))
                eng.tensor_tensor(rt[:, 5], rt[:, 3], rt[:, 4], ALU.add
                    ).then_inc(vchain.sem, vchain.up(at))
                eng.wait_ge(vchain.sem, vchain.last(at))
                eng.tensor_tensor(rt[:, 6], rt[:, 5], rt[:, 2], ALU.mult
                    ).then_inc(vchain.sem, vchain.up(at))
                eng.wait_ge(vchain.sem, vchain.last(at))
                eng.tensor_reduce(rs[:, 3], rt[:, 6], AX, ALU.add).then_inc(vchain.sem, vchain.up(at))
                eng.wait_ge(vchain.sem, vchain.last(at))
                eng.tensor_scalar(rs[:, 1], rs[:, 3], 1e-9, None, ALU.add
                    ).then_inc(vchain.sem, vchain.up(at))
                eng.wait_ge(vchain.sem, vchain.last(at))
                eng.reciprocal(rs[:, 2], rs[:, 1]).then_inc(vchain.sem, vchain.up(at))
                eng.wait_ge(vchain.sem, vchain.last(at))
                eng.tensor_tensor(rt[:, 7], rt[:, 6], per_token(rs[:, 2]), ALU.mult
                    ).then_inc(r_comb.sem, r_comb.up(at))

                def hide(u):
                    e, f = divmod(u, FB)
                    eng.wait_ge(upped.sem, upped.count(at, u + 1))
                    eng.wait_ge(silued.sem, silued.count(at, u + 1))
                    if e >= 2 and f == 0:
                        eng.wait_ge(downed.sem, downed.count(at, e - 1))
                    eng.scalar_tensor_tensor(
                        out=hid[:, e % 2, f, :], in0=bank(2 + u % 2), scalar=w["up_b"][:, e, f:f + 1],
                        in1=gs[:, u % 2, :], op0=ALU.add, op1=ALU.mult
                            ).then_inc(hidden.sem, hidden.up(at))

                def add_expert(e):
                    eng.wait_ge(downed.sem, downed.count(at, e + 1))
                    to = dst if e == NE - 1 else acc
                    for tb in range(TB):
                        ins = eng.scalar_tensor_tensor(
                            out=to[:, tb, :], in0=blocks(6 + e % 2)[:, tb, :],
                            scalar=rt[:, 7, tb, e:e + 1], in1=acc[:, tb, :], op0=ALU.mult, op1=ALU.add)
                    ins.then_inc(summed.sem, summed.up(at))
                    if e == NE - 1:
                        return ins
                    eng.wait_ge(summed.sem, summed.count(at, e + 1))

                for u in range(4):
                    hide(u)
                eng.wait_ge(biased.sem, biased.count(at, 1))
                eng.tensor_tensor(acc, blocks(4), x_res[:], ALU.add).then_inc(vchain.sem, vchain.up(at))
                eng.wait_ge(vchain.sem, vchain.last(at))
                if coming is not None:
                    start(coming, 0)
                for e in range(NE):
                    if e == NE - 1 and ready is not None:
                        eng.wait_ge(stored.sem, stored.count(at, 1))
                    add_expert(e)
                    if e < NE - 2:
                        hide(2 * e + 4)
                        hide(2 * e + 5)
                    if coming is not None:
                        for step in DVE_START[e]:
                            start(coming, step)
                eng.wait_ge(summed.sem, summed.count(at, NE))
                if ready is not None:
                    eng.memset(rs[:, 0], 0.0).then_inc(ready.sem, ready.up(at))

            def ssm_inputs(at):
                norm(at, n_ssm, x_res)
                eng.memset(yT[:], 0.0).then_inc(y_ready.sem, y_ready.up(at))
                eng.wait_ge(dl_abs.sem, dl_abs.count(at, 1))
                eng.tensor_scalar(sp[0], ps[:, 5:7, :].rearrange("p h t -> p (h t)"), 0.0, None, ALU.max
                                  ).then_inc(dl_relu.sem, dl_relu.up(at))
                eng.wait_ge(dl_exp.sem, dl_exp.count(at, 1))
                eng.tensor_scalar(sp[2], sp[1], 1.0, None, ALU.add)
                flat = delta[:].rearrange("p b c -> p (b c)")
                eng.tensor_scalar(flat, sp[1], -0.5, 1.0, ALU.mult, ALU.add
                                  ).then_inc(vchain.sem, vchain.up(at))
                eng.wait_ge(vchain.sem, vchain.last(at))
                eng.scalar_tensor_tensor(out=sp[2], in0=sp[2], scalar=-1.0, in1=sp[1],
                                         op0=ALU.add, op1=ALU.subtract
                                             ).then_inc(vchain.sem, vchain.up(at))
                eng.wait_ge(vchain.sem, vchain.last(at))
                eng.tensor_tensor(sp[2], sp[2], flat, ALU.mult).then_inc(vchain.sem, vchain.up(at))
                eng.wait_ge(vchain.sem, vchain.last(at))
                eng.tensor_tensor(sp[2], sp[0], sp[2], ALU.subtract).then_inc(vchain.sem, vchain.up(at))
                eng.wait_ge(vchain.sem, vchain.last(at))
                eng.wait_ge(dl_ln.sem, dl_ln.count(at, 1))
                eng.tensor_tensor(flat, sp[2], sp[3], ALU.add).then_inc(dl_ready.sem, dl_ready.up(at))
                eng.wait_ge(dl_ready.sem, dl_ready.count(at, 1))
                for e in range(EXPAND):
                    eng.tensor_copy(chunk(e), repeated(e)).then_inc(expanded.sem, expanded.up(at))
                    if e == 0:
                        front_bc(at, 0, 0)
                front_norm(at, 0, 0)
                front_du(at, 0, 0)
                for e in range(EXPAND):
                    eng.wait_ge(dl_rep.sem, dl_rep.count(at, ge * (e + 1)))
                    if e == 0:
                        eng.wait_ge(du_done.sem, du_done.count(at, 1))
                        eng.wait_ge(b_ready.sem, b_ready.count(at, 1))
                    for tb in range(HB):
                        ins = eng.tensor_tensor(
                            scan_in[:, 0, tb, ge * e:ge * (e + 1)],
                            du[:, tb, ge * GC * e:ge * GC * (e + 1)].rearrange(
                                "p (g o c) -> p g o c", o=1, c=GC).broadcast_to([P, ge, NS, GC]),
                            b_norm[:, tb, :].rearrange("p (o n q) -> p o n q", o=1, q=1
                                                       ).broadcast_to([P, ge, NS, GC]), ALU.mult)
                    if e >= EXPAND - 2:
                        filled = (filled_a, filled_v)[e % 2]
                        ins.then_inc(filled.sem, filled.up(at))
                eng.wait_ge(x_mixed_a.sem, x_mixed_a.count(at, 1))
                eng.tensor_tensor(x_skip[:], x_mixed[:],
                                  w["skip"][:].rearrange("p (o c) -> p o c", o=1).broadcast_to([P, TB, DI]),
                                  ALU.mult).then_inc(vchain.sem, vchain.up(at))

            def front_bc(at, hf, kf):
                eng.wait_ge(bc_done.sem, bc_done.count(at, kf + 1))
                eng.tensor_copy(bcs[:].rearrange("p b k n -> p (b k n)"),
                                                 ps[:, 7, 0:HB * 2 * NS]
                                                     ).then_inc(vchain.sem, vchain.up(at))
                eng.wait_ge(vchain.sem, vchain.last(at))
                eng.tensor_tensor(bcq[:], bcs[:], bcs[:], ALU.mult).then_inc(vchain.sem, vchain.up(at))
                eng.wait_ge(vchain.sem, vchain.last(at))
                eng.tensor_reduce(ss[:], bcq[:].rearrange("p b k n -> p (b k) n"),
                                                 AX, ALU.add).then_inc(ss_done.sem, ss_done.up(at))

            def front_norm(at, hf, kf):
                eng.wait_ge(nrm_done.sem, nrm_done.count(at, kf + 1))
                eng.tensor_scalar(rn[:], nrm[:], EPS, None, ALU.max).then_inc(vchain.sem, vchain.up(at))
                eng.wait_ge(vchain.sem, vchain.last(at))
                eng.reciprocal(rn[:], rn[:]).then_inc(vchain.sem, vchain.up(at))
                eng.wait_ge(vchain.sem, vchain.last(at))
                r = rn[:].rearrange("p (b k) -> p k b", k=2)
                eng.tensor_tensor(
                    c_norm[:], bcs[:, :, 1, :].rearrange("p b (n o) -> p b n o", o=1).broadcast_to([P, HB, NS, GC]),
                    r[:, 1].rearrange("p (b o q) -> p b o q", o=1, q=1).broadcast_to([P, HB, NS, GC]),
                    ALU.mult).then_inc(c_ready.sem, c_ready.up(at))
                eng.tensor_tensor(
                    b_norm[:], bcs[:, :, 0, :],
                    r[:, 0].rearrange("p (b o) -> p b o", o=1).broadcast_to([P, HB, NS]), ALU.mult
                        ).then_inc(b_ready.sem, b_ready.up(at))

            def front_du(at, hf, kf):
                eng.wait_ge(u_done.sem, u_done.count(at, kf + 1))
                eng.tensor_tensor(du[:], half6, delta[:, hf * HB:(hf + 1) * HB, :],
                                                 ALU.mult).then_inc(du_done.sem, du_done.up(at))

            def fill(at, hf, kf, ns):
                if ns[0] == 0:
                    eng.wait_ge(du_done.sem, du_done.count(at, kf + 1))
                    eng.wait_ge(b_ready.sem, b_ready.count(at, kf + 1))
                for n in ns:
                    ins = eng.tensor_scalar(scan_in[:, hf, 1, :, n, :], du_groups(1),
                                            b_norm[:, 1, n:n + 1], None, ALU.mult)
                if ns[-1] == NS - ACT_FILL - 1:
                    ins.then_inc(filled_v.sem, filled_v.up(at))

            def back_var(at, hf, kb):
                eng.wait_ge(z_done.sem, z_done.count(at, kb + 1))
                moments(at, half5, zvar, HB)

            def back_norm(at, hf, kb):
                eng.wait_ge(zstd.sem, zstd.count(at, kb + 1))
                eng.reciprocal(rstd[:, 0:HB], std[:, 0:HB]).then_inc(vchain.sem, vchain.up(at))
                eng.wait_ge(vchain.sem, vchain.last(at))
                eng.scalar_tensor_tensor(
                    out=nmr[:, 0:HB], in0=meanvar[:, 0:HB, 0], scalar=-1.0, in1=rstd[:, 0:HB],
                    op0=ALU.mult, op1=ALU.mult).then_inc(znmr.sem, znmr.up(at))

            def back_y(at, hf, kb):
                eng.wait_ge(vt_done.sem, vt_done.count(at, kb + 1))
                eng.wait_ge(ytmp_done.sem, ytmp_done.count(at, kb + 1))
                for h in range(DB):
                    ins = eng.scalar_tensor_tensor(
                        out=yT[:, h, hf * TH + 1:(hf + 1) * TH + 1], in0=ps[:, 5, h * TH:(h + 1) * TH],
                        scalar=gamma_s[:, h:h + 1], in1=ytmp[:, h, :], op0=ALU.mult, op1=ALU.add)
                ins.then_inc(y_ready.sem, y_ready.up(at))

            def scan_unit(at, hf, ks, kb, kf):
                other = 1 - hf
                follows = kb is not None
                for s in range(NG):
                    if s % 2 == 0:
                        eng.wait_ge(in_turned.sem, in_turned.count(at, NG // 2 * ks + s // 2 + 1))
                        if s >= NHID or follows:
                            eng.wait_ge(prod_done.sem, prod_done.count(at, NG // 2 * ks + (s - NHID) // 2 + 1))
                    eng.tensor_tensor_scan(
                        hst[:, s % NHID, :], da[:, ORDER[s], hf * TH:(hf + 1) * TH],
                        ps[:, RING[s // 2 % 4], (s % 2) * TH:(s % 2 + 1) * TH],
                        0.0 if hf == 0 else hend[:, s:s + 1], ALU.mult, ALU.add
                    ).then_inc(scanned.sem, scanned.up(at))
                    if hf == 0 and s % NHID == NHID - 1:
                        eng.wait_ge(scanned.sem, scanned.count(at, NG * ks + s + 1))
                        eng.tensor_copy(hend[:, s - NHID + 1:s + 1], hst[:, :, TH - 1]
                                        ).then_inc(vchain.sem, vchain.up(at))
                        eng.wait_ge(vchain.sem, vchain.last(at))
                    if follows:
                        if s == DVE_VAR:
                            back_var(at, other, kb)
                        if s == DVE_NORM:
                            back_norm(at, other, kb)
                        if s == DVE_Y and kf is not None:
                            back_y(at, other, kb)
                    if kf is not None:
                        if s == (DVE_BC if follows else 8):
                            front_bc(at, other, kf)
                        if s == (DVE_BCN if follows else 11):
                            front_norm(at, other, kf)
                        if s == (DVE_DU if follows else 14):
                            front_du(at, other, kf)
                        n = 2 * (s - DVE_FILL)
                        if 0 <= n < NS - ACT_FILL:
                            fill(at, other, kf, (n, n + 1))

            def ssm_output(at):
                for e in range(DB):
                    eng.wait_ge(z2_silu.sem, z2_silu.count(at, e + 1))
                    eng.tensor_tensor(gy[:, e, :], gz[:, e, :], yT[:, e, 1:T + 1], ALU.mult
                                      ).then_inc(gy_done.sem, gy_done.up(at))
                eng.wait_ge(o2_done.sem, o2_done.count(at, 1))
                eng.tensor_tensor(x_res[:], blocks(2), x_res[:], ALU.add
                    ).then_inc(x3_ready.sem, x3_ready.up(at))
                eng.wait_ge(x3_ready.sem, x3_ready.count(at, 1))

            eng.memset(eps[:], EPS)
            eng.memset(one[:], 1.0)
            eng.memset(dtlow[:], 1.0)
            eng.wait_ge(loaded, 16 * n_loads)
            eng.tensor_scalar(gamma_s[:], w["gamma"][:], STEP, None, ALU.mult)
            eng.tensor_scalar(beta_s[:], w["beta"][:], STEP, None, ALU.mult)
            eng.tensor_copy(ident_b[:], ident[:])
            eng.wait_ge(prep_a, 1)
            eng.tensor_scalar(decay[:], decay[:], -1.0, None, ALU.mult)
            ins = eng.tensor_scalar(mix_y[:], w["w_mix"][:], -1.0, None, ALU.mult)
            ins.then_inc(prepared_v, 1)
            eng.wait_ge(prepared_v, 1)
            for h in range(DB):
                ins = eng.tensor_tensor(mix_y[:, h, h * P:(h + 1) * P], mix_y[:, h, h * P:(h + 1) * P],
                                        ident[:], ALU.add)
            ins.then_inc(prepared_v, 1)
            eng.wait_ge(prepared_v, 2)
            for h in range(DB):
                ins = eng.tensor_tensor(mix_yd[:, h, :], mix_y[:, h, :], w["skip"][:], ALU.mult)
            ins.then_inc(prepared, 1)
            eng.wait_ge(prepared, 1)
            begin_with(start, 10)
            with eng.Fori(0, B) as b:
                at = Place(b, 0)
                attention(at)
                eng.wait_ge(x1_ready.sem, x1_ready.count(at, 1))
                mixture(at, x_res, None)
                ssm_inputs(at)
                scan_unit(at, 0, 0, None, 1)
                hold(eng)
                with eng.Fori(0, ITERS) as i:
                    turn = Place(b, 1, i)
                    scan_unit(turn, 1, 0, 0, 0)
                    scan_unit(turn, 0, 1, 1, 1)
                at = Place(b, 2)
                scan_unit(at, 1, 0, 0, None)
                back_var(at, 1, 1)
                back_norm(at, 1, 1)
                ssm_output(at)
                mixture(at, x_out, out_ready, Place(b + 1, 0))

        @block.gpsimd
        def _(eng):
            def scan_unit(at, hf, ks, ready, carried):
                sums = NG // 4 * ks + (LAG if carried else 0)
                for p in range(NG // 2):
                    eng.wait_ge(scanned.sem, scanned.count(at, NG * ks + 2 * p + 2))
                    if p == 0:
                        eng.wait_ge(c_copied.sem, c_copied.count(at, ready))
                    if p % 2 == 0 and (p >= NPROD // 2 or carried):
                        eng.wait_ge(nsummed.sem, nsummed.count(at, sums + p // 2 - 1))
                    s = 2 * p % NHID
                    eng.tensor_tensor(
                        prod[:, s:s + 2, :], hst[:, s:s + 2, :],
                        crep[:, hf:hf + 1, :].broadcast_to([P, 2, TH]), ALU.mult
                            ).then_inc(prod_done.sem, prod_done.up(at))

            eng.wait_ge(loaded, 16 * n_loads)
            with eng.Fori(0, B) as b:
                at = Place(b, 0)
                scan_unit(at, 0, 0, 1, False)
                with eng.Fori(0, ITERS) as i:
                    turn = Place(b, 1, i)
                    scan_unit(turn, 1, 0, 0, True)
                    scan_unit(turn, 0, 1, 1, True)
                scan_unit(Place(b, 2), 1, 0, 0, True)

        for name, s in sems:
            assert tuple(s.seen) == tuple(s.n), (name, s.seen, s.n)


def _rows(a):
    return np.ascontiguousarray(a.reshape(-1, P, a.shape[-1]).transpose(1, 0, 2))


def kernel(**inputs):
    import concourse.bacc as bacc
    from concourse.bass_utils import run_bass_kernel_spmd

    a = {k: np.asarray(v) for k, v in inputs.items()}
    b, f = (lambda n: a["L0_attn_b_" + n]), (lambda n: a["L0_ffn_" + n])
    wide = lambda v: np.ascontiguousarray(np.broadcast_to(v, (P, v.shape[0])))

    freqs = np.float32(10000.0) ** (np.arange(0, HD, 2, dtype=np.float32) / np.float32(HD))
    angles = np.arange(T, dtype=np.float32)[:, None] * freqs[None, :].astype(np.float32)
    cosine = np.cos(angles.astype(np.float64)).astype(np.float32)
    sine = np.sin(angles.astype(np.float64)).astype(np.float32)
    lanes = np.arange(P)
    sel = np.zeros((P, NR, 32), np.float32)
    for r in range(NR):
        sel[lanes, r, GC * r + lanes % GC] = 1.0

    arrays = {
        "x": a["L0_attn_a_x"],
        "ident": np.eye(P, dtype=np.float32), "sel": sel,
        "cosine": _rows(cosine), "sine": _rows(sine),
        "experts": wide(np.arange(NE, dtype=np.float32)),
        "qkv_w": a["L0_attn_a_qkv_w"], "qkv_b": wide(a["L0_attn_a_qkv_b"]),
        "out_w": a["L0_attn_a_out_w"], "out_b": wide(a["L0_attn_a_out_b"]),
        "w_in": b("W_in").T, "w_x": _rows(b("W_x").T),
        "a_log": b("A_log").reshape(NG, GC, NS).transpose(2, 1, 0).reshape(P, NG),
        "w_bc": _rows(b("W_bc").T), "w_zy": _rows(b("W_zy").T), "w_mix": _rows(b("W_mix").T),
        "skip": wide(b("D")), "gamma": b("ln_gamma").reshape(DB, P).T,
        "beta": b("ln_beta").reshape(DB, P).T, "w_out": _rows(b("W_out").T),
        "router": f("router_w").T,
        "gate_w": f("gate_w").transpose(1, 0, 2), "up_w": f("up_w").transpose(1, 0, 2),
        "gate_b": f("gate_b").reshape(NE, FB, P).transpose(2, 0, 1),
        "up_b": f("up_b").reshape(NE, FB, P).transpose(2, 0, 1),
        "down_w": f("down_w").reshape(NE, FB, P, DM).transpose(2, 0, 1, 3),
        "w_dt": b("W_dt").T, "b_dt": b("b_dt").reshape(1, DI), "down_b": f("down_b"),
    }
    nc = bacc.Bacc("TRN2", target_bir_lowering=False, num_devices=1)
    in_map, tensors = {}, {}
    for name, v in arrays.items():
        v = np.ascontiguousarray(v)
        in_map["in_" + name] = v
        tensors[name] = nc.dram_tensor("in_" + name, v.shape, F32, kind="ExternalInput").ap()
    out = nc.dram_tensor("out", (B, T, DM), F32, kind="ExternalOutput").ap()
    hybrid_kernel(nc, tensors, out)
    r = run_bass_kernel_spmd(nc, [in_map], core_ids=[0])
    return r.results[0]["out"]
```
